# Optimizing a Trainium2 kernel written in Bass

```python
import numpy as np
import jax
import jax.numpy as jnp

def _softmax(x, axis=-1):
    return jax.nn.softmax(x, axis=axis)

def _gelu(x):
    return jax.nn.gelu(x, approximate=True)

def _silu(x):
    return jax.nn.silu(x)

def _sigmoid(x):
    return jax.nn.sigmoid(x)

def _layernorm(x, axis=-1, eps=1e-05):
    m = jnp.mean(x, axis=axis, keepdims=True)
    v = jnp.var(x, axis=axis, keepdims=True)
    return (x - m) / jnp.sqrt(v + eps)

def _scatter_add(tgt, idx, src, axis=0):
    return tgt.at[idx].add(src)

def _segment_sum(src, seg, n):
    return jax.ops.segment_sum(src, seg, n)
kernel_name = 'mk_gnn_resnorm_d4_gnn_r32_514261'

def setup_inputs(seed: int=0):
    np.random.seed(seed)
    _w = jnp.asarray

    def _rec_inputs():
        import jax
        import jax.numpy as jnp
        _gk = jax.random.key(seed)
        x = -0.0009044 + 1 * jax.random.normal(jax.random.fold_in(_gk, 1), (3125, 16), jnp.float32)
        _s = jax.random.randint(jax.random.fold_in(_gk, 2), (50000,), 0, 3125, jnp.int32)
        _d = jax.random.randint(jax.random.fold_in(_gk, 3), (50000,), 0, 3125, jnp.int32)
        _loop = jnp.arange(3125, dtype=jnp.int32)
        src = jnp.concatenate([_s, _d, _loop])
        dst = jnp.concatenate([_d, _s, _loop])
        _o = jnp.argsort(dst, stable=True)
        src = src[_o]
        dst = dst[_o]
        edge_attr_16 = -0.00010739 + 0.99994 * jax.random.normal(jax.random.fold_in(_gk, 12), (103125, 16), jnp.float32)
        edge_type_90 = jax.random.randint(jax.random.fold_in(_gk, 14), (103125,), 0, 90, jnp.int32)
        edge_weight = jax.random.uniform(jax.random.fold_in(_gk, 15), (103125,), jnp.float32, 0.0, 1)
        return (x, src, dst, edge_attr_16, edge_type_90, edge_weight)
    x, src, dst, edge_attr_16, edge_type_90, edge_weight = _rec_inputs()

    def _L0_gnn_setup():
        import jax, jax.numpy as jnp
        import numpy as np
        NUM_NODES = 3125
        NUM_EDGES = 50000

        def gcn_conv(x, row, col, W, b, num_nodes):
            loop = jnp.arange(num_nodes)
            row = jnp.concatenate([row, loop])
            col = jnp.concatenate([col, loop])
            h = x @ W
            deg = jax.ops.segment_sum(jnp.ones_like(col, dtype=h.dtype), col, num_segments=num_nodes)
            dinv = jnp.where(deg > 0, jax.lax.rsqrt(deg), 0.0)
            norm = dinv[row] * dinv[col]
            msg = norm[:, None] * h[row]
            out = jax.ops.segment_sum(msg, col, num_segments=num_nodes)
            return out + b
        key = jax.random.key(seed)
        k1, k2, k3, k4 = jax.random.split(key, 4)
        x = jax.random.normal(k1, (NUM_NODES, 16), dtype=jnp.float32)
        edge_index = jax.random.randint(k2, (2, NUM_EDGES), 0, NUM_NODES, dtype=jnp.int64)
        W1 = jax.random.normal(k3, (16, 32), dtype=jnp.float32) * (1.0 / np.sqrt(16))
        b1 = jnp.zeros((32,), dtype=jnp.float32)
        W2 = jax.random.normal(k4, (32, 16), dtype=jnp.float32) * (1.0 / np.sqrt(32))
        b2 = jnp.zeros((16,), dtype=jnp.float32)
        return {'x': x, 'edge_index': edge_index, 'W1': W1, 'b1': b1, 'W2': W2, 'b2': b2}
    _L0_gnn_all = _L0_gnn_setup()
    _L0_gnn_in = {k: v for k, v in _L0_gnn_all.items() if k in ('W1', 'b1', 'W2', 'b2')}
    del _L0_gnn_all

    def _L1_gnn_setup():
        import jax, jax.numpy as jnp
        import numpy as np
        N, E, IN, OUT, R, B = (50000, 25000, 16, 16, 90, 30)
        key = jax.random.key(seed)
        ks = jax.random.split(key, 9)
        h = jax.random.normal(ks[0], (N, IN), dtype=jnp.float32)
        he = jax.random.normal(ks[1], (E, IN), dtype=jnp.float32)
        Ws = jax.random.normal(ks[2], (OUT, IN), dtype=jnp.float32) * 0.1
        Wa = jax.random.normal(ks[3], (1, 3 * OUT), dtype=jnp.float32) * 0.1
        weight = jax.random.normal(ks[4], (B, IN, OUT), dtype=jnp.float32) * 0.1
        w_comp = jax.random.normal(ks[5], (R, B), dtype=jnp.float32) * 0.1
        src = jax.random.randint(ks[6], (E,), 0, N)
        dst = jax.random.randint(ks[7], (E,), 0, N)
        rel_type = jax.random.randint(ks[8], (E,), 0, R)
        return {'h': h, 'he': he, 'Ws': Ws, 'Wa': Wa, 'weight': weight, 'w_comp': w_comp, 'src': src, 'dst': dst, 'rel_type': rel_type}
    _L1_gnn_all = _L1_gnn_setup()
    _L1_gnn_in = {k: v for k, v in _L1_gnn_all.items() if k in ('Ws', 'Wa', 'weight', 'w_comp')}
    del _L1_gnn_all

    def _L2_gnn_setup():
        import jax, jax.numpy as jnp
        import numpy as np
        N_NODES = 3125
        key = jax.random.key(seed)
        k1, k2, k3, k4 = jax.random.split(key, 4)
        E = 100000
        D = 16
        x = jax.random.uniform(k1, (N_NODES, D), dtype=jnp.float32)
        edge_index = jax.random.randint(k2, (2, E), 0, N_NODES, dtype=jnp.int64)
        edge_probs = jax.random.uniform(k3, (E,), dtype=jnp.float32)
        weight = jnp.ones((D,), dtype=jnp.float32)
        self_loop_weight = jnp.asarray(0.1, dtype=jnp.float32)
        return {'x': x, 'edge_index': edge_index, 'edge_probs': edge_probs, 'weight': weight, 'self_loop_weight': self_loop_weight}
    _L2_gnn_all = _L2_gnn_setup()
    _L2_gnn_in = {k: v for k, v in _L2_gnn_all.items() if k in ('weight', 'self_loop_weight')}
    del _L2_gnn_all

    def _L3_gnn_setup():
        import jax, jax.numpy as jnp
        import numpy as np
        N_NODES = 30000
        N_EDGES = 9375
        IN_FEATS = 16
        OUT_FEATS = 16
        EDGE_DIM = 16
        key = jax.random.key(seed)
        ks = jax.random.split(key, 8)
        feat = jax.random.normal(ks[0], (N_NODES, IN_FEATS), dtype=jnp.float32)
        efeat = jax.random.normal(ks[1], (N_EDGES, EDGE_DIM), dtype=jnp.float32)
        W_msg = jax.random.normal(ks[2], (EDGE_DIM, IN_FEATS * OUT_FEATS), dtype=jnp.float32) * 0.1
        b_msg = jnp.zeros((IN_FEATS * OUT_FEATS,), dtype=jnp.float32)
        W_attn = jax.random.normal(ks[3], (EDGE_DIM, IN_FEATS * OUT_FEATS), dtype=jnp.float32) * 0.1
        b_attn = jnp.zeros((IN_FEATS * OUT_FEATS,), dtype=jnp.float32)
        src = jax.random.randint(ks[4], (N_EDGES,), 0, N_NODES, dtype=jnp.int32)
        dst = jax.random.randint(ks[5], (N_EDGES,), 0, N_NODES, dtype=jnp.int32)
        return {'feat': feat, 'efeat': efeat, 'W_msg': W_msg, 'b_msg': b_msg, 'W_attn': W_attn, 'b_attn': b_attn, 'src': src, 'dst': dst}
    _L3_gnn_all = _L3_gnn_setup()
    _L3_gnn_in = {k: v for k, v in _L3_gnn_all.items() if k in ('W_msg', 'b_msg', 'W_attn', 'b_attn')}
    del _L3_gnn_all
    return {'x': x, 'src': src, 'dst': dst, 'edge_attr_16': edge_attr_16, 'edge_type_90': edge_type_90, 'edge_weight': edge_weight, 'L0_gnn_W1': _L0_gnn_in['W1'], 'L0_gnn_b1': _L0_gnn_in['b1'], 'L0_gnn_W2': _L0_gnn_in['W2'], 'L0_gnn_b2': _L0_gnn_in['b2'], 'L1_gnn_Ws': _L1_gnn_in['Ws'], 'L1_gnn_Wa': _L1_gnn_in['Wa'], 'L1_gnn_weight': _L1_gnn_in['weight'], 'L1_gnn_w_comp': _L1_gnn_in['w_comp'], 'L2_gnn_weight': _L2_gnn_in['weight'], 'L2_gnn_self_loop_weight': _L2_gnn_in['self_loop_weight'], 'L3_gnn_W_msg': _L3_gnn_in['W_msg'], 'L3_gnn_b_msg': _L3_gnn_in['b_msg'], 'L3_gnn_W_attn': _L3_gnn_in['W_attn'], 'L3_gnn_b_attn': _L3_gnn_in['b_attn']}

def reference(x, src, dst, edge_attr_16, edge_type_90, edge_weight, L0_gnn_W1, L0_gnn_b1, L0_gnn_W2, L0_gnn_b2, L1_gnn_Ws, L1_gnn_Wa, L1_gnn_weight, L1_gnn_w_comp, L2_gnn_weight, L2_gnn_self_loop_weight, L3_gnn_W_msg, L3_gnn_b_msg, L3_gnn_W_attn, L3_gnn_b_attn):
    import jax
    import jax.numpy as jnp

    def _L0_gnn_ref(x, edge_index, W1, b1, W2, b2):
        import jax, jax.numpy as jnp
        import numpy as np
        NUM_NODES = 3125
        NUM_EDGES = 50000

        def gcn_conv(x, row, col, W, b, num_nodes):
            loop = jnp.arange(num_nodes)
            row = jnp.concatenate([row, loop])
            col = jnp.concatenate([col, loop])
            h = x @ W
            deg = jax.ops.segment_sum(jnp.ones_like(col, dtype=h.dtype), col, num_segments=num_nodes)
            dinv = jnp.where(deg > 0, jax.lax.rsqrt(deg), 0.0)
            norm = dinv[row] * dinv[col]
            msg = norm[:, None] * h[row]
            out = jax.ops.segment_sum(msg, col, num_segments=num_nodes)
            return out + b
        row, col = (edge_index[0], edge_index[1])
        h = gcn_conv(x, row, col, W1, b1, NUM_NODES)
        h = jax.nn.relu(h)
        out = gcn_conv(h, row, col, W2, b2, NUM_NODES)
        return out

    def _L1_gnn_ref(h, he, Ws, Wa, weight, w_comp, src, dst, rel_type):
        import jax, jax.numpy as jnp
        import numpy as np
        N, E, IN, OUT, R, B = (50000, 25000, 16, 16, 90, 30)
        n_nodes, in_dim = h.shape
        num_bases, _, out_dim = weight.shape
        num_rels = w_comp.shape[0]
        V = weight.reshape(in_dim, num_bases, out_dim)
        W_rel = jnp.matmul(w_comp, V).reshape(num_rels, in_dim, out_dim)
        h_src = h[src]
        z_src = h_src @ Ws.T
        z_dst = h[dst] @ Ws.T
        z_e = he @ Ws.T
        e = jnp.concatenate([z_src, z_e, z_dst], axis=1) @ Wa.T
        msg = jnp.einsum('ei,eio->eo', h_src, W_rel[rel_type]) * e
        h_out = jax.ops.segment_sum(msg, dst, num_segments=n_nodes)
        return h_out

    def _L2_gnn_ref(x, edge_index, edge_probs, weight, self_loop_weight):
        import jax, jax.numpy as jnp
        import numpy as np
        N_NODES = 3125
        src = edge_index[0]
        dst = edge_index[1]
        messages = x[src] * edge_probs[:, None] * weight
        out = jax.ops.segment_sum(messages, dst, num_segments=N_NODES)
        out = out + x * self_loop_weight
        return jnp.clip(x + out, 0.0, 1.0)

    def _L3_gnn_ref(feat, efeat, W_msg, b_msg, W_attn, b_attn, src, dst):
        import jax, jax.numpy as jnp
        import numpy as np
        N_NODES = 30000
        N_EDGES = 9375
        IN_FEATS = 16
        OUT_FEATS = 16
        EDGE_DIM = 16
        N, in_f = feat.shape
        E = efeat.shape[0]
        w_m = (efeat @ W_msg + b_msg).reshape(E, in_f, -1)
        w_a = (efeat @ W_attn + b_attn).reshape(E, in_f, -1)
        h_src = feat[src][:, :, None]
        e1 = w_m * h_src
        e2 = w_a * h_src
        seg_max = jax.ops.segment_max(e2, dst, num_segments=N)
        ex = jnp.exp(e2 - seg_max[dst])
        denom = jax.ops.segment_sum(ex, dst, num_segments=N)
        attn = ex / denom[dst]
        ft = jax.ops.segment_sum(e1 * attn, dst, num_segments=N)
        return ft.sum(axis=1)
    edge_index = jnp.stack([src, dst])
    x = _layernorm(x + _L0_gnn_ref(x, edge_index, L0_gnn_W1, L0_gnn_b1, L0_gnn_W2, L0_gnn_b2), axis=-1)
    x = _layernorm(x + _L1_gnn_ref(x, edge_attr_16, L1_gnn_Ws, L1_gnn_Wa, L1_gnn_weight, L1_gnn_w_comp, src, dst, edge_type_90), axis=-1)
    x = _layernorm(x + _L2_gnn_ref(x, edge_index, edge_weight, L2_gnn_weight, L2_gnn_self_loop_weight), axis=-1)
    x = _layernorm(x + _L3_gnn_ref(x, edge_attr_16, L3_gnn_W_msg, L3_gnn_b_msg, L3_gnn_W_attn, L3_gnn_b_attn, src, dst), axis=-1)
    return x

_drawn_inputs = setup_inputs


def setup_inputs(seed=0):
    import zlib

    import numpy as np

    out = dict(_drawn_inputs(seed))
    spreads = {'L0_gnn_b1': (0.0, 0.1),
     'L0_gnn_b2': (0.0, 0.1),
     'L2_gnn_weight': (1.0, 0.2),
     'L3_gnn_b_msg': (0.0, 0.1),
     'L3_gnn_b_attn': (0.0, 0.1)}
    factors = {}
    for name, (base, spread) in spreads.items():
        noise = np.random.default_rng([zlib.crc32(name.encode()), seed]).standard_normal(out[name].shape)
        drawn = base * np.exp(spread * noise) if base else spread * noise
        out[name] = jnp.asarray(drawn.astype(out[name].dtype))
    for name, factor in factors.items():
        out[name] = (out[name] * factor).astype(out[name].dtype)
    return out
```

```python
import concourse.bass as bass
from concourse import mybir
from contextlib import ExitStack

FP32 = mybir.dt.float32
BF16 = mybir.dt.bfloat16
I32 = mybir.dt.int32
U32 = mybir.dt.uint32
ALU = mybir.AluOpType
ACT = mybir.ActivationFunctionType
X = mybir.AxisListType.X
ds = bass.ds

N, E, F, H1, R, B = 3125, 103125, 16, 32, 90, 30
P = 125
T = N // P
C = E // P
SLOTS = 11
TURNS = C // SLOTS
HALVES = [(0, 6), (6, 5)]
G = 3
GROUPS = C // G
GE = G * P
STEPS = GROUPS + T
SROWS = 100
SCOLS = STEPS // SROWS
FF = F * F
YW = F + 1
TB = 4
TBW = TB * P
NB = T // TB
HC = (T + 1) // 2
NEG = -3.0e38
EPS = 1e-5
TINY = 1e-30


class Chain:

    def __init__(self, engine, sem):
        self.engine, self.sem, self.n = engine, sem, 0

    def __call__(self, ins):
        self.n += 1
        ins.then_inc(self.sem, 1)
        self.engine.wait_ge(self.sem, self.n)


class Trips(Chain):

    def __call__(self, ins):
        self.n += 16
        ins.then_inc(self.sem, 16)
        self.engine.wait_ge(self.sem, self.n)


class Carve:

    def __init__(self, arena):
        self.arena, self.at = arena, 0

    def __call__(self, rows, *shape, dt=FP32):
        n = 1
        for k in shape:
            n *= k
        words = n if dt != BF16 else (n + 1) // 2
        ap = self.arena[0:rows, self.at:self.at + words]
        self.at += words
        assert self.at <= self.arena.shape[1], (self.at, self.arena.shape)
        if dt != FP32:
            ap = ap.bitcast(dt)
        names = "abcd"[:len(shape)]
        if len(shape) > 1:
            ap = ap.rearrange(f"p ({' '.join(names)}) -> p {' '.join(names)}", **dict(zip(names[1:], shape[1:])))
        return ap


def build(nc, x, src_pc, dst_pc, dst_next_pc, dst_prev_pc, group_ends, ef_pc, efT, type_pc,
          weight_pc, W1, b1, W2, b2, Ws, WaT, VT, wcompT, l2w, slw, Wmsg, bmsg, Wattn, battn, out):
    ctx = ExitStack()
    with ctx:
        def sb(name, shape, dt=FP32):
            return ctx.enter_context(nc.sbuf_tensor(name, shape, dt))

        def sem(name):
            return ctx.enter_context(nc.semaphore(name))

        def dram(name, shape, dt=FP32):
            return nc.dram_tensor(name, shape, dt, kind="Internal").ap()

        table = [dram(f"table{i}", (N, F)) for i in range(4)]
        rel_table = dram("rel_table", (N * R, YW))
        rel_flat = dram("rel_flat", (F, R, F))
        pen_dram = dram("pen_dram", (C, P))
        dstf_dram = dram("dstf_dram", (C, P))
        sched_dram = dram("sched_dram", (2, SCOLS, SROWS), I32)

        ident = sb("ident", [128, 128])
        iota = sb("iota", [128, 128])
        pcol = sb("pcol", [128, 1])
        node_id = sb("node_id", [P, T + 1])
        tile_id = sb("tile_id", [P, T + 1])
        src_i = sb("src_i", [P, C], I32)
        rel_idx = sb("rel_idx", [P, C], I32)
        dstf = sb("dstf", [P, C])
        dst_end = sb("dst_end", [P, C])
        dlo = sb("dlo", [P, C])
        dhi = sb("dhi", [P, C])
        edge_w = sb("edge_w", [P, C])
        edge_x = sb("edge_x", [P, C, F])
        xn = sb("xn", [P, T, F])
        tab = sb("tab", [P, T, F])
        yn = sb("yn", [P, T, F])
        nt = [sb(f"nt{i}", [P, T]) for i in range(3)]
        dinv = sb("dinv", [P, T])
        cn = sb("cn", [P, T])
        b2_sb, l2w_sb, slw_sb = sb("b2_sb", [P, F]), sb("l2w_sb", [P, F]), sb("slw_sb", [P, 1])
        a2_row = sb("a2_row", [P, F])
        carry = sb("carry", [128, 2, GROUPS + 1])
        sched = sb("sched", [1, 2 * STEPS], I32)
        Wl3 = sb("Wl3", [F + 1, F, 2, F])

        big = sb("big", [128, (T + 1) * 2 * FF])
        sums = big[0:P, :].rearrange("p (t i w) -> p t i w", i=F, w=2 * F)
        cut = Carve(big)
        Z = [cut(P, HALVES[0][1], T, 2 * F) for _ in range(2)]
        ring = cut(P, SLOTS, YW)
        stage = cut(P, SLOTS, dt=I32)
        cut = Carve(big)
        dst_i, nxt_i, prv_i, t0s = (cut(P, C, dt=I32) for _ in range(4))
        tmpf = cut(P, C)
        grow = cut(1, 5, GROUPS)
        gcmp = cut(SROWS, 2, GROUPS)
        gends = cut(1, 2, GROUPS, dt=I32)
        sch = cut(SROWS, 12)
        sch_i = cut(SROWS, 2 * SCOLS, dt=I32)
        iota_i = cut(128, 128, dt=I32)
        wide = sb("wide", [128, (T + 1) * FF])
        Macc = wide[0:P, :].rearrange("p (t w) -> p t w", w=FF)
        cut = Carve(wide)
        xT = cut(F, T * P)
        hT = cut(H1, T * P)
        work = sb("work", [128, 9500])
        cut = Carve(work)
        S = [cut(P, HALVES[0][1], P) for _ in range(2)]
        mask = [cut(P, HALVES[0][1], T) for _ in range(2)]
        msg = cut(P, HALVES[0][1], 2 * F)
        att = cut(P, HALVES[0][1], F)
        att_s = cut(P, HALVES[0][1])
        xTs = cut(F, P)
        Yt = cut(P, R * YW)
        Tall = cut(F, R, YW)
        W1_sb, W2_sb, b1_sb = cut(F, H1), cut(H1, F), cut(H1, 1)
        Ws_sb, WaT_sb, A_sb = cut(F, F), cut(F, 3), cut(F, 3)
        A2_rep = cut(F, P)
        VT_sb, wcT_sb, rel_sb = cut(B, FF), cut(B, R), cut(R, FF)
        zeros = cut(P, 512)
        ones = cut(1, SROWS)
        cut = Carve(work)
        efs = [cut(F + 1, GE) for _ in range(2)]
        rows = [cut(128, GE) for _ in range(2)]
        at_b = cut.at
        e2 = cut(P, G, FF)
        run_max = cut(128, 2, GE)
        run_maxT = cut(P, G, FF)
        SE = [cut(P, G, P) for _ in range(2)]
        dcol = cut(P, G)
        cut = Carve(work)
        cut.at = at_b
        ST = cut(P, GE)
        SB = [cut(P, G, P) for _ in range(2)]
        em = cut(P, G, F, 2 * F)
        EP = [cut(P, G, F, 2 * F) for _ in range(2)]
        dcolb = cut(P, G)

        bank = ctx.enter_context(nc.psum_tensor("bank", [128, 8, 512], FP32))

        names = {}

        def ev(name):
            if name not in names:
                names[name] = sem(name)
            return names[name]

        s_in, s_dve, s_pool, s_pe = sem("inputs_loaded"), sem("dve_chain"), sem("pool_chain"), sem("pe_chain")
        s_slot = [sem(f"gathered_slot{k}") for k in range(SLOTS)]
        s_stage = sem("indices_staged")
        PASSES = ["deg", "l0a", "l0b", "l1", "l2", "l3"]
        s_z = {p: [sem(f"{p}_operands{h}") for h in range(2)] for p in PASSES}
        s_mm = {p: [sem(f"{p}_summed{h}") for h in range(2)] for p in PASSES[:5]}
        for n in ("stage_seen", "consts", "dstf_ready", "pen_ready", "sched_ready", "rel_ready", "attn_rows", "attn_cols", "attn_rep",
                  "attn_row", "rel_sum", "inc_row", "inc_bc", "round_trips", "deg_sum", "deg_ready", "deg_root",
                  "l0a_sum", "l0b_sum", "l1_sum", "l2_sum", "ax_ready", "axT", "xT_ready", "h_sum", "hT_ready", "z_sum",
                  "x1_ready", "x1T", "x1T_ready", "relidx_ready", "edge_attr_used",
                  "tab0", "tab1", "tab2", "tab3", "tab4", "wrote0", "wrote1", "wrote2", "wrote3", "wrote4",
                  "y_src", "y_mm", "y_copied", "y_wrote",
                  "var0", "var1", "var2", "var3", "root0", "root1", "root2", "root3",
                  "A_ef0", "A_ef1", "A_pen0", "A_pen1", "A_w", "A_e2", "A_tr", "A_scan", "A_trb", "A_copy", "A_se", "A_sc", "A_add", "A_dve", "A_carry",
                  "B_ef0", "B_ef1", "B_row0", "B_row1", "B_w", "B_st", "B_mg", "B_em", "B_d", "B_ex", "B_p", "B_sc", "B_add", "B_dve"):
            ev(n)

        block = ctx.enter_context(nc.Block())
        N_LOADS = 25
        flat = "c p -> (c p)"

        @block.sync
        def _(sp):
            loads = [(xn[:], x.rearrange("(t p) f -> p t f", p=P)), (dst_i, dst_pc), (src_i[:], src_pc),
                     (edge_w[:], weight_pc), (W1_sb, W1), (W2_sb, W2), (b1_sb, b1),
                     (b2_sb[:], b2.to_broadcast([P, F])), (l2w_sb[:], l2w.to_broadcast([P, F])),
                     (slw_sb[:], slw.to_broadcast([P, 1])), (Ws_sb, Ws), (WaT_sb, WaT), (VT_sb, VT),
                     (wcT_sb, wcompT), (gends[0:1, 0, :], group_ends[0:1, :]), (gends[0:1, 1, :], group_ends[1:2, :]),
                     (nxt_i, dst_next_pc), (prv_i, dst_prev_pc), (edge_x[:], ef_pc), (rel_idx[:], type_pc)]
            for c, (w, b) in enumerate(((Wattn, battn), (Wmsg, bmsg))):
                loads.append((Wl3[0:F, :, c, :], w.rearrange("k (i o) -> k i o", i=F)))
                loads.append((Wl3[F:F + 1, :, c, :], b.rearrange("u (i o) -> u i o", i=F)))
            for d, s in loads:
                sp.dma_start(d, s).then_inc(s_in, 16)
            assert len(loads) == N_LOADS - 1

            trips = Trips(sp, ev("round_trips"))
            with nc.allow_non_contiguous_dma(reason="edge layout to flat, once"):
                sp.wait_ge(ev("dstf_ready"), 1)
                trips(sp.dma_start(dstf_dram.rearrange("c (p u) -> p c u", u=1), dstf[:].rearrange("p (c u) -> p c u", u=1)))
                sp.wait_ge(ev("pen_ready"), 1)
                trips(sp.dma_start(pen_dram.rearrange("c (p u) -> p c u", u=1), tmpf.rearrange("p (c u) -> p c u", u=1)))
                sp.wait_ge(ev("sched_ready"), 1)
                trips(sp.dma_start(sched_dram.rearrange("a c (p u) -> p (a c) u", u=1), sch_i.rearrange("p (a u) -> p a u", u=1)))
                trips(sp.dma_start(sched[:], sched_dram.rearrange("(u a) c p -> u (a c p)", u=1)))
                sp.wait_ge(ev("rel_ready"), 1)
                trips(sp.dma_start(rel_flat.rearrange("i r o -> r i o"), rel_sb.rearrange("r (i o) -> r i o", i=F)))
                trips(sp.dma_start(Tall[:, :, 0:F], rel_flat.rearrange("i r o -> (i r) o").rearrange("(r i) o -> i r o", i=F)))

            for i in range(2):
                sp.wait_ge(ev(f"tab{i}"), 1)
                sp.dma_start(table[i].rearrange("(t p) f -> p t f", p=P), tab[:]).then_inc(ev(f"wrote{i}"), 16)
            with sp.Fori(0, T) as t:
                sp.wait_ge(ev("y_copied"), t + 1)
                sp.dma_start(rel_table.rearrange("(t p r) w -> t p (r w)", p=P, r=R)[ds(t, 1), :, :].rearrange("u p w -> (u p) w"), Yt).then_inc(ev("y_wrote"), 16)
            for i in (2, 3):
                sp.wait_ge(ev(f"tab{i}"), 1)
                sp.dma_start(table[i].rearrange("(t p) f -> p t f", p=P), xn[:]).then_inc(ev(f"wrote{i}"), 16)

            sp.wait_ge(s_z["l3"][1], TURNS)
            for ph, row_dram, rown, row_used, parts in (("A", pen_dram, "pen", "scan", 128), ("B", dstf_dram, "row", "st", P)):
                with sp.Fori(0, STEPS // 2) as it:
                    for sl in range(2):
                        g = sp.value_load(sched[0:1, ds(it * 2 + sl, 1)], min_val=0, max_val=GROUPS - 1)
                        sp.wait_ge(ev(ph + "_w"), it * 2)
                        sp.dma_start(efs[sl], efT[:, ds(g * GE, GE)]).then_inc(ev(f"{ph}_ef{sl}"), 16)
                        sp.wait_ge(ev(f"{ph}_{row_used}"), it * 2)
                        row = row_dram.rearrange(flat).rearrange("(u e) -> u e", u=1)[:, ds(g * GE, GE)]
                        sp.dma_start(rows[sl][0:parts, :], row.to_broadcast([parts, GE])).then_inc(ev(f"{ph}_{rown}{sl}"), 16)
                sp.wait_ge(ev(ph + "_add"), STEPS)
            sp.wait_ge(ev("tab4"), 1)
            sp.dma_start(out.rearrange("(t p) f -> p t f", p=P), xn[:]).then_inc(ev("wrote4"), 16)
            sp.wait_ge(ev("wrote4"), 16)

        @block.gpsimd
        def _(pool):
            do = Chain(pool, s_pool)
            do(nc.gpsimd.iota(iota_i, pattern=[[1, 128]], base=0, channel_multiplier=0))
            nc.gpsimd.iota(sch_i[:, 0:SCOLS], pattern=[[SROWS, SCOLS]], base=0, channel_multiplier=1)
            do(nc.gpsimd.tensor_copy(iota[:], iota_i))
            do(nc.gpsimd.iota(iota_i, pattern=[[-1, 128]], base=0, channel_multiplier=1))
            do(nc.gpsimd.tensor_copy(ident[:], iota_i))
            do(nc.gpsimd.memset(zeros, 0.0))
            nc.gpsimd.memset(ones, 1.0)
            nc.gpsimd.memset(carry[:], 0.0).then_inc(ev("consts"), 1)

            def gather(nth, p, source, width, idx, written, count):
                pool.wait_ge(written, count)
                with pool.Fori(0, TURNS) as it:
                    for h, (k0, n) in enumerate(HALVES):
                        pool.wait_ge(s_z[p][h], it)
                        for k in range(k0, k0 + n):
                            pool.wait_ge(s_slot[k], it * 16 + 16 * TURNS * nth)
                        nc.gpsimd.tensor_copy(stage[:, k0:k0 + n], idx[:, ds(it * SLOTS + k0, n)]).then_inc(s_stage, 1)
                        pool.wait_ge(s_stage, it * 2 + 2 * TURNS * nth + h + 1)
                        pool.sem_inc(ev("stage_seen"), 1)
                        for k in range(k0, k0 + n):
                            pool.indirect_dma_start(
                                out=ring[:, k, 0:width], out_offset=None, in_=source,
                                in_offset=bass.IndirectOffsetOnAxis(ap=stage[:, k:k + 1].bitcast(U32), axis=0),
                            ).then_inc(s_slot[k], 16)

            pool.wait_ge(s_in, 16 * (N_LOADS - 1))
            gather(0, "l0a", table[0], F, src_i, ev("wrote0"), 16)
            gather(1, "l0b", table[1], F, src_i, ev("wrote1"), 16)
            pool.wait_ge(ev("relidx_ready"), 1)
            gather(2, "l1", rel_table, YW, rel_idx, ev("y_wrote"), 16 * T)
            gather(3, "l2", table[2], F, src_i, ev("wrote2"), 16)
            gather(4, "l3", table[3], F, src_i, ev("wrote3"), 16)
            with pool.Fori(0, STEPS // 2) as it:
                for sl in range(2):
                    pool.wait_ge(ev("B_ex"), it * 2 + sl + 1)
                    nc.gpsimd.tensor_tensor(EP[sl][:, :, :, F:2 * F], em[:, :, :, F:2 * F], EP[sl][:, :, :, 0:F], ALU.mult).then_inc(ev("B_p"), 1)

        @block.scalar
        def _(act):
            sqrt = lambda o, i: nc.scalar.activation(o, i, ACT.Sqrt)
            act.wait_ge(ev("deg_ready"), 1)
            sqrt(nt[1][:], nt[0][:]).then_inc(ev("deg_root"), 1)
            act.wait_ge(ev("h_sum"), 1)
            nc.scalar.activation(hT[:, 0:NB * TBW].rearrange("p (b w) -> p b w", w=TBW), bank[0:H1, 0:NB, 0:TBW], ACT.Relu, bias=b1_sb)
            nc.scalar.activation(hT[:, NB * TBW:N], bank[0:H1, NB, 0:N - NB * TBW], ACT.Relu, bias=b1_sb).then_inc(ev("hT_ready"), 1)
            act.wait_ge(ev("var0"), 1)
            sqrt(nt[1][:], nt[0][:]).then_inc(ev("root0"), 1)
            act.wait_ge(ev("x1T_ready"), 1)
            with act.Fori(0, T) as t:
                act.wait_ge(ev("y_mm"), t)
                nc.scalar.activation(xTs, xT[:, ds(t * P, P)], ACT.Copy).then_inc(ev("y_src"), 1)
            for i in (1, 2):
                act.wait_ge(ev(f"var{i}"), 1)
                sqrt(nt[1][:], nt[0][:]).then_inc(ev(f"root{i}"), 1)
            with act.Fori(0, STEPS) as s:
                act.wait_ge(ev("A_trb"), s + 1)
                act.wait_ge(ev("A_sc"), s)
                nc.scalar.activation(run_maxT[:, 0:2, :], bank[0:P, 4, :].rearrange("p (g w) -> p g w", g=2), ACT.Copy)
                nc.scalar.activation(run_maxT[:, 2, :], bank[0:P, 5, 0:FF], ACT.Copy).then_inc(ev("A_copy"), 1)
            with act.Fori(0, STEPS // 2) as it:
                for sl in range(2):
                    act.wait_ge(ev("B_d"), it * 2 + sl + 1)
                    nc.scalar.activation(EP[sl][:, :, :, 0:F], EP[sl][:, :, :, 0:F], ACT.Exp).then_inc(ev("B_ex"), 1)
            act.wait_ge(ev("var3"), 1)
            sqrt(nt[1][:], nt[0][:]).then_inc(ev("root3"), 1)

        def wide_bc(ap, shape):
            return ap.to_broadcast(shape)

        @block.vector
        def _(dve):
            do = Chain(dve, s_dve)
            v = nc.vector
            dve.wait_ge(ev("consts"), 1)
            dve.wait_ge(s_in, 16 * (N_LOADS - 1))
            do(v.tensor_copy(sch[:, 0:SCOLS], sch_i[:, 0:SCOLS]))
            do(v.tensor_copy(pcol[:], ident[:, 0:1]))
            do(v.tensor_scalar(tile_id[:], iota[0:P, 0:T + 1], float(P), None, ALU.mult))
            do(v.tensor_scalar(node_id[:], tile_id[:], pcol[0:P, :], None, ALU.add))
            do(v.tensor_scalar(ident[:], ident[:], 0.0, None, ALU.is_equal))
            do(v.tensor_copy(dstf[:], dst_i))
            v.tensor_tensor(t0s, dst_i, nxt_i, ALU.not_equal).then_inc(ev("dstf_ready"), 1)
            dve.wait_ge(ev("dstf_ready"), 1)
            do(v.scalar_tensor_tensor(out=dst_end[:], in0=dstf[:], scalar=1.0, in1=t0s, op0=ALU.add, op1=ALU.mult))
            do(v.tensor_scalar(dst_end[:], dst_end[:], 1.0, None, ALU.subtract))
            do(v.tensor_tensor(tmpf, dst_i, prv_i, ALU.not_equal))
            v.tensor_scalar(tmpf, tmpf, NEG, None, ALU.mult).then_inc(ev("pen_ready"), 1)
            do(v.tensor_scalar(dhi[:], dstf[:], float(P), None, ALU.is_ge))
            do(v.tensor_copy(grow[0:1, 0:2, :], gends[0:1, :, :]))
            do(v.tensor_scalar(grow[0:1, 2:4, :], grow[0:1, 0:2, :], float(P), None, ALU.is_ge))
            for t in range(2, T):
                do(v.scalar_tensor_tensor(out=dhi[:], in0=dstf[:], scalar=float(P * t), in1=dhi[:], op0=ALU.is_ge, op1=ALU.add))
                do(v.scalar_tensor_tensor(out=grow[0:1, 2:4, :], in0=grow[0:1, 0:2, :], scalar=float(P * t), in1=grow[0:1, 2:4, :], op0=ALU.is_ge, op1=ALU.add))
            do(v.scalar_tensor_tensor(out=dlo[:], in0=dhi[:], scalar=-float(P), in1=dstf[:], op0=ALU.mult, op1=ALU.add))
            do(v.scalar_tensor_tensor(out=grow[0:1, 4, :], in0=grow[0:1, 3, :], scalar=1.0, in1=grow[0:1, 2, :], op0=ALU.add, op1=ALU.subtract))
            do(v.memset(grow[0:1, 3, :], 0.0))
            do(v.tensor_tensor_scan(grow[0:1, 0, :], grow[0:1, 4, :], grow[0:1, 3, :], 0.0, ALU.add, ALU.add))
            do(v.tensor_tensor(grow[0:1, 1, :], grow[0:1, 0, :], grow[0:1, 4, :], ALU.subtract))
            v.tensor_tensor(grow[0:1, 2, :], grow[0:1, 2, :], grow[0:1, 1, :], ALU.subtract).then_inc(ev("inc_row"), 1)
            dve.wait_ge(ev("inc_bc"), 1)
            for j in range(SCOLS):
                step = sch[:, j:j + 1]
                do(v.tensor_scalar(gcmp[:, 0, :], bank[0:SROWS, 0, 0:GROUPS], step, None, ALU.is_le))
                do(v.tensor_reduce(sch[:, 3 + j:4 + j], gcmp[:, 0, :], X, ALU.add))
                do(v.scalar_tensor_tensor(out=gcmp[:, 0, :], in0=bank[0:SROWS, 1, 0:GROUPS], scalar=step, in1=gcmp[:, 0, :], op0=ALU.is_le, op1=ALU.subtract))
                do(v.tensor_tensor(gcmp[:, 1, :], bank[0:SROWS, 2, 0:GROUPS], gcmp[:, 0, :], ALU.mult))
                do(v.tensor_reduce(sch[:, 6 + j:7 + j], gcmp[:, 1, :], X, ALU.add))
            do(v.tensor_tensor(sch[:, 6:9], sch[:, 6:9], sch[:, 0:3], ALU.add))
            do(v.tensor_scalar(sch[:, 3:6], sch[:, 3:6], float(GROUPS - 1), None, ALU.min))
            do(v.tensor_scalar(sch[:, 6:9], sch[:, 6:9], float(T), None, ALU.min))
            v.tensor_copy(sch_i, sch[:, 3:9]).then_inc(ev("sched_ready"), 1)
            dve.wait_ge(ev("attn_rows"), 1)
            do(v.tensor_copy(A_sb, bank[0:F, 3, 0:3]))
            do(v.tensor_copy(Tall[:, :, F:F + 1], A_sb[:, 0:1].unsqueeze(1).to_broadcast([F, R, 1])))
            v.tensor_copy(A2_rep, A_sb[:, 1:2].to_broadcast([F, P])).then_inc(ev("attn_rep"), 1)
            dve.wait_ge(ev("attn_row"), 1)
            do(v.tensor_copy(a2_row[:], bank[0:P, 4, 0:F]))
            dve.wait_ge(ev("rel_sum"), 1)
            v.tensor_copy(rel_sb, bank[0:R, 5, 0:FF]).then_inc(ev("rel_ready"), 1)
            dve.wait_ge(ev("pen_ready"), 1)
            dve.wait_ge(ev("round_trips"), 32)
            do(v.tensor_copy(tmpf, rel_idx[:]))
            do(v.scalar_tensor_tensor(out=tmpf, in0=src_i[:], scalar=float(R), in1=tmpf, op0=ALU.mult, op1=ALU.add))
            do(v.tensor_copy(rel_idx[:], tmpf))
            dve.wait_ge(ev("round_trips"), 64)
            v.memset(nt[2][:], 0.0).then_inc(ev("relidx_ready"), 1)

            def spread(p, nth, chain_len, payload):
                ch = sem(f"{p}_dve_chain")
                width = {"deg": 0, "l1": 2 * F, "l3": 0}.get(p, F)
                with dve.Fori(0, TURNS) as it:
                    for h, (k0, n) in enumerate(HALVES):
                        step = [it * (2 * chain_len) + h * chain_len]

                        def link(ins):
                            ins.then_inc(ch, 1)
                            step[0] = step[0] + 1
                            dve.wait_ge(ch, step[0])

                        col = it * SLOTS + k0
                        if p != "l3":
                            dve.wait_ge(s_mm[p][h], it)
                            v.tensor_tensor(S[h][:, 0:n, :], iota[0:P, 0:P].unsqueeze(1).to_broadcast([P, n, P]),
                                            dlo[:, ds(col, n)].unsqueeze(2).to_broadcast([P, n, P]), ALU.is_equal)
                            ins = v.tensor_tensor(mask[h][:, 0:n, :], iota[0:P, 0:T].unsqueeze(1).to_broadcast([P, n, T]),
                                                  dhi[:, ds(col, n)].unsqueeze(2).to_broadcast([P, n, T]), ALU.is_equal)
                            if p == "deg":
                                ins.then_inc(s_z[p][h], 1)
                                continue
                            link(ins)
                        for k in range(k0, k0 + n):
                            dve.wait_ge(s_slot[k], it * 16 + 16 * (TURNS * nth + 1))
                        rowsv = payload(col, ring[:, k0:k0 + n, :], n, link)
                        if p == "l3":
                            v.tensor_copy(edge_x[:, ds(col, n), :], rowsv).then_inc(s_z[p][h], 1)
                            continue
                        z = Z[h].rearrange("p a b c -> p (a b c)")[:, 0:n * T * width].rearrange("p (a b c) -> p a b c", b=T, c=width)
                        v.tensor_tensor(z, mask[h][:, 0:n, :].unsqueeze(3).to_broadcast([P, n, T, width]),
                                        rowsv.unsqueeze(2).to_broadcast([P, n, T, width]), ALU.mult).then_inc(s_z[p][h], 1)

            def plain(col, got, n, link):
                return got[:, :, 0:F]

            def weighted(col, got, n, link):
                link(v.tensor_tensor(msg[:, 0:n, 0:F], got[:, :, 0:F], edge_w[:, ds(col, n)].unsqueeze(2).to_broadcast([P, n, F]), ALU.mult))
                return msg[:, 0:n, 0:F]

            def relational(col, got, n, link):
                link(v.tensor_tensor(att[:, 0:n, :], edge_x[:, ds(col, n), :], a2_row[:].unsqueeze(1).to_broadcast([P, n, F]), ALU.mult))
                link(v.tensor_reduce(att_s[:, 0:n], att[:, 0:n, :], X, ALU.add))
                link(v.tensor_tensor(att_s[:, 0:n], att_s[:, 0:n], got[:, :, F], ALU.add))
                v.tensor_copy(msg[:, 0:n, F:2 * F], got[:, :, 0:F])
                link(v.tensor_tensor(msg[:, 0:n, 0:F], got[:, :, 0:F], att_s[:, 0:n].unsqueeze(2).to_broadcast([P, n, F]), ALU.mult))
                return msg[:, 0:n, :]

            def bct(ap):
                return ap.unsqueeze(2).to_broadcast([P, T, F])

            def bcf(ap):
                return ap.unsqueeze(1).to_broadcast([P, T, F])

            def layernorm(i):
                do(v.tensor_reduce(nt[0][:], xn[:], X, ALU.add))
                do(v.tensor_scalar(nt[0][:], nt[0][:], 1.0 / F, None, ALU.mult))
                do(v.tensor_tensor(xn[:], xn[:], bct(nt[0][:]), ALU.subtract))
                do(v.tensor_tensor(yn[:], xn[:], xn[:], ALU.mult))
                do(v.tensor_reduce(nt[0][:], yn[:], X, ALU.add))
                v.tensor_scalar(nt[0][:], nt[0][:], 1.0 / F, EPS, ALU.mult, ALU.add).then_inc(ev(f"var{i}"), 1)
                dve.wait_ge(ev(f"root{i}"), 1)
                do(v.reciprocal(nt[2][:], nt[1][:]))
                return v.tensor_tensor(xn[:], xn[:], bct(nt[2][:]), ALU.mult)

            def agg(width=F):
                return bank[0:P, 0, 0:T * width].rearrange("p (t w) -> p t w", w=width)

            def take_xT(done):
                v.tensor_copy(xT[:, 0:NB * TBW].rearrange("p (b w) -> p b w", w=TBW), bank[0:F, 1:1 + NB, 0:TBW])
                v.tensor_copy(xT[:, NB * TBW:N], bank[0:F, 1 + NB, 0:N - NB * TBW]).then_inc(done, 1)

            spread("deg", 0, 0, None)
            dve.wait_ge(ev("deg_sum"), 1)
            v.tensor_scalar(nt[0][:], bank[0:P, 0, 0:T], 1.0, None, ALU.add).then_inc(ev("deg_ready"), 1)
            dve.wait_ge(ev("deg_root"), 1)
            do(v.reciprocal(dinv[:], nt[1][:]))
            v.tensor_tensor(tab[:], xn[:], bct(dinv[:]), ALU.mult).then_inc(ev("tab0"), 1)
            spread("l0a", 0, 1, plain)
            dve.wait_ge(ev("l0a_sum"), 1)
            dve.wait_ge(ev("tab0"), 1)
            do(v.tensor_tensor(yn[:], agg(), tab[:], ALU.add))
            v.tensor_tensor(yn[:], yn[:], bct(dinv[:]), ALU.mult).then_inc(ev("ax_ready"), 1)
            dve.wait_ge(ev("axT"), 1)
            take_xT(ev("xT_ready"))
            dve.wait_ge(ev("z_sum"), 1)
            v.tensor_tensor(tab[:], bank[0:P, 7, 0:T * F].rearrange("p (t w) -> p t w", w=F), bct(dinv[:]), ALU.mult).then_inc(ev("tab1"), 1)
            spread("l0b", 1, 1, plain)
            dve.wait_ge(ev("l0b_sum"), 1)
            dve.wait_ge(ev("tab1"), 1)
            do(v.tensor_tensor(yn[:], agg(), tab[:], ALU.add))
            do(v.tensor_tensor(yn[:], yn[:], bct(dinv[:]), ALU.mult))
            do(v.tensor_tensor(yn[:], yn[:], bcf(b2_sb[:]), ALU.add))
            do(v.tensor_tensor(xn[:], xn[:], yn[:], ALU.add))
            layernorm(0).then_inc(ev("x1_ready"), 1)
            dve.wait_ge(ev("x1T"), 1)
            take_xT(ev("x1T_ready"))
            with dve.Fori(0, T) as t:
                dve.wait_ge(ev("y_mm"), t + 1)
                dve.wait_ge(ev("y_wrote"), t * 16)
                v.tensor_copy(cn[:, ds(t, 1)], bank[0:P, 4, 0:1])
                v.tensor_copy(Yt.rearrange("p (b w) -> p b w", b=3), bank[0:P, 1:4, 0:R * YW // 3]).then_inc(ev("y_copied"), 1)
            spread("l1", 2, 5, relational)
            dve.wait_ge(ev("l1_sum"), 1)
            dve.wait_ge(ev("y_copied"), T)
            for b, (t0, t1) in enumerate(((0, HC), (HC, T))):
                part = bank[0:P, b, 0:(t1 - t0) * 2 * F].rearrange("p (t w) -> p t w", w=2 * F)
                do(v.tensor_tensor(yn[:, t0:t1, :], part[:, :, F:2 * F], cn[:, t0:t1].unsqueeze(2).to_broadcast([P, t1 - t0, F]), ALU.mult))
                do(v.tensor_tensor(yn[:, t0:t1, :], part[:, :, 0:F], yn[:, t0:t1, :], ALU.add))
            do(v.tensor_tensor(xn[:], xn[:], yn[:], ALU.add))
            layernorm(1).then_inc(ev("tab2"), 1)
            spread("l2", 3, 2, weighted)
            dve.wait_ge(ev("l2_sum"), 1)
            dve.wait_ge(ev("tab2"), 1)
            do(v.tensor_tensor(yn[:], agg(), bcf(l2w_sb[:]), ALU.mult))
            do(v.tensor_tensor(yn[:], yn[:], xn[:], ALU.add))
            do(v.tensor_scalar(tab[:], xn[:], slw_sb[:], None, ALU.mult))
            do(v.tensor_tensor(yn[:], yn[:], tab[:], ALU.add))
            do(v.tensor_scalar(yn[:], yn[:], 0.0, 1.0, ALU.max, ALU.min))
            do(v.tensor_tensor(xn[:], xn[:], yn[:], ALU.add))
            layernorm(2).then_inc(ev("tab3"), 1)
            do(v.memset(Macc, 0.0))
            spread("l3", 4, 0, plain)
            for h in range(2):
                dve.wait_ge(s_z["l3"][h], TURNS)
            do(v.memset(big[0:P, :], 0.0))

            chA, nA = ev("A_dve"), [0]

            def values(s):
                g = dve.value_load(sched[0:1, ds(s, 1)], min_val=0, max_val=GROUPS - 1)
                t = dve.value_load(sched[0:1, ds(s + STEPS, 1)], min_val=0, max_val=T)
                return g, t

            def onehot(o, place, col, s, nth, t, g):
                v.tensor_scalar(col, place[:, ds(g * G, G)], tile_id[:, ds(t, 1)], None, ALU.subtract).then_inc(nth, 1)
                dve.wait_ge(nth, s + 1)
                return v.tensor_tensor(o, iota[0:P, 0:P].unsqueeze(1).to_broadcast([P, G, P]),
                                       col.unsqueeze(2).to_broadcast([P, G, P]), ALU.is_equal)

            def a_product(s, sl):
                g, t = values(s)
                dve.wait_ge(ev("A_w"), s + 1)
                xs = edge_x[:, ds(g * G, G), :].unsqueeze(3)
                v.tensor_tensor(e2[:, 0:2, :].rearrange("p g (i o) -> p g i o", i=F), bank[0:P, 0, :].rearrange("p (g i o) -> p g i o", g=2, i=F), xs[:, 0:2].to_broadcast([P, 2, F, F]), ALU.mult)
                v.tensor_tensor(e2[:, 2, :].rearrange("p (i o) -> p i o", i=F), bank[0:P, 1, 0:FF].rearrange("p (i o) -> p i o", i=F), xs[:, 2].to_broadcast([P, F, F]), ALU.mult).then_inc(ev("A_e2"), 1)
                onehot(SE[sl], dst_end, dcol, s, chA, t, g).then_inc(ev("A_se"), 1)

            def a_scan(s, sl, row_count):
                g = dve.value_load(sched[0:1, ds(s, 1)], min_val=0, max_val=GROUPS - 1)
                dve.wait_ge(ev(f"A_pen{sl}"), row_count)
                dve.wait_ge(ev("A_tr"), s + 1)
                dve.wait_ge(ev("A_trb"), s)
                for half in range(2):
                    ins = v.tensor_tensor_scan(run_max[:, half, :], rows[sl], bank[:, 2 + half, 0:GE], carry[:, half, ds(g, 1)], ALU.add, ALU.max)
                ins.then_inc(ev("A_scan"), 1)
                dve.wait_ge(ev("A_scan"), s + 1)
                v.tensor_copy(carry[:, :, ds(g + 1, 1)], run_max[:, :, GE - 1:GE]).then_inc(ev("A_carry"), 1)
                dve.wait_ge(ev("A_carry"), s + 1)

            def a_add(s, sl):
                t = dve.value_load(sched[0:1, ds(s + STEPS, 1)], min_val=0, max_val=T)
                dve.wait_ge(ev("A_sc"), s + 1)
                v.tensor_tensor(Macc[:, ds(t, 1), :], bank[0:P, 6 + sl, 0:FF].unsqueeze(1), Macc[:, ds(t, 1), :], ALU.add).then_inc(ev("A_add"), 1)

            a_product(0, 0)
            a_scan(0, 0, 16)
            a_product(1, 1)
            with dve.Fori(0, STEPS // 2 - 1) as it:
                for sl in (1, 0):
                    s = it * 2 + (1 if sl else 2)
                    a_scan(s, sl, it * 16 + (16 if sl else 32))
                    a_product(s + 1, 1 - sl)
                    dve.wait_ge(ev("A_add"), s - 1)
                    a_add(s - 1, 1 - sl)
            a_scan(STEPS - 1, 1, 16 * (STEPS // 2))
            for s in (STEPS - 2, STEPS - 1):
                dve.wait_ge(ev("A_add"), s)
                a_add(s, s % 2)
            dve.wait_ge(ev("A_add"), STEPS)

            chB = ev("B_dve")

            def b_front(s, sl, row_count):
                g, t = values(s)
                dve.wait_ge(ev(f"B_row{sl}"), row_count)
                dve.wait_ge(ev("B_mg"), s)
                v.tensor_scalar(ST, rows[sl][0:P, :], node_id[:, ds(t, 1)], None, ALU.is_equal).then_inc(ev("B_st"), 1)
                onehot(SB[sl], dstf, dcolb, s, chB, t, g)
                dve.wait_ge(ev("B_w"), s + 1)
                dve.wait_ge(ev("B_p"), s)
                xs = edge_x[:, ds(g * G, G), :].unsqueeze(3)
                v.tensor_tensor(em, bank[0:P, 0:3, :].rearrange("p g (i w) -> p g i w", i=F), xs.to_broadcast([P, G, F, 2 * F]), ALU.mult).then_inc(ev("B_em"), 1)
                dve.wait_ge(ev("B_em"), s + 1)
                dve.wait_ge(ev("B_mg"), s + 1)
                v.tensor_tensor(EP[sl][:, 0:2, :, 0:F], em[:, 0:2, :, 0:F], bank[0:P, 3, :].rearrange("p (g i o) -> p g i o", g=2, i=F), ALU.subtract)
                v.tensor_tensor(EP[sl][:, 2, :, 0:F], em[:, 2, :, 0:F], bank[0:P, 4, 0:FF].rearrange("p (i o) -> p i o", i=F), ALU.subtract).then_inc(ev("B_d"), 1)

            def b_add(s, sl):
                t = dve.value_load(sched[0:1, ds(s + STEPS, 1)], min_val=0, max_val=T)
                dve.wait_ge(ev("B_sc"), s + 1)
                v.tensor_tensor(sums[:, ds(t, 1), :, :], bank[0:P, 5 + sl, :].rearrange("p (u i w) -> p u i w", u=1, i=F), sums[:, ds(t, 1), :, :], ALU.add).then_inc(ev("B_add"), 1)

            b_front(0, 0, 16)
            b_front(1, 1, 16)
            with dve.Fori(0, STEPS // 2 - 1) as it:
                for sl in range(2):
                    s = it * 2 + sl
                    dve.wait_ge(ev("B_add"), s)
                    b_add(s, sl)
                    b_front(s + 2, sl, it * 16 + 32)
            for s in (STEPS - 2, STEPS - 1):
                dve.wait_ge(ev("B_add"), s)
                b_add(s, s % 2)
            dve.wait_ge(ev("B_add"), STEPS)
            den, num = sums[:, 0:T, :, 0:F], sums[:, 0:T, :, F:2 * F]
            do(v.tensor_scalar(den, den, TINY, None, ALU.max))
            do(v.reciprocal(den, den))
            do(v.tensor_tensor(num, num, den, ALU.mult))
            do(v.tensor_reduce(yn[:], num.rearrange("p t i o -> p t o i"), X, ALU.add))
            do(v.tensor_tensor(xn[:], xn[:], yn[:], ALU.add))
            layernorm(3).then_inc(ev("tab4"), 1)

        @block.tensor
        def _(pe):
            mm = nc.tensor.matmul
            idn = ident[0:P, 0:P]
            pe.wait_ge(s_in, 16 * (N_LOADS - 1))
            pe.wait_ge(ev("inc_row"), 1)
            for i in range(3):
                ins = mm(bank[0:SROWS, i, 0:GROUPS], ones, grow[0:1, i, :], start=True, stop=True)
            ins.then_inc(ev("inc_bc"), 1)
            mm(bank[0:F, 3, 0:3], Ws_sb, WaT_sb, start=True, stop=True).then_inc(ev("attn_rows"), 1)
            pe.wait_ge(ev("attn_rep"), 1)
            mm(bank[0:P, 4, 0:F], A2_rep, ident[0:F, 0:F], start=True, stop=True).then_inc(ev("attn_row"), 1)
            mm(bank[0:R, 5, 0:FF], wcT_sb, VT_sb, start=True, stop=True).then_inc(ev("rel_sum"), 1)

            def summed(p, parts, done):
                pe.wait_ge(s_z[p][0], 1)
                for b, c0, w in parts:
                    mm(bank[0:P, b, 0:w], zeros[:, 0:P], zeros[:, 0:w], start=True, stop=False, skip_group_check=True)
                total = sum(w for _, _, w in parts)
                with pe.Fori(0, TURNS) as it:
                    for h, (k0, n) in enumerate(HALVES):
                        pe.wait_ge(s_z[p][h], it + 1)
                        for k in range(n):
                            for b, c0, w in parts:
                                src = mask[h][:, k, :] if p == "deg" else Z[h].rearrange("p a b c -> p (a b c)")[:, k * total + c0:k * total + c0 + w]
                                ins = mm(bank[0:P, b, 0:w], S[h][:, k, :], src, start=False, stop=False, skip_group_check=True)
                        ins.then_inc(s_mm[p][h], 1)
                for b, c0, w in parts:
                    ins = mm(bank[0:P, b, 0:w], zeros[:, 0:P], zeros[:, 0:w], start=False, stop=True, skip_group_check=True)
                ins.then_inc(done, 1)

            def transpose_nodes(src, done):
                for t in range(T):
                    ins = nc.tensor.transpose(bank[0:F, 1 + t // TB, (t % TB) * P:(t % TB + 1) * P], src[:, t, :], idn)
                ins.then_inc(done, 1)

            summed("deg", [(0, 0, T)], ev("deg_sum"))
            one = [(0, 0, T * F)]
            summed("l0a", one, ev("l0a_sum"))
            pe.wait_ge(ev("ax_ready"), 1)
            transpose_nodes(yn, ev("axT"))
            pe.wait_ge(ev("xT_ready"), 1)
            for b in range(NB + 1):
                w = min(TBW, N - b * TBW)
                ins = mm(bank[0:H1, b, 0:w], W1_sb, xT[:, b * TBW:b * TBW + w], start=True, stop=True)
            ins.then_inc(ev("h_sum"), 1)
            pe.wait_ge(ev("hT_ready"), 1)
            for t in range(T):
                ins = mm(bank[0:P, 7, t * F:(t + 1) * F], hT[:, t * P:(t + 1) * P], W2_sb, start=True, stop=True)
            ins.then_inc(ev("z_sum"), 1)
            summed("l0b", one, ev("l0b_sum"))
            pe.wait_ge(ev("x1_ready"), 1)
            transpose_nodes(xn, ev("x1T"))
            pe.wait_ge(ev("x1T_ready"), 1)
            pe.wait_ge(ev("round_trips"), 16 * 6)
            with pe.Fori(0, T) as t:
                pe.wait_ge(ev("y_src"), t + 1)
                pe.wait_ge(ev("y_copied"), t)
                w = R * YW // 3
                for b in range(3):
                    mm(bank[0:P, 1 + b, 0:w], xTs, Tall.rearrange("i r w -> i (r w)")[:, b * w:(b + 1) * w], start=True, stop=True)
                mm(bank[0:P, 4, 0:1], xTs, A_sb[:, 2:3], start=True, stop=True).then_inc(ev("y_mm"), 1)
            summed("l1", [(0, 0, HC * 2 * F), (1, HC * 2 * F, (T - HC) * 2 * F)], ev("l1_sum"))
            summed("l2", one, ev("l2_sum"))

            def a_weights(s, sl, ef_count):
                pe.wait_ge(ev(f"A_ef{sl}"), ef_count)
                pe.wait_ge(ev("A_e2"), s)
                for k in range(G):
                    ins = mm(bank[0:P, k // 2, (k % 2) * FF:(k % 2 + 1) * FF], efs[sl][:, k * P:(k + 1) * P], Wl3[:, :, 0, :], start=True, stop=True)
                ins.then_inc(ev("A_w"), 1)

            def a_transpose(s):
                pe.wait_ge(ev("A_e2"), s + 1)
                pe.wait_ge(ev("A_scan"), s)
                for half in range(2):
                    for k in range(G):
                        ins = nc.tensor.transpose(bank[:, 2 + half, k * P:(k + 1) * P], e2[:, k, half * 128:(half + 1) * 128], idn)
                ins.then_inc(ev("A_tr"), 1)

            def a_back(s):
                pe.wait_ge(ev("A_scan"), s + 1)
                pe.wait_ge(ev("A_copy"), s)
                for half in range(2):
                    for k in range(G):
                        c0 = (k % 2) * FF + half * 128
                        ins = nc.tensor.transpose(bank[0:P, 4 + k // 2, c0:c0 + 128], run_max[:, half, k * P:(k + 1) * P], ident[:])
                ins.then_inc(ev("A_trb"), 1)

            def a_sum(s, sl, two_before):
                pe.wait_ge(ev("A_copy"), s + 1)
                pe.wait_ge(ev("A_se"), s + 1)
                if two_before is not None:
                    pe.wait_ge(ev("A_add"), two_before)
                for k in range(G):
                    ins = mm(bank[0:P, 6 + sl, 0:FF], SE[sl][:, k, :], run_maxT[:, k, :], start=(k == 0), stop=(k == G - 1))
                ins.then_inc(ev("A_sc"), 1)

            a_weights(0, 0, 16)
            a_transpose(0)
            a_weights(1, 1, 16)
            a_back(0)
            a_sum(0, 0, None)
            with pe.Fori(0, STEPS // 2 - 1) as it:
                for sl in (1, 0):
                    s = it * 2 + (1 if sl else 2)
                    a_transpose(s)
                    a_weights(s + 1, 1 - sl, it * 16 + 32)
                    a_back(s)
                    a_sum(s, sl, s - 1)
            a_transpose(STEPS - 1)
            a_back(STEPS - 1)
            a_sum(STEPS - 1, 1, STEPS - 2)
            pe.wait_ge(ev("A_add"), STEPS)

            def b_front(s, sl, ef_count):
                pe.wait_ge(ev(f"B_ef{sl}"), ef_count)
                pe.wait_ge(ev("B_em"), s)
                for k in range(G):
                    ins = mm(bank[0:P, k, :], efs[sl][:, k * P:(k + 1) * P], Wl3[:].rearrange("k i c o -> k (i c o)"), start=True, stop=True)
                ins.then_inc(ev("B_w"), 1)
                t = pe.value_load(sched[0:1, ds(s + STEPS, 1)], min_val=0, max_val=T)
                pe.wait_ge(ev("B_st"), s + 1)
                pe.wait_ge(ev("B_d"), s)
                for k in range(G):
                    ins = mm(bank[0:P, 3 + k // 2, (k % 2) * FF:(k % 2 + 1) * FF], ST[:, k * P:(k + 1) * P], Macc[:, ds(t, 1), :].rearrange("p u w -> p (u w)"), start=True, stop=True)
                ins.then_inc(ev("B_mg"), 1)

            def b_sum(s, sl, two_before):
                pe.wait_ge(ev("B_p"), s + 1)
                if two_before is not None:
                    pe.wait_ge(ev("B_add"), two_before)
                for k in range(G):
                    ins = mm(bank[0:P, 5 + sl, :], SB[sl][:, k, :], EP[sl][:, k, :, :].rearrange("p i w -> p (i w)"), start=(k == 0), stop=(k == G - 1))
                ins.then_inc(ev("B_sc"), 1)

            b_front(0, 0, 16)
            b_front(1, 1, 16)
            b_sum(0, 0, None)
            b_front(2, 0, 32)
            b_sum(1, 1, None)
            with pe.Fori(0, STEPS // 2 - 2) as it:
                b_front(it * 2 + 3, 1, it * 16 + 32)
                b_sum(it * 2 + 2, 0, it * 2 + 1)
                b_front(it * 2 + 4, 0, it * 16 + 48)
                b_sum(it * 2 + 3, 1, it * 2 + 2)
            b_front(STEPS - 1, 1, 16 * (STEPS // 2))
            b_sum(STEPS - 2, 0, STEPS - 3)
            b_sum(STEPS - 1, 1, STEPS - 2)


def kernel(**inputs):
    import numpy as np
    import concourse.bacc as bacc
    from concourse.bass_utils import run_bass_kernel_spmd as run

    a = {k: np.asarray(v) for k, v in inputs.items()}

    def by_column(e):
        return np.ascontiguousarray(np.moveaxis(e.reshape(C, P, *e.shape[1:]), 0, 1))

    dst, ef = a["dst"], a["edge_attr_16"]
    none = np.full(1, -1, dst.dtype)
    laid = {
        "x": a["x"], "src_pc": by_column(a["src"]), "dst_pc": by_column(dst),
        "dst_next_pc": by_column(np.concatenate([dst[1:], none])), "dst_prev_pc": by_column(np.concatenate([none, dst[:-1]])),
        "group_ends": np.stack([dst[0::GE], dst[GE - 1::GE]]), "ef_pc": by_column(ef),
        "efT": np.concatenate([ef.T, np.ones((1, E), ef.dtype)]), "type_pc": by_column(a["edge_type_90"]),
        "weight_pc": by_column(a["edge_weight"]),
        "W1": a["L0_gnn_W1"], "b1": a["L0_gnn_b1"].reshape(H1, 1), "W2": a["L0_gnn_W2"], "b2": a["L0_gnn_b2"].reshape(1, F),
        "Ws": a["L1_gnn_Ws"], "WaT": a["L1_gnn_Wa"].reshape(3, F).T,
        "VT": a["L1_gnn_weight"].reshape(F, B, F).transpose(1, 0, 2).reshape(B, FF), "wcompT": a["L1_gnn_w_comp"].T,
        "l2w": a["L2_gnn_weight"].reshape(1, F), "slw": a["L2_gnn_self_loop_weight"].reshape(1, 1),
        "Wmsg": a["L3_gnn_W_msg"], "bmsg": a["L3_gnn_b_msg"].reshape(1, FF),
        "Wattn": a["L3_gnn_W_attn"], "battn": a["L3_gnn_b_attn"].reshape(1, FF),
    }
    nc = bacc.Bacc("TRN2", target_bir_lowering=False, num_devices=1)
    arrays, args = {}, []
    for name, v in laid.items():
        v = np.ascontiguousarray(v)
        arrays[f"in_{name}"] = v
        args.append(nc.dram_tensor(f"in_{name}", v.shape, mybir.dt.from_np(v.dtype), kind="ExternalInput").ap())
    out = nc.dram_tensor("out_0", (N, F), FP32, kind="ExternalOutput").ap()
    build(nc, *args, out)
    return run(nc, [arrays], core_ids=[0]).results[0]["out_0"]
```

```python
import concourse.bass as bass
from concourse import mybir
from contextlib import ExitStack

FP32 = mybir.dt.float32
BF16 = mybir.dt.bfloat16
I32 = mybir.dt.int32
U32 = mybir.dt.uint32
ALU = mybir.AluOpType
ACT = mybir.ActivationFunctionType
X = mybir.AxisListType.X
ds = bass.ds
DVE, PE, ACTE, SP = mybir.EngineType.DVE, mybir.EngineType.PE, mybir.EngineType.Activation, mybir.EngineType.SP

N, E, F, H1, R, B = 3125, 103125, 16, 32, 90, 30
P = 125
T = N // P
C = E // P
G = 3
GROUPS = C // G
GE = G * P
PARTS = 5
SLOTS = PARTS * G
TURNS = C // SLOTS
TE_PARTS = 2
STEPS = GROUPS + T
BLOCKS = STEPS // PARTS
SROWS = 100
SCOLS = STEPS // SROWS
FF = F * F
YW = F + 1
TB = 4
TBW = TB * P
NB = T // TB
EXTRA = STEPS - GROUPS
SPLIT_A, SPLIT_B = 5, E // 5
PIECE = 1875
PIECES = SPLIT_B // PIECE
KW = 6 * F + 3
NEG = -3.0e38
EPS = 1e-5
TINY = 1e-30
ROUND = 12582912.0


class Chain:

    def __init__(self, engine, sem):
        self.engine, self.sem, self.n = engine, sem, 0

    def __call__(self, ins):
        self.n += 1
        ins.then_inc(self.sem, 1)
        self.engine.wait_ge(self.sem, self.n)


class Trips(Chain):

    def __call__(self, ins):
        self.n += 16
        ins.then_inc(self.sem, 16)
        self.engine.wait_ge(self.sem, self.n)


class Signal:

    def __init__(self, sem, credit=0, base=0):
        self.sem, self.credit, self.base = sem, credit, base

    def give(self, engine):
        engine.sem_inc(self.sem, self.credit)

    def wait(self, engine, n):
        engine.wait_ge(self.sem, n + (self.credit + self.base))

    def on(self, ins):
        ins.then_inc(self.sem, 1)


class LoopChain:

    def __init__(self, engine, sem, turn, per_turn, base=0):
        self.engine, self.sem, self.value = engine, sem, turn * per_turn + base

    def __call__(self, ins):
        ins.then_inc(self.sem, 1)
        self.value = self.value + 1
        self.engine.wait_ge(self.sem, self.value)


class Carve:

    def __init__(self, arena):
        self.arena, self.at = arena, 0

    def __call__(self, rows, *shape, dt=FP32):
        n = 1
        for k in shape:
            n *= k
        words = n if dt != BF16 else (n + 1) // 2
        ap = self.arena[0:rows, self.at:self.at + words]
        self.at += words
        assert self.at <= self.arena.shape[1], (self.at, self.arena.shape)
        if dt != FP32:
            ap = ap.bitcast(dt)[:, 0:n]
        names = "abcd"[:len(shape)]
        if len(shape) > 1:
            ap = ap.rearrange(f"p ({' '.join(names)}) -> p {' '.join(names)}", **dict(zip(names[1:], shape[1:])))
        return ap


def build(nc, x, src_pc, dst_pc, dst_next_pc, src_flat, dst_flat, dst_prev_flat, group_ends, ef_pc, efT, type_pc,
          weight_pc, W1, b1, W2, b2, Ws, WaT, VT, wcompT, l2w, slw, Wmsg, bmsg, Wattn, battn, out):
    ctx = ExitStack()
    with ctx:
        def sb(name, shape, dt=FP32):
            return ctx.enter_context(nc.sbuf_tensor(name, shape, dt))

        def sem(name):
            return ctx.enter_context(nc.semaphore(name))

        def dram(name, shape, dt=FP32):
            return nc.dram_tensor(name, shape, dt, kind="Internal").ap()

        table = [dram(f"table{i}", (N, F)) for i in range(4)]
        rel_table = dram("rel_table", (N * R, YW))
        rel_flat = dram("rel_flat", (F, R, F))
        pen_dram = dram("pen_dram", (1, E))
        slo_dram = dram("slo_dram", (1, E), BF16)
        sched_dram = dram("sched_dram", (2, SCOLS, SROWS), I32)
        ef_parts = dram("ef_parts", (KW, E), BF16)

        ident = sb("ident", [128, 128])
        iota = sb("iota", [128, 128])
        pcol = sb("pcol", [128, 1])
        step_base = sb("step_base", [P, STEPS])
        step_node = sb("step_node", [P, STEPS])
        step_dst = sb("step_dst", [P, STEPS * G, 2])
        src_i = sb("src_i", [P, C + SLOTS], I32)
        rel_idx = sb("rel_idx", [P, C + SLOTS], I32)
        shi = sb("shi", [P, C])
        edge_w = sb("edge_w", [P, C])
        att = sb("att", [P, C])
        att_src = sb("att_src", [P, C])
        xn = sb("xn", [P, T, F])
        tab = sb("tab", [P, T, F])
        yn = sb("yn", [P, T, F])
        nsum = sb("nsum", [P, T + 1, 2 * F])
        nt = [sb(f"nt{i}", [P, T]) for i in range(3)]
        dinv = sb("dinv", [P, T])
        cn = sb("cn", [P, T])
        b2_sb, l2w_sb, slw_sb = sb("b2_sb", [P, F]), sb("l2w_sb", [P, F]), sb("slw_sb", [P, 1])
        a2_row = sb("a2_row", [P, F])
        carry = sb("carry", [128, 2, GROUPS + 1])
        sched = sb("sched", [1, 2 * STEPS], I32)
        W6 = sb("W6", [KW, 2 * FF], BF16)
        ring = sb("ring", [P, SLOTS, YW])
        stage = sb("stage", [P, SLOTS], I32)

        wide = sb("wide", [128, C * F + (T + 1) * 2 * FF])
        edge_x, big = wide[:, 0:C * F], wide[:, C * F:]
        both = wide[0:P, 0:2 * C * F].rearrange("p (h c f) -> p c h f", h=2, f=F)
        rows_of = edge_x[0:P, :].rearrange("p (c f) -> p c f", f=F)
        cut = Carve(edge_x)
        dst_i, nxt_i, neq_i = (cut(P, C, dt=I32) for _ in range(3))
        src_f, dst_f, prv_f = (cut(P, C, dt=I32) for _ in range(3))
        tmpf, slo = cut(P, C), cut(P, C)
        dsts = cut(P, C, 2)
        step_row = cut(1, 2 * STEPS)
        slo16 = cut(P, C, dt=BF16)
        grow = cut(1, 5, GROUPS)
        gcmp = cut(SROWS, 2, GROUPS)
        gends = cut(1, 2, GROUPS, dt=I32)
        sch = cut(SROWS, 12)
        sch_i = cut(SROWS, 2 * SCOLS, dt=I32)
        iota_i = cut(128, 128, dt=I32)
        ones = cut(1, P)
        Ws_sb, WaT_sb = cut(F, F), cut(F, 3)
        A2_rep = cut(F, P)
        VT_sb, wcT_sb, rel_sb = cut(B, FF), cut(B, R), cut(R, FF)

        ef_sb = big[0:P, 0:C * F].rearrange("p (c f) -> p c f", f=F)
        scaled = big[0:P, 0:C * F].rearrange("p (c f) -> p c f", f=F)
        Macc = big[0:P, 0:(T + 1) * FF].rearrange("p (t w) -> p t w", w=FF)
        sums = big[0:P, :].rearrange("p (t i w) -> p t i w", i=F, w=2 * F)
        cut = Carve(big)
        xT = cut(F, N)
        hT = cut(H1, N)
        xTs = [cut(F, P) for _ in range(2)]
        Yt = [cut(P, R * YW) for _ in range(2)]

        msplit = sb("msplit", [128, (T + 1) * FF])
        M16 = [msplit[0:P, i * (T + 1) * FF // 2:(i + 1) * (T + 1) * FF // 2].bitcast(BF16).rearrange("p (t w) -> p t w", w=FF) for i in range(2)]
        cut = Carve(msplit)
        W3 = cut(F + 1, F, 2, F)
        W3_rest = cut(F + 1, 2 * FF)
        W3_parts = [cut(F + 1, 2 * FF, dt=BF16) for _ in range(3)]
        parts = cut(P, 3, T * F, dt=BF16)
        cut = Carve(msplit)
        SR = F * SPLIT_A
        f_x, f_rest = cut(SR, PIECE), cut(SR, PIECE)
        f_parts = [cut(SR, PIECE, dt=BF16) for _ in range(3)]

        work = sb("work", [128, 8300])
        cut = Carve(work)
        lo_oh = [cut(P, SLOTS, P, dt=BF16) for _ in range(2)]
        hi_oh = [cut(P, SLOTS, T, dt=BF16) for _ in range(2)]
        d_lo, d_hi = cut(P, C), cut(P, C)
        cut = Carve(work)
        S = cut(P, SLOTS, P)
        slo_row = cut(P, TE_PARTS * GE, dt=BF16)
        oh = cut(P, TE_PARTS * GE, dt=BF16)
        mask = cut(P, TE_PARTS * G, T)
        picked = [cut(P, G, T, F) for _ in range(TE_PARTS)]
        Tall = cut(F, R, YW)
        W1_sb, W2_sb, b1_sb, A_sb = cut(F, H1), cut(H1, F), cut(H1, 1), cut(F, 3)
        ones16 = cut(P, C, dt=BF16)
        cut = Carve(work)
        efs = [cut(KW, GE, dt=BF16) for _ in range(2)]
        rows = [cut(128, GE) for _ in range(2)]
        at_b = cut.at
        e2 = cut(P, G, FF)
        run_max = cut(128, 2, GE)
        run_maxT = cut(P, G, FF)
        SE = [cut(P, G, P) for _ in range(2)]
        cut = Carve(work)
        cut.at = at_b
        ST = cut(P, GE, dt=BF16)
        SB = [cut(P, G, P) for _ in range(2)]
        em = [cut(P, G, F, 2 * F) for _ in range(2)]
        EP = [cut(P, G, F, 2 * F) for _ in range(2)]

        bank = ctx.enter_context(nc.psum_tensor("bank", [128, 8, 512], FP32))

        names = {}

        def ev(name):
            if name not in names:
                names[name] = sem(name)
            return names[name]

        PASSES = ["l0a", "l0b", "l1", "l2"]
        for n in ("inputs_dst", "inputs", "dve_chain", "pool_chain", "act_chain", "consts",
                  "pen_ready", "slo_ready", "sched_ready", "rel_ready", "attn_rows", "attn_rep", "w3_ready", "w6_ready",
                  "attn_row", "a2_ready", "att_product", "rel_sum", "inc_row", "step_row", "step_bc", "step_base_ready", "step_dst_ready", "inc_bc", "round_trips", "round_trips_a", "deg_ready", "deg_root",
                  "ax_ready", "axT", "xT_ready", "h_sum", "hT_ready", "z_sum",
                  "x1_ready", "x1T", "x1T_ready", "relidx_ready",
                  "tab", "wrote",
                  "y_last_wrote", "f_in", "f_split", "f_out", "f_chain", "c_sum",
                  "var", "root",
                  "A_ef0", "A_ef1", "A_pen0", "A_pen1", "A_dve", "A_carry", "A_se", "A_tr", "A_trb",
                  "B_ef0", "B_ef1", "B_row0", "B_row1", "B_dve", "B_ex", "B_sc"):
            ev(n)
        s_slot = [sem(f"gathered_slot{k}") for k in range(SLOTS)]
        s_part = [sem(f"part_emptied{i}") for i in range(PARTS)]
        s_chain = sem("pass_chain")
        deg_made, deg_used = Signal(sem("deg_onehots")), Signal(sem("deg_multiplied"), 2)
        s_S, s_sum = sem("onehots_made"), sem("block_multiplied")
        s_row, s_mask = sem("slo_rows"), sem("tile_masks")
        s_te = [sem(f"te_gathered{i}") for i in range(TE_PARTS)]
        m_oh, m_pick = sem("src_onehots"), [sem(f"picked{i}") for i in range(TE_PARTS)]
        TE_NO = {"l0a": 0, "l0b": 1, "l2": 2}
        g_oh = {p: Signal(m_oh, 1, n * (TURNS + 1)) for p, n in TE_NO.items()}
        g_pick = {p: [Signal(m_pick[i], 1, n * (TURNS + 1)) for i in range(TE_PARTS)] for p, n in TE_NO.items()}
        y_src, y_mm, y_copied = Signal(sem("y_src")), Signal(sem("y_mm"), 2), Signal(sem("y_copied"), 2)
        y_wrote = [sem("y_wrote0"), sem("y_wrote1")]
        l3_rows = sem("l3_rows")
        A_w, A_scan = Signal(sem("A_w"), 2), Signal(sem("A_scan"), 2)
        A_e2, A_copy, A_sc, A_add = (Signal(sem(n), 1) for n in ("A_e2", "A_copy", "A_sc", "A_add"))
        B_w, B_st, B_p = Signal(sem("B_w"), 2), Signal(sem("B_st"), 2), Signal(sem("B_p"), 2)
        B_mg, B_em, B_d, B_add = (Signal(sem(n), 1) for n in ("B_mg", "B_em", "B_d", "B_add"))

        for n in ("settled", "parts_ready", "setup_free", "M_ready"):
            ev(n)
        N_FIRST, N_LOADS, N_TRIPS = 8, 18, 4

        block = ctx.enter_context(nc.Block())
        PASS_NO = {"l0a": 0, "l0b": 1, "l1": 2, "l2": 3, "l3": 4}
        TE_SLOTS = TE_PARTS * G

        def fetched_parts(p):
            return range(0 if p in ("l1", "l3") else TE_PARTS, PARTS)

        def settle(engine):
            engine.sem_inc(ev("settled"), 1)

        def scheduled(engine, first, n, greatest):
            return nc.values_load_multi_w_load_instructions(
                sched[0:1, ds(first, n)], engines=(engine,), min_val=0, max_val=greatest,
                skip_runtime_bounds_check_because="the schedule is clamped when it is computed")[1]

        def groups_of(engine, step, n):
            return scheduled(engine, step, n, GROUPS - 1)

        def tiles_of(engine, step, n):
            return scheduled(engine, step + STEPS, n, T)

        def fetches_before(p, part):
            return sum(TURNS for q in PASS_NO if PASS_NO[q] < PASS_NO[p] and part in fetched_parts(q))

        def parts_before(p, part):
            return (TURNS + 1) * sum(1 for q in PASS_NO if PASS_NO[q] < PASS_NO[p] and part in fetched_parts(q))

        @block.sync
        def _(sp):
            first = [(dst_i, dst_pc), (gends[0:1, 0, :], group_ends[0:1, :]), (gends[0:1, 1, :], group_ends[1:2, :]),
                     (nxt_i, dst_next_pc), (src_i[:, 0:C], src_pc)]
            first += [(t, s.rearrange("u (p c) -> (u p) c", p=P)) for t, s in ((src_f, src_flat), (dst_f, dst_flat), (prv_f, dst_prev_flat))]
            loads = [(xn[:], x.rearrange("(t p) f -> p t f", p=P)),
                     (edge_w[:], weight_pc), (W1_sb, W1), (W2_sb, W2), (b1_sb, b1),
                     (b2_sb[:], b2.to_broadcast([P, F])), (l2w_sb[:], l2w.to_broadcast([P, F])),
                     (slw_sb[:], slw.to_broadcast([P, 1])), (Ws_sb, Ws), (WaT_sb, WaT), (VT_sb, VT),
                     (wcT_sb, wcompT), (rel_idx[:, 0:C], type_pc), (ef_sb, ef_pc)]
            for c, (w, b) in enumerate(((Wattn, battn), (Wmsg, bmsg))):
                loads.append((W3[0:F, :, c, :], w.rearrange("k (i o) -> k i o", i=F)))
                loads.append((W3[F:F + 1, :, c, :], b.rearrange("u (i o) -> u i o", i=F)))
            for d, s in first:
                sp.dma_start(d, s).then_inc(ev("inputs_dst"), 16)
            for d, s in loads:
                sp.dma_start(d, s).then_inc(ev("inputs"), 16)
            assert (len(first), len(loads)) == (N_FIRST, N_LOADS)

            trips = Trips(sp, ev("round_trips"))
            with nc.allow_non_contiguous_dma(reason="edge layout to flat, once"):
                sp.wait_ge(ev("sched_ready"), 1)
                trips(sp.dma_start(sched_dram.rearrange("a c (p u) -> p (a c) u", u=1), sch_i.rearrange("p (a u) -> p a u", u=1)))
                trips(sp.dma_start(sched[:], sched_dram.rearrange("(u a) c p -> u (a c p)", u=1)))
                sp.wait_ge(ev("slo_ready"), 1)
                trips(sp.dma_start(slo_dram.rearrange("u (p c) -> (u p) c", p=P), slo16))
                sp.wait_ge(ev("pen_ready"), 1)
                trips(sp.dma_start(pen_dram.rearrange("u (p c) -> (u p) c", p=P), tmpf))
                sp.wait_ge(ev("w3_ready"), 1)
                for j, i in enumerate((0, 1, 2, 0, 1, 0)):
                    sp.dma_start(W6[j * F:(j + 1) * F, :], W3_parts[i][0:F, :]).then_inc(ev("w6_ready"), 16)
                for i in range(3):
                    sp.dma_start(W6[6 * F + i:6 * F + i + 1, :], W3_parts[i][F:F + 1, :]).then_inc(ev("w6_ready"), 16)
                sp.wait_ge(ev("w6_ready"), 16 * 9)
                for i in range(3):
                    sp.dma_start(ef_parts[6 * F + i:6 * F + i + 1, :].rearrange("u (p c) -> (u p) c", p=P), ones16).then_inc(ev("f_out"), 16)

            def slo_rows(p):
                with sp.Fori(0, TURNS) as it:
                    g_oh[p].wait(sp, it)
                    settle(sp)
                    sp.dma_start(slo_row, slo_dram[:, ds(it * (SLOTS * P), TE_SLOTS * P)].to_broadcast([P, TE_SLOTS * P])).then_inc(s_row, 16)

            for i, p in enumerate(("l0a", "l0b")):
                sp.wait_ge(ev("tab"), i + 1)
                sp.dma_start(table[i].rearrange("(t p) f -> p t f", p=P), tab[:]).then_inc(ev("wrote"), 16)
                slo_rows(p)

            def put_tile(t, par, count):
                y_copied.wait(sp, t + 1)
                settle(sp)
                dst = rel_table.rearrange("(t p r) w -> t p (r w)", p=P, r=R)[ds(t, 1), :, :].rearrange("u p w -> (u p) w")
                sp.dma_start(dst, Yt[par]).then_inc(y_wrote[par], 16)

            with sp.Fori(0, T // 2) as it:
                for par in range(2):
                    put_tile(it * 2 + par, par, None)
            put_tile(T - 1, 0, None)
            efT_v = efT.rearrange("i (a b) -> (i a) b", a=SPLIT_A)
            with sp.Fori(0, PIECES) as it:
                sp.wait_ge(ev("f_chain"), it * 5 + 1)
                settle(sp)
                sp.dma_start(f_x, efT_v[:, ds(it * PIECE, PIECE)]).then_inc(ev("f_in"), 16)
                sp.wait_ge(ev("f_chain"), it * 5 + 6)
                settle(sp)
                for j, i in enumerate((0, 0, 0, 1, 1, 2)):
                    sp.dma_start(ef_parts[j * F:(j + 1) * F, :].rearrange("i (a b) -> (i a) b", a=SPLIT_A)[:, ds(it * PIECE, PIECE)], f_parts[i]).then_inc(ev("f_out"), 16)
            sp.wait_ge(ev("tab"), 3)
            sp.dma_start(table[2].rearrange("(t p) f -> p t f", p=P), xn[:]).then_inc(ev("wrote"), 16)
            slo_rows("l2")
            sp.wait_ge(ev("tab"), 4)
            sp.dma_start(table[3].rearrange("(t p) f -> p t f", p=P), xn[:]).then_inc(ev("wrote"), 16)
            sp.wait_ge(ev("f_out"), 16 * (3 + 6 * PIECES))

            for ph, row_dram, rown, used, row_used, nrow in (("A", pen_dram, "pen", A_w, A_scan, 128), ("B", dst_flat, "row", B_w, B_st, P)):
                with sp.Fori(0, STEPS // 2) as it:
                    groups = groups_of(SP, it * 2, 2)
                    for sl, g in enumerate(groups):
                        used.wait(sp, it * 2 + sl - 1)
                        settle(sp)
                        sp.dma_start(efs[sl], ef_parts[:, ds(g * GE, GE)]).then_inc(ev(f"{ph}_ef{sl}"), 16)
                        row_used.wait(sp, it * 2 + sl - 1)
                        settle(sp)
                        sp.dma_start(rows[sl][0:nrow, :] if ph == "A" else rows[sl][0:nrow, :].bitcast(I32), row_dram[:, ds(g * GE, GE)].to_broadcast([nrow, GE])).then_inc(ev(f"{ph}_{rown}{sl}"), 16)
                (A_add if ph == "A" else B_add).wait(sp, STEPS)
            sp.wait_ge(ev("tab"), 5)
            sp.dma_start(out.rearrange("(t p) f -> p t f", p=P), xn[:]).then_inc(ev("wrote"), 16)
            sp.wait_ge(ev("wrote"), 80)

        @block.gpsimd
        def _(pool):
            do = Chain(pool, ev("pool_chain"))
            do(nc.gpsimd.iota(iota_i, pattern=[[1, 128]], base=0, channel_multiplier=0))
            nc.gpsimd.iota(sch_i[:, 0:SCOLS], pattern=[[SROWS, SCOLS]], base=0, channel_multiplier=1)
            do(nc.gpsimd.tensor_copy(iota[:], iota_i))
            do(nc.gpsimd.iota(iota_i, pattern=[[-1, 128]], base=0, channel_multiplier=1))
            do(nc.gpsimd.tensor_copy(ident[:], iota_i))
            for t, val in ((ones, 1.0), (ones16, 1.0), (src_i[:, C:], 0), (rel_idx[:, C:], 0)):
                nc.gpsimd.memset(t, val)
            nc.gpsimd.memset(carry[:], 0.0).then_inc(ev("consts"), 1)
            pool.wait_ge(ev("inputs"), 16 * N_LOADS)
            pool.wait_ge(ev("a2_ready"), 1)
            nc.gpsimd.tensor_tensor(ef_sb, ef_sb, a2_row[:].unsqueeze(1).to_broadcast([P, C, F]), ALU.mult).then_inc(ev("att_product"), 1)

            def gather(p, source, width, written, count):
                pool.wait_ge(written, count)
                with pool.Fori(0, TURNS) as it:
                    for part in fetched_parts(p):
                        pool.wait_ge(s_part[part], it + (parts_before(p, part) + 1))
                        settle(pool)
                        for k in range(part * G, (part + 1) * G):
                            pool.indirect_dma_start(
                                out=ring[:, k, 0:width], out_offset=None, in_=source,
                                in_offset=bass.IndirectOffsetOnAxis(ap=stage[:, k:k + 1].bitcast(U32), axis=0),
                            ).then_inc(s_slot[k], 16)

            gather("l0a", table[0], F, ev("wrote"), 16)
            gather("l0b", table[1], F, ev("wrote"), 32)
            pool.wait_ge(y_wrote[1], 16 + 16 * (T // 2))
            gather("l1", rel_table, YW, y_wrote[0], 16 + 16 * (T - T // 2))
            gather("l2", table[2], F, ev("wrote"), 48)
            gather("l3", table[3], F, ev("wrote"), 64)
            B_p.give(pool)
            with pool.Fori(0, STEPS // 2) as it:
                for sl in range(2):
                    pool.wait_ge(ev("B_ex"), it * 2 + sl + 1)
                    B_p.on(nc.gpsimd.tensor_tensor(EP[sl][:, :, :, F:2 * F], em[sl][:, :, :, F:2 * F], EP[sl][:, :, :, 0:F], ALU.mult))

        @block.scalar
        def _(act):
            copy = lambda o, i: nc.scalar.activation(o, i, ACT.Copy)

            def sqrt(ready, n, done):
                act.wait_ge(ev(ready), n)
                nc.scalar.activation(nt[1][:], nt[0][:], ACT.Sqrt).then_inc(ev(done), 1)

            def stage_first(p, idx):
                for part in fetched_parts(p):
                    c = part * G
                    copy(stage[:, c:c + G], idx[:, c:c + G]).then_inc(s_part[part], 1)

            def empty_part(p, it, part, idx):
                for k in range(part * G, (part + 1) * G):
                    act.wait_ge(s_slot[k], it * 16 + 16 * (fetches_before(p, part) + 1))
                c, col = part * G, it * SLOTS + part * G
                if p == "l1":
                    copy(att_src[:, ds(col, G)].unsqueeze(2), ring[:, c:c + G, F:F + 1])
                ins = copy(rows_of[:, ds(col, G), :], ring[:, c:c + G, 0:F])
                if p == "l3":
                    ins.then_inc(l3_rows, 1)
                copy(stage[:, c:c + G], idx[:, ds(col + SLOTS, G)]).then_inc(s_part[part], 1)

            def empty(p, idx):
                stage_first(p, idx)
                with act.Fori(0, TURNS) as it:
                    for part in fetched_parts(p):
                        empty_part(p, it, part, idx)

            act.wait_ge(ev("consts"), 1)
            act.wait_ge(ev("inputs_dst"), 16 * N_FIRST)
            act.wait_ge(ev("step_base_ready"), 1)
            with act.Fori(0, BLOCKS) as b:
                for j, g in enumerate(groups_of(ACTE, b * PARTS, PARTS)):
                    s = b * PARTS + j
                    ins = nc.scalar.activation(step_dst[:, ds(s * G, G), :], dsts[:, ds(g * G, G), :], ACT.Identity, bias=step_base[:, ds(s, 1)])
                ins.then_inc(ev("step_dst_ready"), 1)
            sqrt("deg_ready", 1, "deg_root")
            with nc.allow_non_contiguous_dma(reason="edge layout to flat, once"):
                act.wait_ge(ev("rel_ready"), 1)
                act.dma_start(rel_flat.rearrange("i r o -> r i o"), rel_sb.rearrange("r (i o) -> r i o", i=F)).then_inc(ev("setup_free"), 16)
                act.wait_ge(ev("setup_free"), 16)
                act.dma_start(Tall[:, :, 0:F], rel_flat.rearrange("i r o -> (i r) o").rearrange("(r i) o -> i r o", i=F)).then_inc(ev("setup_free"), 16)
            act.wait_ge(ev("tab"), 1)
            empty("l0a", src_i)
            act.wait_ge(ev("h_sum"), 1)
            nc.scalar.activation(hT[:, 0:NB * TBW].rearrange("p (b w) -> p b w", w=TBW), bank[0:H1, 0:NB, 0:TBW], ACT.Relu, bias=b1_sb)
            nc.scalar.activation(hT[:, NB * TBW:N], bank[0:H1, NB, 0:N - NB * TBW], ACT.Relu, bias=b1_sb).then_inc(ev("hT_ready"), 1)
            empty("l0b", src_i)
            sqrt("var", 1, "root")
            act.wait_ge(ev("x1T_ready"), 1)

            def source_tile(t, par):
                y_mm.wait(act, t - 1)
                y_src.on(copy(xTs[par], xT[:, ds(t * P, P)]))

            with act.Fori(0, T // 2) as it:
                for par in range(2):
                    source_tile(it * 2 + par, par)
            source_tile(T - 1, 0)
            act.wait_ge(ev("relidx_ready"), 1)
            empty("l1", rel_idx)
            sqrt("var", 2, "root")
            empty("l2", src_i)
            sqrt("var", 3, "root")
            A_copy.give(act)

            def maxima(s):
                act.wait_ge(ev("A_trb"), s + 1)
                A_sc.wait(act, s)
                copy(run_maxT[:, 0:2, :], bank[0:P, 4, :].rearrange("p (g w) -> p g w", g=2))
                A_copy.on(copy(run_maxT[:, 2, :], bank[0:P, 5, 0:FF]))

            stage_first("l3", src_i)
            for part in range(PARTS):
                empty_part("l3", 0, part, src_i)
            with act.Fori(1, TURNS) as it:
                for part in range(PARTS):
                    empty_part("l3", it, part, src_i)
                    maxima((it - 1) * PARTS + part)
            act.sem_inc(l3_rows, EXTRA)
            with act.Fori((TURNS - 1) * PARTS, STEPS) as s:
                maxima(s)
            with act.Fori(0, STEPS // 2) as it:
                for sl in range(2):
                    B_d.wait(act, it * 2 + sl + 1)
                    nc.scalar.activation(EP[sl][:, :, :, 0:F], EP[sl][:, :, :, 0:F], ACT.Exp).then_inc(ev("B_ex"), 1)
            sqrt("var", 4, "root")

        @block.vector
        def _(dve):
            do = Chain(dve, ev("dve_chain"))
            v = nc.vector
            dve.wait_ge(ev("consts"), 1)
            dve.wait_ge(ev("inputs_dst"), 16 * N_FIRST)

            def quotient(o, i):
                do(v.tensor_scalar(o, i, 1.0 / P, -(P - 1) / (2.0 * P), ALU.mult, ALU.add))
                do(v.tensor_scalar(o, o, ROUND, None, ALU.add))
                do(v.tensor_scalar(o, o, ROUND, None, ALU.subtract))

            do(v.tensor_copy(sch[:, 0:SCOLS], sch_i[:, 0:SCOLS]))
            do(v.tensor_copy(grow[0:1, 0:2, :], gends[0:1, :, :]))
            quotient(grow[0:1, 2:4, :], grow[0:1, 0:2, :])
            do(v.scalar_tensor_tensor(out=grow[0:1, 4, :], in0=grow[0:1, 3, :], scalar=1.0, in1=grow[0:1, 2, :], op0=ALU.add, op1=ALU.subtract))
            do(v.memset(grow[0:1, 3, :], 0.0))
            do(v.tensor_tensor_scan(grow[0:1, 0, :], grow[0:1, 4, :], grow[0:1, 3, :], 0.0, ALU.add, ALU.add))
            do(v.tensor_tensor(grow[0:1, 1, :], grow[0:1, 0, :], grow[0:1, 4, :], ALU.subtract))
            v.tensor_tensor(grow[0:1, 2, :], grow[0:1, 2, :], grow[0:1, 1, :], ALU.subtract).then_inc(ev("inc_row"), 1)
            do(v.tensor_copy(pcol[:], ident[:, 0:1]))
            do(v.tensor_scalar(ident[:], ident[:], 0.0, None, ALU.is_equal))
            do(v.tensor_copy(dsts[:, :, 0], dst_i))
            do(v.tensor_tensor(neq_i, dst_i, nxt_i, ALU.not_equal))
            do(v.scalar_tensor_tensor(out=dsts[:, :, 1], in0=dsts[:, :, 0], scalar=1.0, in1=neq_i, op0=ALU.add, op1=ALU.mult))
            do(v.tensor_scalar(dsts[:, :, 1], dsts[:, :, 1], 1.0, None, ALU.subtract))
            dve.wait_ge(ev("inc_bc"), 1)
            for j in range(SCOLS):
                step = sch[:, j:j + 1]
                do(v.tensor_scalar(gcmp[:, 0, :], bank[0:SROWS, 0, 0:GROUPS], step, None, ALU.is_le))
                do(v.tensor_reduce(sch[:, 3 + j:4 + j], gcmp[:, 0, :], X, ALU.add))
                do(v.scalar_tensor_tensor(out=gcmp[:, 0, :], in0=bank[0:SROWS, 1, 0:GROUPS], scalar=step, in1=gcmp[:, 0, :], op0=ALU.is_le, op1=ALU.subtract))
                do(v.tensor_tensor(gcmp[:, 1, :], bank[0:SROWS, 2, 0:GROUPS], gcmp[:, 0, :], ALU.mult))
                do(v.tensor_reduce(sch[:, 6 + j:7 + j], gcmp[:, 1, :], X, ALU.add))
            do(v.tensor_tensor(sch[:, 6:9], sch[:, 6:9], sch[:, 0:3], ALU.add))
            do(v.tensor_scalar(sch[:, 3:6], sch[:, 3:6], float(GROUPS - 1), None, ALU.min))
            do(v.tensor_scalar(sch[:, 6:9], sch[:, 6:9], float(T), None, ALU.min))
            v.tensor_copy(sch_i, sch[:, 3:9]).then_inc(ev("sched_ready"), 1)
            quotient(shi[:], src_i[:, 0:C])
            quotient(tmpf, src_f)
            do(v.scalar_tensor_tensor(out=slo, in0=tmpf, scalar=-float(P), in1=src_f, op0=ALU.mult, op1=ALU.add))
            v.tensor_copy(slo16, slo).then_inc(ev("slo_ready"), 1)
            dve.wait_ge(ev("round_trips"), 32)
            v.tensor_copy(step_row, sched[:]).then_inc(ev("step_row"), 1)
            dve.wait_ge(ev("step_bc"), 1)
            v.tensor_scalar(step_base[:], bank[0:P, 3, 0:STEPS], -float(P), None, ALU.mult).then_inc(ev("step_base_ready"), 1)
            do(v.tensor_scalar(step_node[:], bank[0:P, 3, 0:STEPS], float(P), None, ALU.mult))
            do(v.tensor_scalar(step_node[:], step_node[:], pcol[0:P, :], None, ALU.add))

            def bct(ap):
                return ap.unsqueeze(2).to_broadcast([P, T, F])

            def bcf(ap):
                return ap.unsqueeze(1).to_broadcast([P, T, F])

            def onehots(b):
                v.tensor_tensor(S, iota[0:P, 0:P].unsqueeze(1).to_broadcast([P, SLOTS, P]),
                                step_dst[:, ds(b * SLOTS, SLOTS), 0:1].to_broadcast([P, SLOTS, P]), ALU.is_equal).then_inc(s_S, 1)

            def block_adds(p, b, tiles, width, link):
                dve.wait_ge(s_sum, b + (PASSES.index(p) * BLOCKS + 1))
                for j, t in enumerate(tiles):
                    at, got = nsum[:, ds(t, 1), 0:width], bank[0:P, 6, j * width:(j + 1) * width].unsqueeze(1)
                    link(v.tensor_tensor(at, got, at, ALU.add))

            WIDTH = {"l0a": F, "l0b": F, "l1": 2 * F, "l2": F}
            ADDS = PARTS
            chained = [0]

            def node_pass(p, prepare=None, prepare_links=0):
                te = p in g_oh
                width = WIDTH[p]
                loop_links = (TE_PARTS if te else 0) + prepare_links + ADDS

                def source_onehot(it):
                    dve.wait_ge(s_row, it * 16 + 16 * (TE_NO[p] * TURNS + 1))
                    g_oh[p].on(v.tensor_scalar(oh, slo_row, pcol[0:P, :], None, ALU.is_equal))

                def turn(it, b, link, more=True):
                    if te:
                        col = it * SLOTS
                        v.tensor_tensor(mask, iota[0:P, 0:T].unsqueeze(1).to_broadcast([P, TE_SLOTS, T]),
                                        shi[:, ds(col, TE_SLOTS)].unsqueeze(2).to_broadcast([P, TE_SLOTS, T]), ALU.is_equal).then_inc(s_mask, 1)
                    if b is not None:
                        for part in fetched_parts(p):
                            dve.wait_ge(s_part[part], b + (parts_before(p, part) + 2))
                        if prepare:
                            prepare(b, link)
                        onehots(b)
                        tiles = tiles_of(DVE, b * PARTS, PARTS)
                    if te:
                        dve.wait_ge(s_mask, it + (TE_NO[p] * TURNS + 1))
                        for i in range(TE_PARTS):
                            dve.wait_ge(s_te[i], it + (TE_NO[p] * TURNS + 1))
                            if i == TE_PARTS - 1 and more:
                                source_onehot(it + 1)
                            sel = mask[:, i * G:(i + 1) * G, :].unsqueeze(3).to_broadcast([P, G, T, F])
                            src = bank[0:P, i * G:(i + 1) * G, 0:T * F].rearrange("p g (t f) -> p g t f", f=F)
                            ins = v.tensor_tensor(picked[i], src, sel, ALU.mult)
                            ins.then_inc(g_pick[p][i].sem, 1)
                            g_pick[p][i].wait(dve, it + 1)
                            link(v.tensor_reduce(rows_of[:, ds(it * SLOTS + i * G, G), :], picked[i].rearrange("p g t f -> p g f t"), X, ALU.add))
                    if b is not None:
                        block_adds(p, b, tiles, width, link)

                if te:
                    g_oh[p].give(dve)
                    for i in range(TE_PARTS):
                        g_pick[p][i].give(dve)
                    source_onehot(0)
                    turn(0, None, LoopChain(dve, s_chain, 0, 0, chained[0]))
                    chained[0] += TE_PARTS
                with dve.Fori(1, TURNS - 1) as it:
                    turn(it, it - 1, LoopChain(dve, s_chain, it - 1, loop_links, chained[0]))
                chained[0] += (TURNS - 2) * loop_links
                turn(TURNS - 1, TURNS - 2, LoopChain(dve, s_chain, 0, 0, chained[0]), more=False)
                chained[0] += loop_links
                last = LoopChain(dve, s_chain, 0, 0, chained[0])
                for part in fetched_parts(p):
                    dve.wait_ge(s_part[part], parts_before(p, part) + TURNS + 1)
                if prepare:
                    prepare(TURNS - 1, last)
                chained[0] += prepare_links
                with dve.Fori(TURNS - 1, BLOCKS) as b:
                    link = LoopChain(dve, s_chain, b - (TURNS - 1), ADDS, chained[0])
                    onehots(b)
                    tiles = tiles_of(DVE, b * PARTS, PARTS)
                    block_adds(p, b, tiles, width, link)
                chained[0] += (BLOCKS - (TURNS - 1)) * ADDS

            def weigh(b, link):
                at = rows_of[:, ds(b * SLOTS, SLOTS), :]
                link(v.tensor_tensor(at, at, edge_w[:, ds(b * SLOTS, SLOTS)].unsqueeze(2).to_broadcast([P, SLOTS, F]), ALU.mult))

            def attend(b, link):
                c = ds(b * SLOTS, SLOTS)
                link(v.tensor_tensor(att_src[:, c], att_src[:, c], att[:, c], ALU.add))
                link(v.tensor_tensor(scaled[:, c, :], rows_of[:, c, :], att_src[:, c].unsqueeze(2).to_broadcast([P, SLOTS, F]), ALU.mult))

            def layernorm(i):
                do(v.tensor_reduce(nt[0][:], xn[:], X, ALU.add))
                do(v.tensor_scalar(nt[0][:], nt[0][:], 1.0 / F, None, ALU.mult))
                do(v.tensor_tensor(xn[:], xn[:], bct(nt[0][:]), ALU.subtract))
                do(v.tensor_tensor(yn[:], xn[:], xn[:], ALU.mult))
                do(v.tensor_reduce(nt[0][:], yn[:], X, ALU.add))
                v.tensor_scalar(nt[0][:], nt[0][:], 1.0 / F, EPS, ALU.mult, ALU.add).then_inc(ev("var"), 1)
                dve.wait_ge(ev("root"), i + 1)
                do(v.reciprocal(nt[2][:], nt[1][:]))
                return v.tensor_tensor(xn[:], xn[:], bct(nt[2][:]), ALU.mult)

            def split(source):
                fl = lambda ap: ap.rearrange("p t f -> p (t f)")
                do(v.tensor_copy(parts[:, 0, :], fl(source)))
                do(v.tensor_tensor(fl(yn[:]), fl(source), parts[:, 0, :], ALU.subtract))
                do(v.tensor_copy(parts[:, 1, :], fl(yn[:])))
                do(v.tensor_tensor(fl(yn[:]), fl(yn[:]), parts[:, 1, :], ALU.subtract))
                do(v.tensor_copy(parts[:, 2, :], fl(yn[:])))

            def take_xT(done):
                v.tensor_copy(xT[:, 0:NB * TBW].rearrange("p (b w) -> p b w", w=TBW), bank[0:F, 1:1 + NB, 0:TBW])
                v.tensor_copy(xT[:, NB * TBW:N], bank[0:F, 1 + NB, 0:N - NB * TBW]).then_inc(done, 1)

            agg = nsum[:, 0:T, 0:F]

            quotient(d_hi, dsts[:, :, 0])
            do(v.scalar_tensor_tensor(out=d_lo, in0=d_hi, scalar=-float(P), in1=dsts[:, :, 0], op0=ALU.mult, op1=ALU.add))
            deg_used.give(dve)

            def degree_onehots(it, par):
                deg_used.wait(dve, it - 1)
                c = ds(it * SLOTS, SLOTS)
                for o, place, w in ((hi_oh, d_hi, T), (lo_oh, d_lo, P)):
                    ins = v.tensor_tensor(o[par], iota[0:P, 0:w].unsqueeze(1).to_broadcast([P, SLOTS, w]),
                                          place[:, c].unsqueeze(2).to_broadcast([P, SLOTS, w]), ALU.is_equal)
                deg_made.on(ins)

            with dve.Fori(0, TURNS // 2) as it:
                for par in range(2):
                    degree_onehots(it * 2 + par, par)
            degree_onehots(TURNS - 1, 0)
            deg_used.wait(dve, TURNS)
            v.tensor_scalar(nt[0][:], bank[0:P, 6, 0:T], 1.0, None, ALU.add).then_inc(ev("deg_ready"), 1)
            dve.wait_ge(ev("inputs"), 16 * N_LOADS)
            do(v.tensor_tensor(tmpf, dst_f, prv_f, ALU.not_equal))
            v.tensor_scalar(tmpf, tmpf, NEG, None, ALU.mult).then_inc(ev("pen_ready"), 1)
            do(v.tensor_copy(slo, rel_idx[:, 0:C]))
            do(v.scalar_tensor_tensor(out=slo, in0=src_i[:, 0:C], scalar=float(R), in1=slo, op0=ALU.mult, op1=ALU.add))
            v.tensor_copy(rel_idx[:, 0:C], slo).then_inc(ev("relidx_ready"), 1)
            dve.wait_ge(ev("attn_rows"), 1)
            do(v.tensor_copy(A_sb, bank[0:F, 3, 0:3]))
            do(v.tensor_copy(Tall[:, :, F:F + 1], A_sb[:, 0:1].unsqueeze(1).to_broadcast([F, R, 1])))
            v.tensor_copy(A2_rep, A_sb[:, 1:2].to_broadcast([F, P])).then_inc(ev("attn_rep"), 1)
            dve.wait_ge(ev("attn_row"), 1)
            v.tensor_copy(a2_row[:], bank[0:P, 4, 0:F]).then_inc(ev("a2_ready"), 1)
            dve.wait_ge(ev("rel_sum"), 1)
            v.tensor_copy(rel_sb, bank[0:R, 5, 0:FF]).then_inc(ev("rel_ready"), 1)
            W3f = W3.rearrange("k i c o -> k (i c o)")
            do(v.tensor_copy(W3_parts[0], W3f))
            do(v.tensor_tensor(W3_rest, W3f, W3_parts[0], ALU.subtract))
            do(v.tensor_copy(W3_parts[1], W3_rest))
            do(v.tensor_tensor(W3_rest, W3_rest, W3_parts[1], ALU.subtract))
            v.tensor_copy(W3_parts[2], W3_rest).then_inc(ev("w3_ready"), 1)
            dve.wait_ge(ev("deg_root"), 1)
            do(v.reciprocal(dinv[:], nt[1][:]))
            do(v.tensor_tensor(tab[:], xn[:], bct(dinv[:]), ALU.mult))
            v.memset(nt[2][:], 0.0).then_inc(ev("tab"), 1)
            split(tab[:])
            do(v.memset(nsum[:], 0.0))
            dve.wait_ge(ev("att_product"), 1)
            do(v.tensor_reduce(att[:], ef_sb, X, ALU.add))
            v.memset(nt[2][:], 0.0).then_inc(ev("parts_ready"), 1)
            dve.wait_ge(ev("setup_free"), 32)
            dve.wait_ge(ev("round_trips"), 16 * N_TRIPS)
            dve.wait_ge(ev("w6_ready"), 16 * 9)
            dve.wait_ge(ev("step_dst_ready"), BLOCKS)
            node_pass("l0a")
            do(v.tensor_tensor(yn[:], agg, tab[:], ALU.add))
            v.tensor_tensor(yn[:], yn[:], bct(dinv[:]), ALU.mult).then_inc(ev("ax_ready"), 1)
            dve.wait_ge(ev("axT"), 1)
            take_xT(ev("xT_ready"))
            do(v.memset(nsum[:], 0.0))
            dve.wait_ge(ev("z_sum"), 1)
            v.tensor_tensor(tab[:], bank[0:P, 7, 0:T * F].rearrange("p (t w) -> p t w", w=F), bct(dinv[:]), ALU.mult).then_inc(ev("tab"), 1)
            dve.wait_ge(ev("tab"), 2)
            split(tab[:])
            v.memset(nt[2][:], 0.0).then_inc(ev("parts_ready"), 1)
            node_pass("l0b")
            do(v.tensor_tensor(yn[:], agg, tab[:], ALU.add))
            do(v.tensor_tensor(yn[:], yn[:], bct(dinv[:]), ALU.mult))
            do(v.tensor_tensor(yn[:], yn[:], bcf(b2_sb[:]), ALU.add))
            do(v.tensor_tensor(xn[:], xn[:], yn[:], ALU.add))
            layernorm(0).then_inc(ev("x1_ready"), 1)
            do(v.memset(nsum[:], 0.0))
            dve.wait_ge(ev("x1T"), 1)
            take_xT(ev("x1T_ready"))
            dve.wait_ge(ev("c_sum"), 1)
            do(v.tensor_copy(cn[:], bank[0:P, 7, 0:T]))
            y_copied.give(dve)
            for par in range(2):
                dve.sem_inc(y_wrote[par], 16)

            def take_tile(t, par, it):
                y_mm.wait(dve, t + 1)
                dve.wait_ge(y_wrote[par], it * 16 + 16)
                y_copied.on(v.tensor_copy(Yt[par].rearrange("p (b w) -> p b w", b=3), bank[0:P, 3 * par:3 * par + 3, 0:R * YW // 3]))

            with dve.Fori(0, T // 2) as it:
                for par in range(2):
                    take_tile(it * 2 + par, par, it)
            take_tile(T - 1, 0, T // 2)
            dve.sem_inc(ev("f_chain"), 1)
            with dve.Fori(0, PIECES) as it:
                link = LoopChain(dve, ev("f_chain"), it, 5)
                link.value = link.value + 1
                dve.wait_ge(ev("f_in"), it * 16 + 16)
                dve.wait_ge(ev("f_out"), it * (16 * 6) + 48)
                link(v.tensor_copy(f_parts[0], f_x))
                link(v.tensor_tensor(f_rest, f_x, f_parts[0], ALU.subtract))
                link(v.tensor_copy(f_parts[1], f_rest))
                link(v.tensor_tensor(f_rest, f_rest, f_parts[1], ALU.subtract))
                link(v.tensor_copy(f_parts[2], f_rest))
            dve.wait_ge(y_wrote[0], 16 + 16 * (T - T // 2))
            dve.wait_ge(y_wrote[1], 16 + 16 * (T // 2))
            node_pass("l1", attend, 2)
            do(v.tensor_tensor(yn[:], agg, cn[:].unsqueeze(2).to_broadcast([P, T, F]), ALU.mult))
            do(v.tensor_tensor(yn[:], nsum[:, 0:T, F:2 * F], yn[:], ALU.add))
            do(v.tensor_tensor(xn[:], xn[:], yn[:], ALU.add))
            layernorm(1).then_inc(ev("tab"), 1)
            dve.wait_ge(ev("tab"), 3)
            dve.wait_ge(ev("f_out"), 16 * (3 + 6 * PIECES))
            split(xn[:])
            do(v.memset(nsum[:], 0.0))
            v.memset(nt[2][:], 0.0).then_inc(ev("parts_ready"), 1)
            node_pass("l2", weigh, 1)
            do(v.tensor_tensor(yn[:], agg, bcf(l2w_sb[:]), ALU.mult))
            do(v.tensor_tensor(yn[:], yn[:], xn[:], ALU.add))
            do(v.tensor_scalar(tab[:], xn[:], slw_sb[:], None, ALU.mult))
            do(v.tensor_tensor(yn[:], yn[:], tab[:], ALU.add))
            do(v.tensor_scalar(yn[:], yn[:], 0.0, 1.0, ALU.max, ALU.min))
            do(v.tensor_tensor(xn[:], xn[:], yn[:], ALU.add))
            layernorm(2).then_inc(ev("tab"), 1)
            do(v.memset(Macc, 0.0))

            def onehot(o, s, which):
                return v.tensor_tensor(o, iota[0:P, 0:P].unsqueeze(1).to_broadcast([P, G, P]),
                                       step_dst[:, ds(s * G, G), which:which + 1].to_broadcast([P, G, P]), ALU.is_equal)

            A_e2.give(dve)
            A_scan.give(dve)
            A_add.give(dve)

            def a_product(s, sl, g):
                dve.wait_ge(l3_rows, s + 1)
                A_w.wait(dve, s + 1)
                xs = rows_of[:, ds(g * G, G), :].unsqueeze(3)
                v.tensor_tensor(e2[:, 0:2, :].rearrange("p g (i o) -> p g i o", i=F), bank[0:P, 0, :].rearrange("p (g i o) -> p g i o", g=2, i=F), xs[:, 0:2].to_broadcast([P, 2, F, F]), ALU.mult)
                A_e2.on(v.tensor_tensor(e2[:, 2, :].rearrange("p (i o) -> p i o", i=F), bank[0:P, 1, 0:FF].rearrange("p (i o) -> p i o", i=F), xs[:, 2].to_broadcast([P, F, F]), ALU.mult))
                onehot(SE[sl], s, 1).then_inc(ev("A_se"), 1)

            def a_scan(s, sl, row_count, g):
                dve.wait_ge(ev(f"A_pen{sl}"), row_count)
                dve.wait_ge(ev("A_tr"), s + 1)
                for half in range(2):
                    ins = v.tensor_tensor_scan(run_max[:, half, :], rows[sl], bank[:, 2 + half, 0:GE], carry[:, half, ds(g, 1)], ALU.add, ALU.max)
                A_scan.on(ins)
                A_scan.wait(dve, s + 1)
                v.tensor_copy(carry[:, :, ds(g + 1, 1)], run_max[:, :, GE - 1:GE]).then_inc(ev("A_carry"), 1)
                dve.wait_ge(ev("A_carry"), s + 1)

            def a_add(s, sl, t):
                A_add.wait(dve, s)
                A_sc.wait(dve, s + 1)
                A_add.on(v.tensor_tensor(Macc[:, ds(t, 1), :], bank[0:P, 6 + sl, 0:FF].unsqueeze(1), Macc[:, ds(t, 1), :], ALU.add))

            groups = groups_of(DVE, 0, 2)
            a_product(0, 0, groups[0])
            a_scan(0, 0, 16, groups[0])
            a_product(1, 1, groups[1])
            with dve.Fori(0, STEPS // 2 - 1) as it:
                groups, tiles = groups_of(DVE, it * 2 + 1, 3), tiles_of(DVE, it * 2, 2)
                for j, sl in enumerate((1, 0)):
                    s = it * 2 + (j + 1)
                    a_scan(s, sl, it * 16 + (16 if sl else 32), groups[j])
                    a_product(s + 1, 1 - sl, groups[j + 1])
                    a_add(s - 1, 1 - sl, tiles[j])
            a_scan(STEPS - 1, 1, 16 * (STEPS // 2), groups_of(DVE, STEPS - 1, 1)[0])
            for s, t in zip((STEPS - 2, STEPS - 1), tiles_of(DVE, STEPS - 2, 2)):
                a_add(s, s % 2, t)
            A_add.wait(dve, STEPS)
            do(v.tensor_copy(M16[0], Macc))
            do(v.tensor_tensor(M16[1], Macc, M16[0], ALU.subtract))
            v.memset(big[0:P, :], 0.0).then_inc(ev("M_ready"), 1)
            dve.wait_ge(ev("M_ready"), 1)

            B_st.give(dve)
            for sg in (B_em, B_d, B_add):
                sg.give(dve)

            def b_front(s, sl, row_count, g):
                dve.wait_ge(ev(f"B_row{sl}"), row_count)
                B_mg.wait(dve, s)
                B_st.on(v.tensor_scalar(ST, rows[sl][0:P, :].bitcast(I32), step_node[:, ds(s, 1)], None, ALU.is_equal))
                onehot(SB[sl], s, 0)
                B_w.wait(dve, s + 1)
                B_p.wait(dve, s - 1)
                xs = rows_of[:, ds(g * G, G), :].unsqueeze(3)
                B_em.on(v.tensor_tensor(em[sl], bank[0:P, 0:3, :].rearrange("p g (i w) -> p g i w", i=F), xs.to_broadcast([P, G, F, 2 * F]), ALU.mult))
                B_em.wait(dve, s + 1)
                B_mg.wait(dve, s + 1)
                v.tensor_tensor(EP[sl][:, 0:2, :, 0:F], em[sl][:, 0:2, :, 0:F], bank[0:P, 3, :].rearrange("p (g i o) -> p g i o", g=2, i=F), ALU.subtract)
                B_d.on(v.tensor_tensor(EP[sl][:, 2, :, 0:F], em[sl][:, 2, :, 0:F], bank[0:P, 4, 0:FF].rearrange("p (i o) -> p i o", i=F), ALU.subtract))

            def b_add(s, sl, t):
                B_add.wait(dve, s)
                dve.wait_ge(ev("B_sc"), s + 1)
                B_add.on(v.tensor_tensor(sums[:, ds(t, 1), :, :], bank[0:P, 5 + sl, :].rearrange("p (u i w) -> p u i w", u=1, i=F), sums[:, ds(t, 1), :, :], ALU.add))

            for s, g in enumerate(groups_of(DVE, 0, 2)):
                b_front(s, s, 16, g)
            with dve.Fori(0, STEPS // 2 - 1) as it:
                groups, tiles = groups_of(DVE, it * 2 + 2, 2), tiles_of(DVE, it * 2, 2)
                for sl in range(2):
                    s = it * 2 + sl
                    b_add(s, sl, tiles[sl])
                    b_front(s + 2, sl, it * 16 + 32, groups[sl])
            for s, t in zip((STEPS - 2, STEPS - 1), tiles_of(DVE, STEPS - 2, 2)):
                b_add(s, s % 2, t)
            B_add.wait(dve, STEPS)
            den, num = sums[:, 0:T, :, 0:F], sums[:, 0:T, :, F:2 * F]
            do(v.tensor_scalar(den, den, TINY, None, ALU.max))
            do(v.reciprocal(den, den))
            do(v.tensor_tensor(num, num, den, ALU.mult))
            do(v.tensor_reduce(yn[:], num.rearrange("p t i o -> p t o i"), X, ALU.add))
            do(v.tensor_tensor(xn[:], xn[:], yn[:], ALU.add))
            layernorm(3).then_inc(ev("tab"), 1)

        @block.tensor
        def _(pe):
            mm = nc.tensor.matmul
            idn = ident[0:P, 0:P]
            pe.wait_ge(ev("consts"), 1)
            pe.wait_ge(ev("inc_row"), 1)
            for i in range(3):
                ins = mm(bank[0:SROWS, i, 0:GROUPS], ones[:, 0:SROWS], grow[0:1, i, :], start=True, stop=True)
            ins.then_inc(ev("inc_bc"), 1)
            pe.wait_ge(ev("step_row"), 1)
            mm(bank[0:P, 3, 0:STEPS], ones, step_row[0:1, STEPS:2 * STEPS], start=True, stop=True).then_inc(ev("step_bc"), 1)

            def summed(p, b):
                width = 2 * F if p == "l1" else F
                source = both if p == "l1" else both[:, :, 0:1, :]
                pe.wait_ge(s_S, b + (PASSES.index(p) * BLOCKS + 1))
                for j, g in enumerate(groups_of(PE, b * PARTS, PARTS)):
                    for k in range(G):
                        ins = mm(bank[0:P, 6, j * width:(j + 1) * width], S[:, j * G + k, :],
                                 source[:, ds(g * G + k, 1), :, :].rearrange("p u h f -> p (u h) f"), start=(k == 0), stop=(k == G - 1))
                ins.then_inc(s_sum, 1)

            def count(it, par, first=False, last=False):
                deg_made.wait(pe, it + 1)
                for k in range(SLOTS):
                    ins = mm(bank[0:P, 6, 0:T], lo_oh[par][:, k, :], hi_oh[par][:, k, :], start=(first and k == 0), stop=(last and k == SLOTS - 1))
                deg_used.on(ins)

            count(0, 0, first=True)
            with pe.Fori(0, TURNS // 2 - 1) as it:
                count(it * 2 + 1, 1)
                count(it * 2 + 2, 0)
            count(TURNS - 2, 1)
            count(TURNS - 1, 0, last=True)
            pe.wait_ge(ev("inputs"), 16 * N_LOADS)
            mm(bank[0:F, 3, 0:3], Ws_sb, WaT_sb, start=True, stop=True).then_inc(ev("attn_rows"), 1)
            pe.wait_ge(ev("attn_rep"), 1)
            mm(bank[0:P, 4, 0:F], A2_rep, ident[0:F, 0:F], start=True, stop=True).then_inc(ev("attn_row"), 1)
            mm(bank[0:R, 5, 0:FF], wcT_sb, VT_sb, start=True, stop=True).then_inc(ev("rel_sum"), 1)

            def node_pass(p):
                te = p in g_oh

                def turn(it):
                    for i in range(TE_PARTS):
                        if i == 0:
                            g_oh[p].wait(pe, it + 1)
                        g_pick[p][i].wait(pe, it)
                        for k in range(G):
                            for q in range(3):
                                ins = mm(bank[0:P, i * G + k, 0:T * F], oh[:, (i * G + k) * P:(i * G + k + 1) * P], parts[:, q, :], start=(q == 0), stop=(q == 2))
                        ins.then_inc(s_te[i], 1)

                if te:
                    turn(0)
                    turn(1)
                with pe.Fori(1, TURNS - 1) as it:
                    summed(p, it - 1)
                    if te:
                        turn(it + 1)
                with pe.Fori(TURNS - 2, BLOCKS) as b:
                    summed(p, b)

            def transpose_nodes(src, done):
                for t in range(T):
                    ins = nc.tensor.transpose(bank[0:F, 1 + t // TB, (t % TB) * P:(t % TB + 1) * P], src[:, t, :], idn)
                ins.then_inc(done, 1)

            pe.wait_ge(ev("parts_ready"), 1)
            node_pass("l0a")
            pe.wait_ge(ev("ax_ready"), 1)
            transpose_nodes(yn, ev("axT"))
            pe.wait_ge(ev("xT_ready"), 1)
            for b in range(NB + 1):
                w = min(TBW, N - b * TBW)
                ins = mm(bank[0:H1, b, 0:w], W1_sb, xT[:, b * TBW:b * TBW + w], start=True, stop=True)
            ins.then_inc(ev("h_sum"), 1)
            pe.wait_ge(ev("hT_ready"), 1)
            for t in range(T):
                ins = mm(bank[0:P, 7, t * F:(t + 1) * F], hT[:, t * P:(t + 1) * P], W2_sb, start=True, stop=True)
            ins.then_inc(ev("z_sum"), 1)
            pe.wait_ge(ev("parts_ready"), 2)
            node_pass("l0b")
            pe.wait_ge(ev("x1_ready"), 1)
            transpose_nodes(xn, ev("x1T"))
            pe.wait_ge(ev("x1T_ready"), 1)
            for t in range(T):
                ins = mm(bank[0:P, 7, t:t + 1], xT[:, t * P:(t + 1) * P], A_sb[:, 2:3], start=True, stop=True)
            ins.then_inc(ev("c_sum"), 1)
            pe.wait_ge(ev("setup_free"), 32)
            y_mm.give(pe)

            def relation_tile(t, par):
                y_src.wait(pe, t + 1)
                y_copied.wait(pe, t - 1)
                w = R * YW // 3
                for b in range(3):
                    ins = mm(bank[0:P, 3 * par + b, 0:w], xTs[par], Tall.rearrange("i r w -> i (r w)")[:, b * w:(b + 1) * w], start=True, stop=True)
                y_mm.on(ins)

            with pe.Fori(0, T // 2) as it:
                for par in range(2):
                    relation_tile(it * 2 + par, par)
            relation_tile(T - 1, 0)
            node_pass("l1")
            pe.wait_ge(ev("parts_ready"), 3)
            node_pass("l2")

            A_w.give(pe)
            A_sc.give(pe)
            Wa = W6[:].rearrange("k (i c o) -> k i c o", i=F, c=2)[:, :, 0, :]

            def a_weights(s, sl, ef_count):
                pe.wait_ge(ev(f"A_ef{sl}"), ef_count)
                A_e2.wait(pe, s)
                for k in range(G):
                    ins = mm(bank[0:P, k // 2, (k % 2) * FF:(k % 2 + 1) * FF], efs[sl][:, k * P:(k + 1) * P], Wa, start=True, stop=True)
                A_w.on(ins)

            def a_transpose(s):
                A_e2.wait(pe, s + 1)
                A_scan.wait(pe, s)
                for half in range(2):
                    for k in range(G):
                        ins = nc.tensor.transpose(bank[:, 2 + half, k * P:(k + 1) * P], e2[:, k, half * 128:(half + 1) * 128], idn)
                ins.then_inc(ev("A_tr"), 1)

            def a_back(s):
                A_scan.wait(pe, s + 1)
                A_copy.wait(pe, s)
                for half in range(2):
                    for k in range(G):
                        c0 = (k % 2) * FF + half * 128
                        ins = nc.tensor.transpose(bank[0:P, 4 + k // 2, c0:c0 + 128], run_max[:, half, k * P:(k + 1) * P], ident[:])
                ins.then_inc(ev("A_trb"), 1)

            def a_sum(s, sl):
                A_copy.wait(pe, s + 1)
                pe.wait_ge(ev("A_se"), s + 1)
                A_add.wait(pe, s - 1 if not isinstance(s, int) else max(s - 1, 0))
                for k in range(G):
                    ins = mm(bank[0:P, 6 + sl, 0:FF], SE[sl][:, k, :], run_maxT[:, k, :], start=(k == 0), stop=(k == G - 1))
                A_sc.on(ins)

            a_weights(0, 0, 16)
            a_transpose(0)
            a_weights(1, 1, 16)
            a_back(0)
            a_sum(0, 0)
            with pe.Fori(0, STEPS // 2 - 1) as it:
                for sl in (1, 0):
                    s = it * 2 + (1 if sl else 2)
                    a_transpose(s)
                    a_weights(s + 1, 1 - sl, it * 16 + 32)
                    a_back(s)
                    a_sum(s, sl)
            a_transpose(STEPS - 1)
            a_back(STEPS - 1)
            a_sum(STEPS - 1, 1)
            A_add.wait(pe, STEPS)
            pe.wait_ge(ev("M_ready"), 1)

            B_w.give(pe)
            B_mg.give(pe)

            def b_front(s, sl, ef_count, t):
                pe.wait_ge(ev(f"B_ef{sl}"), ef_count)
                B_em.wait(pe, s)
                for k in range(G):
                    ins = mm(bank[0:P, k, :], efs[sl][:, k * P:(k + 1) * P], W6[:], start=True, stop=True)
                B_w.on(ins)
                B_st.wait(pe, s + 1)
                B_d.wait(pe, s)
                for k in range(G):
                    for q in range(2):
                        ins = mm(bank[0:P, 3 + k // 2, (k % 2) * FF:(k % 2 + 1) * FF], ST[:, k * P:(k + 1) * P], M16[q][:, ds(t, 1), :].rearrange("p u w -> p (u w)"), start=(q == 0), stop=(q == 1))
                B_mg.on(ins)

            def b_sum(s, sl):
                B_p.wait(pe, s + 1)
                B_add.wait(pe, s - 1 if not isinstance(s, int) else max(s - 1, 0))
                for k in range(G):
                    ins = mm(bank[0:P, 5 + sl, :], SB[sl][:, k, :], EP[sl][:, k, :, :].rearrange("p i w -> p (i w)"), start=(k == 0), stop=(k == G - 1))
                ins.then_inc(ev("B_sc"), 1)

            tiles = tiles_of(PE, 0, 3)
            b_front(0, 0, 16, tiles[0])
            b_front(1, 1, 16, tiles[1])
            b_sum(0, 0)
            b_front(2, 0, 32, tiles[2])
            b_sum(1, 1)
            with pe.Fori(0, STEPS // 2 - 2) as it:
                tiles = tiles_of(PE, it * 2 + 3, 2)
                b_front(it * 2 + 3, 1, it * 16 + 32, tiles[0])
                b_sum(it * 2 + 2, 0)
                b_front(it * 2 + 4, 0, it * 16 + 48, tiles[1])
                b_sum(it * 2 + 3, 1)
            b_front(STEPS - 1, 1, 16 * (STEPS // 2), tiles_of(PE, STEPS - 1, 1)[0])
            b_sum(STEPS - 2, 0)
            b_sum(STEPS - 1, 1)


def kernel(**inputs):
    import numpy as np
    import concourse.bacc as bacc
    from concourse.bass_utils import run_bass_kernel_spmd as run

    a = {k: np.asarray(v) for k, v in inputs.items()}

    def by_column(e):
        return np.ascontiguousarray(np.moveaxis(e.reshape(C, P, *e.shape[1:]), 0, 1))

    dst, ef = a["dst"], a["edge_attr_16"]
    none = np.full(1, -1, dst.dtype)
    laid = {
        "x": a["x"], "src_pc": by_column(a["src"]), "dst_pc": by_column(dst),
        "dst_next_pc": by_column(np.concatenate([dst[1:], none])), "src_flat": a["src"].reshape(1, E), "dst_flat": dst.reshape(1, E),
        "dst_prev_flat": np.concatenate([none, dst[:-1]]).reshape(1, E),
        "group_ends": np.stack([dst[0::GE], dst[GE - 1::GE]]), "ef_pc": by_column(ef),
        "efT": ef.T, "type_pc": by_column(a["edge_type_90"]),
        "weight_pc": by_column(a["edge_weight"]),
        "W1": a["L0_gnn_W1"], "b1": a["L0_gnn_b1"].reshape(H1, 1), "W2": a["L0_gnn_W2"], "b2": a["L0_gnn_b2"].reshape(1, F),
        "Ws": a["L1_gnn_Ws"], "WaT": a["L1_gnn_Wa"].reshape(3, F).T,
        "VT": a["L1_gnn_weight"].reshape(F, B, F).transpose(1, 0, 2).reshape(B, FF), "wcompT": a["L1_gnn_w_comp"].T,
        "l2w": a["L2_gnn_weight"].reshape(1, F), "slw": a["L2_gnn_self_loop_weight"].reshape(1, 1),
        "Wmsg": a["L3_gnn_W_msg"], "bmsg": a["L3_gnn_b_msg"].reshape(1, FF),
        "Wattn": a["L3_gnn_W_attn"], "battn": a["L3_gnn_b_attn"].reshape(1, FF),
    }
    nc = bacc.Bacc("TRN2", target_bir_lowering=False, num_devices=1)
    arrays, args = {}, []
    for name, v in laid.items():
        v = np.ascontiguousarray(v)
        arrays[f"in_{name}"] = v
        args.append(nc.dram_tensor(f"in_{name}", v.shape, mybir.dt.from_np(v.dtype), kind="ExternalInput").ap())
    out = nc.dram_tensor("out_0", (N, F), FP32, kind="ExternalOutput").ap()
    build(nc, *args, out)
    return run(nc, [arrays], core_ids=[0]).results[0]["out_0"]
```

```python
import concourse.bass as bass
from concourse import mybir
from contextlib import ExitStack

FP32 = mybir.dt.float32
BF16 = mybir.dt.bfloat16
I32 = mybir.dt.int32
U32 = mybir.dt.uint32
ALU = mybir.AluOpType
ACT = mybir.ActivationFunctionType
X = mybir.AxisListType.X
ds = bass.ds
DVE, PE, ACTE, SP = mybir.EngineType.DVE, mybir.EngineType.PE, mybir.EngineType.Activation, mybir.EngineType.SP

N, E, F, H1, R, B = 3125, 103125, 16, 32, 90, 30
P = 125
T = N // P
C = E // P
G = 3
GROUPS = C // G
GE = G * P
PARTS = 5
SLOTS = PARTS * G
TURNS = C // SLOTS
TE_PARTS = 2
STEPS = GROUPS + T
BLOCKS = STEPS // PARTS
SROWS = 100
SCOLS = STEPS // SROWS
FF = F * F
YW = F + 1
TB = 4
TBW = TB * P
NB = T // TB
EXTRA = STEPS - GROUPS
SPLIT_A, SPLIT_B = 5, E // 5
PIECE = 1875
PIECES = SPLIT_B // PIECE
KW = 6 * F + 3
Y_SLOTS = 3
B_SLOTS = 3
KX = 6 * F
NEG = -3.0e38
EPS = 1e-5
TINY = 1e-30
ROUND = 12582912.0


assert TURNS % 2 == 1 and (BLOCKS - TURNS + 1) % 2 == 0 and T % (2 * Y_SLOTS) == 1
assert STEPS % 2 == 0 and STEPS % B_SLOTS == 0 and (TURNS - 1) * PARTS % 2 == 0


class Chain:

    def __init__(self, engine, sem):
        self.engine, self.sem, self.n = engine, sem, 0

    def __call__(self, ins):
        self.n += 1
        ins.then_inc(self.sem, 1)
        self.engine.wait_ge(self.sem, self.n)


class Trips(Chain):

    def __call__(self, ins):
        self.n += 16
        ins.then_inc(self.sem, 16)
        self.engine.wait_ge(self.sem, self.n)


class Signal:

    def __init__(self, sem, credit=0, base=0):
        self.sem, self.credit, self.base = sem, credit, base

    def give(self, engine):
        engine.sem_inc(self.sem, self.credit)

    def wait(self, engine, n):
        engine.wait_ge(self.sem, n + (self.credit + self.base))

    def on(self, ins):
        ins.then_inc(self.sem, 1)


class LoopChain:

    def __init__(self, engine, sem, turn, per_turn, base=0):
        self.engine, self.sem, self.value = engine, sem, turn * per_turn + base

    def __call__(self, ins):
        ins.then_inc(self.sem, 1)
        self.value = self.value + 1
        self.engine.wait_ge(self.sem, self.value)


    def mark(self, ins):
        ins.then_inc(self.sem, 1)
        self.value = self.value + 1
        return self.value

    def after(self, value):
        self.engine.wait_ge(self.sem, value)


class Carve:

    def __init__(self, arena):
        self.arena, self.at = arena, 0

    def __call__(self, rows, *shape, dt=FP32):
        n = 1
        for k in shape:
            n *= k
        words = n if dt != BF16 else (n + 1) // 2
        ap = self.arena[0:rows, self.at:self.at + words]
        self.at += words
        assert self.at <= self.arena.shape[1], (self.at, self.arena.shape)
        if dt != FP32:
            ap = ap.bitcast(dt)[:, 0:n]
        names = "abcd"[:len(shape)]
        if len(shape) > 1:
            ap = ap.rearrange(f"p ({' '.join(names)}) -> p {' '.join(names)}", **dict(zip(names[1:], shape[1:])))
        return ap


def build(nc, x, src_pc, dst_pc, dst_next_pc, src_flat, dst_flat, dst_prev_flat, group_ends, ef_pc, efT, type_pc,
          weight_pc, W1, b1, W2, b2, Ws, WaT, VT, wcompT, l2w, slw, Wmsg, bmsg, Wattn, battn, out):
    ctx = ExitStack()
    with ctx:
        def sb(name, shape, dt=FP32):
            return ctx.enter_context(nc.sbuf_tensor(name, shape, dt))

        def sem(name):
            return ctx.enter_context(nc.semaphore(name))

        def dram(name, shape, dt=FP32):
            return nc.dram_tensor(name, shape, dt, kind="Internal").ap()

        table = [dram(f"table{i}", (N, F)) for i in range(4)]
        rel_table = dram("rel_table", (N * R, YW))
        rel_flat = dram("rel_flat", (F, R, F))
        pen_dram = dram("pen_dram", (1, E))
        slo_dram = dram("slo_dram", (1, E), BF16)
        sched_dram = dram("sched_dram", (2, SCOLS, SROWS), I32)
        ef_parts = dram("ef_parts", (KW, E), BF16)

        ident = sb("ident", [128, 128])
        iota = sb("iota", [128, 128])
        pcol = sb("pcol", [128, 1])
        step_base = sb("step_base", [P, STEPS])
        step_node = sb("step_node", [P, STEPS])
        step_dst = sb("step_dst", [P, STEPS * G, 2])
        src_i = sb("src_i", [P, C + SLOTS], I32)
        rel_idx = sb("rel_idx", [P, C + SLOTS], I32)
        per_edge = sb("per_edge", [P, 4 * C])
        shi, edge_w, att, att_src = (per_edge[:, i * C:(i + 1) * C] for i in range(4))
        xn = sb("xn", [P, T, F])
        tab = sb("tab", [P, T, F])
        yn = sb("yn", [P, T, F])
        nsum = sb("nsum", [P, T + 1, 2 * F])
        nt = [sb(f"nt{i}", [P, T]) for i in range(3)]
        dinv = sb("dinv", [P, T])
        cn = sb("cn", [P, T])
        b2_sb, l2w_sb, slw_sb = sb("b2_sb", [P, F]), sb("l2w_sb", [P, F]), sb("slw_sb", [P, 1])
        a2_row = sb("a2_row", [P, F])
        warm, one_col = sb("warm", [P, 1]), sb("one_col", [P, 1])
        carry = sb("carry", [128, 2, GROUPS + 1])
        sched = sb("sched", [1, 2 * STEPS], I32)
        W6 = sb("W6", [KW, 2 * FF], BF16)
        ring = sb("ring", [P, SLOTS, YW])
        stage = sb("stage", [P, SLOTS], I32)

        wide = sb("wide", [128, C * F + (T + 1) * 2 * FF])
        edge_x, big = wide[:, 0:C * F], wide[:, C * F:]
        both = wide[0:P, 0:2 * C * F].rearrange("p (h c f) -> p c h f", h=2, f=F)
        rows_of = edge_x[0:P, :].rearrange("p (c f) -> p c f", f=F)
        cut = Carve(edge_x)
        dst_i, nxt_i, neq_i = (cut(P, C, dt=I32) for _ in range(3))
        src_f, dst_f, prv_f = (cut(P, C, dt=I32) for _ in range(3))
        tmpf, slo = cut(P, C), cut(P, C)
        dsts = cut(P, C, 2)
        step_row = cut(1, 2 * STEPS)
        slo16 = cut(P, C, dt=BF16)
        grow = cut(1, 5, GROUPS)
        gcmp = cut(SROWS, 2, GROUPS)
        gends = cut(1, 2, GROUPS, dt=I32)
        sch = cut(SROWS, 12)
        sch_i = cut(SROWS, 2 * SCOLS, dt=I32)
        iota_i = cut(128, 128, dt=I32)
        ones = cut(1, P)
        Ws_sb, WaT_sb = cut(F, F), cut(F, 3)
        A2_rep = cut(F, P)
        VT_sb, wcT_sb, rel_sb = cut(B, FF), cut(B, R), cut(R, FF)

        ef_sb = big[0:P, 0:C * F].rearrange("p (c f) -> p c f", f=F)
        scaled = big[0:P, 0:C * F].rearrange("p (c f) -> p c f", f=F)
        Macc = big[0:P, 0:(T + 1) * FF].rearrange("p (t w) -> p t w", w=FF)
        sums = big[0:P, :].rearrange("p (t i w) -> p t i w", i=F, w=2 * F)
        cut = Carve(big)
        x6 = cut(P, T, KX)
        cut.at = 0
        xT = cut(F, N)
        at_hT = cut.at
        hT = cut(H1, N)
        xTs = [cut(KX, P, dt=BF16) for _ in range(2)]
        Yt = [cut(P, R * YW) for _ in range(Y_SLOTS)]
        cut.at = at_hT
        xT6 = cut(KX, N, dt=BF16)

        msplit = sb("msplit", [128, (T + 1) * FF])
        M16 = [msplit[0:P, i * (T + 1) * FF // 2:(i + 1) * (T + 1) * FF // 2].bitcast(BF16).rearrange("p (t w) -> p t w", w=FF) for i in range(2)]
        cut = Carve(msplit)
        W3 = cut(F + 1, F, 2, F)
        W3_rest = cut(F + 1, 2 * FF)
        W3_parts = [cut(F + 1, 2 * FF, dt=BF16) for _ in range(3)]
        Tall_rest = cut(F, R * YW + 1)
        Tall_parts = [cut(F, R * YW + 1, dt=BF16) for _ in range(3)]
        parts = cut(P, 3, T * F, dt=BF16)
        cut = Carve(msplit)
        SR = F * SPLIT_A
        f_x, f_rest = cut(SR, PIECE), cut(SR, PIECE)
        f_parts = [cut(SR, PIECE, dt=BF16) for _ in range(3)]

        work = sb("work", [128, 8300])
        cut = Carve(work)
        lo_oh = [cut(P, SLOTS, P, dt=BF16) for _ in range(2)]
        hi_oh = [cut(P, SLOTS, T, dt=BF16) for _ in range(2)]
        d_lo, d_hi = cut(P, C), cut(P, C)
        cut = Carve(work)
        S = [cut(P, SLOTS, P)]
        slo_row = cut(P, TE_PARTS * GE, dt=BF16)
        oh = cut(P, TE_PARTS * GE, dt=BF16)
        mask = cut(P, TE_PARTS * G, T)
        at_picked = cut.at
        picked = [cut(P, G, T, F) for _ in range(TE_PARTS)]
        after_picked, cut.at = cut.at, at_picked
        S.append(cut(P, SLOTS, P))
        assert cut.at <= after_picked
        cut.at = after_picked
        Tall1 = cut(F, R * YW + 1)
        Tall = Tall1[:, 0:R * YW].rearrange("i (r w) -> i r w", r=R)
        Tall6 = cut(KX, R * YW + 1, dt=BF16)
        W1_sb, W2_sb, b1_sb, A_sb = cut(F, H1), cut(H1, F), cut(H1, 1), cut(F, 3)
        ones16 = cut(P, C, dt=BF16)
        cut = Carve(work)
        efs = [cut(KW, GE, dt=BF16) for _ in range(2)]
        rows = [cut(128, GE) for _ in range(2)]
        at_b = cut.at
        e2 = [cut(P, G, FF) for _ in range(2)]
        run_max = [cut(128, 2, GE) for _ in range(2)]
        run_maxT = [cut(P, G, FF) for _ in range(2)]
        distance_a = cut(P, G, P)
        SE = [cut(P, G, P) for _ in range(2)]
        cut = Carve(work)
        cut.at = at_b
        ST = cut(P, GE, dt=BF16)
        SB = [cut(P, G, P) for _ in range(2)]
        em = [cut(P, G, F, 2 * F) for _ in range(2)]
        EP = [cut(P, G, F, 2 * F) for _ in range(2)]
        cut = Carve(per_edge)
        em, EP = em + [cut(P, G, F, 2 * F)], EP + [cut(P, G, F, 2 * F)]
        cut = Carve(nsum[:].rearrange("p t f -> p (t f)"))
        SB, rows_b = SB + [cut(P, G, P)], [t[0:P, :] for t in rows] + [cut(P, GE)]
        efs_b = efs + [Carve(ring[:].rearrange("p k w -> p (k w)"))(KW, GE, dt=BF16)]
        flat = [tab[:].rearrange("p t f -> p (t f)"), yn[:].rearrange("p t f -> p (t f)"), rel_idx[:].bitcast(FP32)]
        distance = [t[:, 0:GE].rearrange("p (g e) -> p g e", g=G) for t in flat]

        bank = ctx.enter_context(nc.psum_tensor("bank", [128, 8, 512], FP32))

        names = {}

        def ev(name):
            if name not in names:
                names[name] = sem(name)
            return names[name]

        PASSES = ["l0a", "l0b", "l1", "l2"]
        for n in ("inputs_dst", "inputs", "dve_chain", "pool_chain", "consts",
                  "pen_ready", "slo_ready", "sched_ready", "rel_ready", "attn_rows", "attn_rep", "w3_ready", "w6_ready",
                  "attn_row", "a2_ready", "att_product", "rel_sum", "inc_row", "step_row", "step_bc", "step_base_ready", "step_dst_ready", "inc_bc", "round_trips", "deg_ready", "deg_root",
                  "ax_ready", "axT", "xT_ready", "h_sum", "hT_ready", "z_sum",
                  "x1_ready", "tall_split", "tall6_ready", "x1T", "x1T_ready", "relidx_ready",
                  "tab", "wrote",
                  "f_in", "f_out", "f_chain",
                  "var", "root",
                  "A_carry", "A_dist", "oh_dist", "A_tr", "A_trb",
                  "half_cleared", "B_ex", "B_dist", "B_sb"):
            ev(n)
        for n in ("A_ef0", "A_ef1", "A_pen0", "A_pen1", "B_ef0", "B_ef1", "B_ef2", "B_row0", "B_row1", "B_row2"):
            ev(n)
        s_slot = [sem(f"gathered_slot{k}") for k in range(SLOTS)]
        s_part = [sem(f"part_emptied{i}") for i in range(PARTS)]
        s_chain = sem("pass_chain")
        deg_made, deg_used = Signal(sem("deg_onehots")), Signal(sem("deg_multiplied"), 2)
        s_S, s_sum = sem("onehots_made"), sem("block_multiplied")
        s_row, s_mask = sem("slo_rows"), sem("tile_masks")
        s_te = [sem(f"te_gathered{i}") for i in range(TE_PARTS)]
        m_oh, m_pick = sem("src_onehots"), [sem(f"picked{i}") for i in range(TE_PARTS)]
        TE_NO = {"l0a": 0, "l0b": 1, "l2": 2}
        g_oh = {p: Signal(m_oh, 1, n * (TURNS + 1)) for p, n in TE_NO.items()}
        g_pick = {p: [Signal(m_pick[i], 1, n * (TURNS + 1)) for i in range(TE_PARTS)] for p, n in TE_NO.items()}
        y_src, y_mm, y_copied = Signal(sem("y_src")), Signal(sem("y_mm"), 2), Signal(sem("y_copied"), 2)
        y_wrote = [sem(f"y_wrote{i}") for i in range(Y_SLOTS)]
        l3_rows = sem("l3_rows")
        A_w, A_scan = Signal(sem("A_w"), 2), Signal(sem("A_scan"), 2)
        A_e2, A_copy, A_se, A_add = (Signal(sem(n), 1) for n in ("A_e2", "A_copy", "A_se", "A_add"))
        A_sc = Signal(sem("A_sc"), 2)
        B_w, B_st, B_p, B_sc, B_add = (Signal(sem(n), B_SLOTS) for n in ("B_w", "B_st", "B_p", "B_sc", "B_add"))
        B_mg, B_em, B_d = (Signal(sem(n), 1) for n in ("B_mg", "B_em", "B_d"))

        for n in ("settled", "parts_ready", "setup_free", "M_ready"):
            ev(n)
        N_FIRST, N_LOADS, N_TRIPS = 8, 18, 4

        block = ctx.enter_context(nc.Block())
        PASS_NO = {"l0a": 0, "l0b": 1, "l1": 2, "l2": 3, "l3": 4}
        TE_SLOTS = TE_PARTS * G

        def fetched_parts(p):
            return range(0 if p in ("l1", "l3") else TE_PARTS, PARTS)

        def settle(engine):
            engine.sem_inc(ev("settled"), 1)

        def scheduled(engine, first, n, greatest):
            return nc.values_load_multi_w_load_instructions(
                sched[0:1, ds(first, n)], engines=(engine,), min_val=0, max_val=greatest,
                skip_runtime_bounds_check_because="the schedule is clamped when it is computed")[1]

        def groups_of(engine, step, n):
            return scheduled(engine, step, n, GROUPS - 1)

        def tiles_of(engine, step, n):
            return scheduled(engine, step + STEPS, n, T)

        def fetches_before(p, part):
            return sum(TURNS for q in PASS_NO if PASS_NO[q] < PASS_NO[p] and part in fetched_parts(q))

        def parts_before(p, part):
            return (TURNS + 1) * sum(1 for q in PASS_NO if PASS_NO[q] < PASS_NO[p] and part in fetched_parts(q))

        @block.sync
        def _(sp):
            first = [(dst_i, dst_pc), (gends[0:1, 0, :], group_ends[0:1, :]), (gends[0:1, 1, :], group_ends[1:2, :]),
                     (nxt_i, dst_next_pc), (src_i[:, 0:C], src_pc)]
            first += [(t, s.rearrange("u (p c) -> (u p) c", p=P)) for t, s in ((src_f, src_flat), (dst_f, dst_flat), (prv_f, dst_prev_flat))]
            loads = [(xn[:], x.rearrange("(t p) f -> p t f", p=P)),
                     (edge_w, weight_pc), (W1_sb, W1), (W2_sb, W2), (b1_sb, b1),
                     (b2_sb[:], b2.to_broadcast([P, F])), (l2w_sb[:], l2w.to_broadcast([P, F])),
                     (slw_sb[:], slw.to_broadcast([P, 1])), (Ws_sb, Ws), (WaT_sb, WaT), (VT_sb, VT),
                     (wcT_sb, wcompT), (rel_idx[:, 0:C], type_pc), (ef_sb, ef_pc)]
            for c, (w, b) in enumerate(((Wattn, battn), (Wmsg, bmsg))):
                loads.append((W3[0:F, :, c, :], w.rearrange("k (i o) -> k i o", i=F)))
                loads.append((W3[F:F + 1, :, c, :], b.rearrange("u (i o) -> u i o", i=F)))
            for d, s in first:
                sp.dma_start(d, s).then_inc(ev("inputs_dst"), 16)
            for d, s in loads:
                sp.dma_start(d, s).then_inc(ev("inputs"), 16)
            assert (len(first), len(loads)) == (N_FIRST, N_LOADS)

            trips = Trips(sp, ev("round_trips"))
            with nc.allow_non_contiguous_dma(reason="edge layout to flat, once"):
                sp.wait_ge(ev("sched_ready"), 1)
                trips(sp.dma_start(sched_dram.rearrange("a c (p u) -> p (a c) u", u=1), sch_i.rearrange("p (a u) -> p a u", u=1)))
                trips(sp.dma_start(sched[:], sched_dram.rearrange("(u a) c p -> u (a c p)", u=1)))
                sp.wait_ge(ev("slo_ready"), 1)
                trips(sp.dma_start(slo_dram.rearrange("u (p c) -> (u p) c", p=P), slo16))
                sp.wait_ge(ev("pen_ready"), 1)
                trips(sp.dma_start(pen_dram.rearrange("u (p c) -> (u p) c", p=P), tmpf))
                sp.wait_ge(ev("w3_ready"), 1)
                for j, i in enumerate((0, 1, 2, 0, 1, 0)):
                    sp.dma_start(W6[j * F:(j + 1) * F, :], W3_parts[i][0:F, :]).then_inc(ev("w6_ready"), 16)
                for i in range(3):
                    sp.dma_start(W6[6 * F + i:6 * F + i + 1, :], W3_parts[i][F:F + 1, :]).then_inc(ev("w6_ready"), 16)
                sp.wait_ge(ev("w6_ready"), 16 * 9)
                for i in range(3):
                    sp.dma_start(ef_parts[6 * F + i:6 * F + i + 1, :].rearrange("u (p c) -> (u p) c", p=P), ones16).then_inc(ev("f_out"), 16)

            def slo_rows(p):
                with sp.Fori(0, TURNS) as it:
                    g_oh[p].wait(sp, it)
                    settle(sp)
                    sp.dma_start(slo_row, slo_dram[:, ds(it * (SLOTS * P), TE_SLOTS * P)].to_broadcast([P, TE_SLOTS * P])).then_inc(s_row, 16)

            for i, p in enumerate(("l0a", "l0b")):
                sp.wait_ge(ev("tab"), i + 1)
                sp.dma_start(table[i].rearrange("(t p) f -> p t f", p=P), tab[:]).then_inc(ev("wrote"), 16)
                slo_rows(p)
                if p == "l0a":
                    sp.wait_ge(ev("tall_split"), 1)
                    for j, k in enumerate((0, 1, 2, 0, 1, 0)):
                        sp.dma_start(Tall6[j * F:(j + 1) * F, :], Tall_parts[k]).then_inc(ev("tall6_ready"), 16)
                    sp.wait_ge(ev("tall6_ready"), 16 * 6)

            def put_tile(t, slot):
                y_copied.wait(sp, t + 1)
                settle(sp)
                dst = rel_table.rearrange("(t p r) w -> t p (r w)", p=P, r=R)[ds(t, 1), :, :].rearrange("u p w -> (u p) w")
                sp.dma_start(dst, Yt[slot]).then_inc(y_wrote[slot], 16)

            with sp.Fori(0, T // Y_SLOTS) as it:
                for slot in range(Y_SLOTS):
                    put_tile(it * Y_SLOTS + slot, slot)
            put_tile(T - 1, 0)
            efT_v = efT.rearrange("i (a b) -> (i a) b", a=SPLIT_A)
            with sp.Fori(0, PIECES) as it:
                sp.wait_ge(ev("f_chain"), it * 5 + 1)
                settle(sp)
                sp.dma_start(f_x, efT_v[:, ds(it * PIECE, PIECE)]).then_inc(ev("f_in"), 16)
                sp.wait_ge(ev("f_chain"), it * 5 + 6)
                settle(sp)
                for j, i in enumerate((0, 0, 0, 1, 1, 2)):
                    sp.dma_start(ef_parts[j * F:(j + 1) * F, :].rearrange("i (a b) -> (i a) b", a=SPLIT_A)[:, ds(it * PIECE, PIECE)], f_parts[i]).then_inc(ev("f_out"), 16)
            sp.wait_ge(ev("tab"), 3)
            sp.dma_start(table[2].rearrange("(t p) f -> p t f", p=P), xn[:]).then_inc(ev("wrote"), 16)
            slo_rows("l2")
            sp.wait_ge(ev("tab"), 4)
            sp.dma_start(table[3].rearrange("(t p) f -> p t f", p=P), xn[:]).then_inc(ev("wrote"), 16)
            sp.wait_ge(ev("f_out"), 16 * (3 + 6 * PIECES))

            def features(ph, used, s, behind, slot, tile, g):
                used.wait(sp, s - behind)
                settle(sp)
                sp.dma_start(tile, ef_parts[:, ds(g * GE, GE)]).then_inc(ev(f"{ph}_ef{slot}"), 16)

            def row(name, used, s, behind, tile, source, g):
                used.wait(sp, s - behind)
                settle(sp)
                sp.dma_start(tile, source[:, ds(g * GE, GE)].to_broadcast([tile.shape[0], GE])).then_inc(ev(name), 16)

            for s, g in enumerate(groups_of(SP, 0, 2)):
                features("A", A_w, s, 1, s, efs[s], g)
            with sp.Fori(0, STEPS // 2 - 1) as it:
                groups = groups_of(SP, it * 2, 4)
                for sl in range(2):
                    row(f"A_pen{sl}", A_scan, it * 2 + sl, 1, rows[sl], pen_dram, groups[sl])
                    features("A", A_w, it * 2 + (sl + 2), 1, sl, efs[sl], groups[sl + 2])
            for sl, g in enumerate(groups_of(SP, STEPS - 2, 2)):
                row(f"A_pen{sl}", A_scan, STEPS - 2 + sl, 1, rows[sl], pen_dram, g)
            A_add.wait(sp, STEPS)
            with sp.Fori(0, STEPS // B_SLOTS) as it:
                for sl, g in enumerate(groups_of(SP, it * B_SLOTS, B_SLOTS)):
                    features("B", B_w, it * B_SLOTS + sl, 2, sl, efs_b[sl], g)
                    row(f"B_row{sl}", B_st, it * B_SLOTS + sl, 2, rows_b[sl].bitcast(I32), dst_flat, g)
            B_add.wait(sp, STEPS)
            sp.wait_ge(ev("tab"), 5)
            sp.dma_start(out.rearrange("(t p) f -> p t f", p=P), xn[:]).then_inc(ev("wrote"), 16)
            sp.wait_ge(ev("wrote"), 80)

        @block.gpsimd
        def _(pool):
            do = Chain(pool, ev("pool_chain"))
            do(nc.gpsimd.iota(iota_i, pattern=[[1, 128]], base=0, channel_multiplier=0))
            nc.gpsimd.iota(sch_i[:, 0:SCOLS], pattern=[[SROWS, SCOLS]], base=0, channel_multiplier=1)
            do(nc.gpsimd.tensor_copy(iota[:], iota_i))
            do(nc.gpsimd.iota(iota_i, pattern=[[-1, 128]], base=0, channel_multiplier=1))
            do(nc.gpsimd.tensor_copy(ident[:], iota_i))
            for t, val in ((ones, 1.0), (ones16, 1.0), (one_col[:], 1.0), (src_i[:, C:], 0), (rel_idx[:, C:], 0)):
                nc.gpsimd.memset(t, val)
            nc.gpsimd.memset(carry[:], 0.0).then_inc(ev("consts"), 1)
            pool.wait_ge(ev("inputs"), 16 * N_LOADS)
            pool.wait_ge(ev("a2_ready"), 1)
            nc.gpsimd.tensor_tensor(ef_sb, ef_sb, a2_row[:].unsqueeze(1).to_broadcast([P, C, F]), ALU.mult).then_inc(ev("att_product"), 1)

            def gather(p, source, width, written, count):
                pool.wait_ge(written, count)
                with pool.Fori(0, TURNS) as it:
                    for part in fetched_parts(p):
                        pool.wait_ge(s_part[part], it + (parts_before(p, part) + 1))
                        settle(pool)
                        for k in range(part * G, (part + 1) * G):
                            pool.indirect_dma_start(
                                out=ring[:, k, 0:width], out_offset=None, in_=source,
                                in_offset=bass.IndirectOffsetOnAxis(ap=stage[:, k:k + 1].bitcast(U32), axis=0),
                            ).then_inc(s_slot[k], 16)

            gather("l0a", table[0], F, ev("wrote"), 16)
            gather("l0b", table[1], F, ev("wrote"), 32)
            for slot in range(1, Y_SLOTS):
                pool.wait_ge(y_wrote[slot], 16 + 16 * (T // Y_SLOTS))
            gather("l1", rel_table, YW, y_wrote[0], 32 + 16 * (T // Y_SLOTS))
            gather("l2", table[2], F, ev("wrote"), 48)
            gather("l3", table[3], F, ev("wrote"), 64)
            nc.gpsimd.memset(big[0:P, (T + 1) * FF:], 0.0).then_inc(ev("half_cleared"), 1)
            B_p.give(pool)
            with pool.Fori(0, STEPS // B_SLOTS) as it:
                for sl in range(B_SLOTS):
                    pool.wait_ge(ev("B_ex"), it * B_SLOTS + sl + 1)
                    B_p.on(nc.gpsimd.tensor_tensor(EP[sl][:, :, :, F:2 * F], em[sl][:, :, :, F:2 * F], EP[sl][:, :, :, 0:F], ALU.mult))

        @block.scalar
        def _(act):
            copy = lambda o, i: nc.scalar.activation(o, i, ACT.Copy)

            def sqrt(ready, n, done):
                act.wait_ge(ev(ready), n)
                nc.scalar.activation(nt[1][:], nt[0][:], ACT.Sqrt).then_inc(ev(done), 1)

            def stage_first(p, idx):
                for part in fetched_parts(p):
                    c = part * G
                    copy(stage[:, c:c + G], idx[:, c:c + G]).then_inc(s_part[part], 1)

            def empty_part(p, it, part, idx):
                for k in range(part * G, (part + 1) * G):
                    act.wait_ge(s_slot[k], it * 16 + 16 * (fetches_before(p, part) + 1))
                c, col = part * G, it * SLOTS + part * G
                if p == "l1":
                    copy(att_src[:, ds(col, G)].unsqueeze(2), ring[:, c:c + G, F:F + 1])
                ins = copy(rows_of[:, ds(col, G), :], ring[:, c:c + G, 0:F])
                if p == "l3":
                    ins.then_inc(l3_rows, 1)
                copy(stage[:, c:c + G], idx[:, ds(col + SLOTS, G)]).then_inc(s_part[part], 1)

            def source_onehot(p, it, first=False):
                act.wait_ge(s_row, it * 16 + 16 * (TE_NO[p] * TURNS + 1))
                if not first:
                    act.wait_ge(s_te[TE_PARTS - 1], it + TE_NO[p] * TURNS)
                nc.scalar.activation(slo_row, slo_row, ACT.Abs, scale=-1.0, bias=pcol[0:P, :]).then_inc(ev("oh_dist"), 1)
                act.wait_ge(ev("oh_dist"), it + (TE_NO[p] * TURNS + 1))
                g_oh[p].on(nc.scalar.activation(oh, slo_row, ACT.Relu, scale=-1.0, bias=one_col[:]))

            def empty(p, idx):
                te = p in g_oh
                stage_first(p, idx)
                if te:
                    g_oh[p].give(act)
                    source_onehot(p, 0, first=True)
                with act.Fori(0, TURNS - 1) as it:
                    if te:
                        source_onehot(p, it + 1)
                    for part in fetched_parts(p):
                        empty_part(p, it, part, idx)
                for part in fetched_parts(p):
                    empty_part(p, TURNS - 1, part, idx)

            act.wait_ge(ev("consts"), 1)
            act.wait_ge(ev("inputs_dst"), 16 * N_FIRST)
            act.wait_ge(ev("step_base_ready"), 1)
            with act.Fori(0, BLOCKS) as b:
                for j, g in enumerate(groups_of(ACTE, b * PARTS, PARTS)):
                    s = b * PARTS + j
                    ins = nc.scalar.activation(step_dst[:, ds(s * G, G), :], dsts[:, ds(g * G, G), :], ACT.Identity, bias=step_base[:, ds(s, 1)])
                ins.then_inc(ev("step_dst_ready"), 1)
            sqrt("deg_ready", 1, "deg_root")
            with nc.allow_non_contiguous_dma(reason="edge layout to flat, once"):
                act.wait_ge(ev("rel_ready"), 1)
                act.dma_start(rel_flat.rearrange("i r o -> r i o"), rel_sb.rearrange("r (i o) -> r i o", i=F)).then_inc(ev("setup_free"), 16)
                act.wait_ge(ev("setup_free"), 16)
                act.dma_start(Tall[:, :, 0:F], rel_flat.rearrange("i r o -> (i r) o").rearrange("(r i) o -> i r o", i=F)).then_inc(ev("setup_free"), 16)
            act.wait_ge(ev("tab"), 1)
            empty("l0a", src_i)
            for b in range(NB + 1):
                w = min(TBW, N - b * TBW)
                act.wait_ge(ev("h_sum"), b + 1)
                nc.scalar.activation(hT[:, b * TBW:b * TBW + w], bank[0:H1, b, 0:w], ACT.Relu, bias=b1_sb).then_inc(ev("hT_ready"), 1)
            empty("l0b", src_i)
            sqrt("var", 1, "root")
            act.wait_ge(ev("x1T_ready"), NB + 1)

            def source_tile(t, par):
                y_mm.wait(act, t - 1)
                y_src.on(copy(xTs[par], xT6[:, ds(t * P, P)]))

            with act.Fori(0, T // 2) as it:
                for par in range(2):
                    source_tile(it * 2 + par, par)
            source_tile(T - 1, 0)
            act.wait_ge(ev("relidx_ready"), 1)
            empty("l1", rel_idx)
            sqrt("var", 2, "root")
            empty("l2", src_i)
            sqrt("var", 3, "root")
            A_copy.give(act)

            def maxima(s, par):
                A_se.wait(act, s)
                for k in range(G):
                    one = ds(s * G + k, 1)
                    ins = nc.scalar.activation(distance_a[:, k, :], iota[0:P, 0:P], ACT.Abs, scale=-1.0, bias=step_dst[:, one, 1:2].rearrange("p a b -> p (a b)"))
                ins.then_inc(ev("A_dist"), 1)
                act.wait_ge(ev("A_dist"), s + 1)
                A_sc.wait(act, s - 1)
                A_se.on(nc.scalar.activation(SE[par], distance_a, ACT.Relu, scale=-1.0, bias=one_col[:]))
                act.wait_ge(ev("A_trb"), s + 1)
                copy(run_maxT[par][:, 0:2, :], bank[0:P, 4, :].rearrange("p (g w) -> p g w", g=2))
                A_copy.on(copy(run_maxT[par][:, 2, :], bank[0:P, 5, 0:FF]))

            A_se.give(act)
            stage_first("l3", src_i)
            for part in range(PARTS):
                empty_part("l3", 0, part, src_i)
            with act.Fori(0, (TURNS - 1) // 2) as it:
                for half in range(2):
                    for part in range(PARTS):
                        step = half * PARTS + part
                        empty_part("l3", it * 2 + (half + 1), part, src_i)
                        maxima(it * (2 * PARTS) + step, step % 2)
            act.sem_inc(l3_rows, EXTRA)
            with act.Fori((TURNS - 1) * PARTS // 2, STEPS // 2) as it:
                for par in range(2):
                    maxima(it * 2 + par, par)
            nc.scalar.activation(warm[:], pcol[0:P, :], ACT.Exp, scale=0.0)
            with act.Fori(0, STEPS // B_SLOTS) as it:
                for sl in range(B_SLOTS):
                    s = it * B_SLOTS + sl
                    B_d.wait(act, s + 1)
                    nc.scalar.activation(EP[sl][:, :, :, 0:F], EP[sl][:, :, :, 0:F], ACT.Exp).then_inc(ev("B_ex"), 1)
                    B_sc.wait(act, s - 2)
                    for k in range(G):
                        one = ds(s * G + k, 1)
                        ins = nc.scalar.activation(distance[sl][:, k, :], iota[0:P, 0:P], ACT.Abs, scale=-1.0, bias=step_dst[:, one, 0:1].rearrange("p a b -> p (a b)"))
                    ins.then_inc(ev("B_dist"), 1)
                    act.wait_ge(ev("B_dist"), s + 1)
                    nc.scalar.activation(SB[sl], distance[sl], ACT.Relu, scale=-1.0, bias=one_col[:]).then_inc(ev("B_sb"), 1)
            sqrt("var", 4, "root")

        @block.vector
        def _(dve):
            do = Chain(dve, ev("dve_chain"))
            v = nc.vector
            dve.wait_ge(ev("consts"), 1)
            dve.wait_ge(ev("inputs_dst"), 16 * N_FIRST)

            def quotient(o, i):
                do(v.tensor_scalar(o, i, 1.0 / P, -(P - 1) / (2.0 * P), ALU.mult, ALU.add))
                do(v.tensor_scalar(o, o, ROUND, None, ALU.add))
                do(v.tensor_scalar(o, o, ROUND, None, ALU.subtract))

            do(v.tensor_copy(sch[:, 0:SCOLS], sch_i[:, 0:SCOLS]))
            do(v.tensor_copy(grow[0:1, 0:2, :], gends[0:1, :, :]))
            quotient(grow[0:1, 2:4, :], grow[0:1, 0:2, :])
            do(v.scalar_tensor_tensor(out=grow[0:1, 4, :], in0=grow[0:1, 3, :], scalar=1.0, in1=grow[0:1, 2, :], op0=ALU.add, op1=ALU.subtract))
            do(v.memset(grow[0:1, 3, :], 0.0))
            do(v.tensor_tensor_scan(grow[0:1, 0, :], grow[0:1, 4, :], grow[0:1, 3, :], 0.0, ALU.add, ALU.add))
            do(v.tensor_tensor(grow[0:1, 1, :], grow[0:1, 0, :], grow[0:1, 4, :], ALU.subtract))
            v.tensor_tensor(grow[0:1, 2, :], grow[0:1, 2, :], grow[0:1, 1, :], ALU.subtract).then_inc(ev("inc_row"), 1)
            do(v.tensor_copy(pcol[:], ident[:, 0:1]))
            do(v.tensor_scalar(ident[:], ident[:], 0.0, None, ALU.is_equal))
            do(v.tensor_copy(dsts[:, :, 0], dst_i))
            do(v.tensor_tensor(neq_i, dst_i, nxt_i, ALU.not_equal))
            do(v.scalar_tensor_tensor(out=dsts[:, :, 1], in0=dsts[:, :, 0], scalar=1.0, in1=neq_i, op0=ALU.add, op1=ALU.mult))
            do(v.tensor_scalar(dsts[:, :, 1], dsts[:, :, 1], 1.0, None, ALU.subtract))
            dve.wait_ge(ev("inc_bc"), 1)
            for j in range(SCOLS):
                step = sch[:, j:j + 1]
                do(v.tensor_scalar(gcmp[:, 0, :], bank[0:SROWS, 0, 0:GROUPS], step, None, ALU.is_le))
                do(v.tensor_reduce(sch[:, 3 + j:4 + j], gcmp[:, 0, :], X, ALU.add))
                do(v.scalar_tensor_tensor(out=gcmp[:, 0, :], in0=bank[0:SROWS, 1, 0:GROUPS], scalar=step, in1=gcmp[:, 0, :], op0=ALU.is_le, op1=ALU.subtract))
                do(v.tensor_tensor(gcmp[:, 1, :], bank[0:SROWS, 2, 0:GROUPS], gcmp[:, 0, :], ALU.mult))
                do(v.tensor_reduce(sch[:, 6 + j:7 + j], gcmp[:, 1, :], X, ALU.add))
            do(v.tensor_tensor(sch[:, 6:9], sch[:, 6:9], sch[:, 0:3], ALU.add))
            do(v.tensor_scalar(sch[:, 3:6], sch[:, 3:6], float(GROUPS - 1), None, ALU.min))
            do(v.tensor_scalar(sch[:, 6:9], sch[:, 6:9], float(T), None, ALU.min))
            v.tensor_copy(sch_i, sch[:, 3:9]).then_inc(ev("sched_ready"), 1)
            quotient(shi, src_i[:, 0:C])
            quotient(tmpf, src_f)
            do(v.scalar_tensor_tensor(out=slo, in0=tmpf, scalar=-float(P), in1=src_f, op0=ALU.mult, op1=ALU.add))
            v.tensor_copy(slo16, slo).then_inc(ev("slo_ready"), 1)
            dve.wait_ge(ev("round_trips"), 32)
            v.tensor_copy(step_row, sched[:]).then_inc(ev("step_row"), 1)
            dve.wait_ge(ev("step_bc"), 1)
            v.tensor_scalar(step_base[:], bank[0:P, 3, 0:STEPS], -float(P), None, ALU.mult).then_inc(ev("step_base_ready"), 1)
            do(v.tensor_scalar(step_node[:], bank[0:P, 3, 0:STEPS], float(P), None, ALU.mult))
            do(v.tensor_scalar(step_node[:], step_node[:], pcol[0:P, :], None, ALU.add))

            def bct(ap):
                return ap.unsqueeze(2).to_broadcast([P, T, F])

            def bcf(ap):
                return ap.unsqueeze(1).to_broadcast([P, T, F])

            def onehots(b, slot=0):
                v.tensor_tensor(S[slot], iota[0:P, 0:P].unsqueeze(1).to_broadcast([P, SLOTS, P]),
                                step_dst[:, ds(b * SLOTS, SLOTS), 0:1].to_broadcast([P, SLOTS, P]), ALU.is_equal).then_inc(s_S, 1)

            WIDTH = {"l0a": F, "l0b": F, "l1": 2 * F, "l2": F}
            chained = [0]

            def node_pass(p, prepare=None, prepare_links=0):
                te = p in g_oh
                width = WIDTH[p]
                turn_links = prepare_links + PARTS + (TE_PARTS if te else 0)

                def chain(turn=0, per_turn=0):
                    return LoopChain(dve, s_chain, turn, per_turn, chained[0])

                def multiplied(b):
                    dve.wait_ge(s_sum, b + (PASSES.index(p) * BLOCKS + 1))

                def add(b, par, j, t, link, last):
                    link.after(last)
                    at = nsum[:, ds(t, 1), 0:width]
                    return link.mark(v.tensor_tensor(at, bank[0:P, 6 + par, j * width:(j + 1) * width].unsqueeze(1), at, ALU.add))

                def block(b, par, link):
                    onehots(b, 1 - par)
                    multiplied(b - 1)
                    last = link.value
                    for j, t in enumerate(tiles_of(DVE, (b - 1) * PARTS, PARTS)):
                        last = add(b - 1, 1 - par, j, t, link, last)

                def turn(it, par, link, onehot=True, sums=True):
                    b = it - 1
                    if te:
                        v.tensor_tensor(mask, iota[0:P, 0:T].unsqueeze(1).to_broadcast([P, TE_SLOTS, T]),
                                        shi[:, ds(it * SLOTS, TE_SLOTS)].unsqueeze(2).to_broadcast([P, TE_SLOTS, T]), ALU.is_equal).then_inc(s_mask, 1)
                    if onehot:
                        for part in fetched_parts(p):
                            dve.wait_ge(s_part[part], b + (parts_before(p, part) + 2))
                        if prepare:
                            prepare(b, link)
                        if sums:
                            multiplied(b - 1)
                        onehots(b)
                    last = link.value
                    tiles = list(enumerate(tiles_of(DVE, (b - 1) * PARTS, PARTS))) if sums else []
                    if te:
                        dve.wait_ge(s_mask, it + (TE_NO[p] * TURNS + 1))
                        for i in range(TE_PARTS):
                            dve.wait_ge(s_te[i], it + (TE_NO[p] * TURNS + 1))
                            sel = mask[:, i * G:(i + 1) * G, :].unsqueeze(3).to_broadcast([P, G, T, F])
                            src = bank[0:P, i * G:(i + 1) * G, 0:T * F].rearrange("p g (t f) -> p g t f", f=F)
                            v.tensor_tensor(picked[i], src, sel, ALU.mult).then_inc(g_pick[p][i].sem, 1)
                            if tiles:
                                last = add(b - 1, 1 - par, *tiles.pop(0), link, last)
                            g_pick[p][i].wait(dve, it + 1)
                            summed = link.mark(v.tensor_reduce(rows_of[:, ds(it * SLOTS + i * G, G), :], picked[i].rearrange("p g t f -> p g f t"), X, ALU.add))
                            if tiles:
                                last = add(b - 1, 1 - par, *tiles.pop(0), link, last)
                        link.after(summed)
                    while tiles:
                        last = add(b - 1, 1 - par, *tiles.pop(0), link, last)

                if te:
                    for i in range(TE_PARTS):
                        g_pick[p][i].give(dve)
                    turn(0, 1, chain(), onehot=False, sums=False)
                    chained[0] += TE_PARTS
                turn(1, 0, chain(), sums=False)
                chained[0] += turn_links - PARTS
                with dve.Fori(0, (TURNS - 3) // 2) as it:
                    link = chain(it, 2 * turn_links)
                    for j in range(2):
                        turn(it * 2 + (j + 2), 1 - j, link)
                chained[0] += (TURNS - 3) * turn_links
                turn(TURNS - 1, 1, chain())
                chained[0] += turn_links
                for part in fetched_parts(p):
                    dve.wait_ge(s_part[part], parts_before(p, part) + TURNS + 1)
                if prepare:
                    prepare(TURNS - 1, chain())
                chained[0] += prepare_links
                with dve.Fori(0, (BLOCKS - TURNS + 1) // 2) as it:
                    link = chain(it, 2 * PARTS)
                    for j in range(2):
                        block(it * 2 + (TURNS - 1 + j), j, link)
                chained[0] += (BLOCKS - TURNS + 1) * PARTS
                multiplied(BLOCKS - 1)
                link = chain()
                last = link.value
                for j, t in enumerate(tiles_of(DVE, STEPS - PARTS, PARTS)):
                    last = add(BLOCKS - 1, 1, j, t, link, last)
                link.after(last)
                chained[0] += PARTS

            def weigh(b, link):
                at = rows_of[:, ds(b * SLOTS, SLOTS), :]
                link.mark(v.tensor_tensor(at, at, edge_w[:, ds(b * SLOTS, SLOTS)].unsqueeze(2).to_broadcast([P, SLOTS, F]), ALU.mult))

            def attend(b, link):
                c = ds(b * SLOTS, SLOTS)
                link(v.tensor_tensor(att_src[:, c], att_src[:, c], att[:, c], ALU.add))
                link.mark(v.tensor_tensor(scaled[:, c, :], rows_of[:, c, :], att_src[:, c].unsqueeze(2).to_broadcast([P, SLOTS, F]), ALU.mult))

            def layernorm(i):
                do(v.tensor_reduce(nt[0][:], xn[:], X, ALU.add))
                do(v.tensor_scalar(nt[0][:], nt[0][:], 1.0 / F, None, ALU.mult))
                do(v.tensor_tensor(xn[:], xn[:], bct(nt[0][:]), ALU.subtract))
                do(v.tensor_tensor(yn[:], xn[:], xn[:], ALU.mult))
                do(v.tensor_reduce(nt[0][:], yn[:], X, ALU.add))
                v.tensor_scalar(nt[0][:], nt[0][:], 1.0 / F, EPS, ALU.mult, ALU.add).then_inc(ev("var"), 1)
                dve.wait_ge(ev("root"), i + 1)
                do(v.reciprocal(nt[2][:], nt[1][:]))
                return v.tensor_tensor(xn[:], xn[:], bct(nt[2][:]), ALU.mult)

            def split(source):
                fl = lambda ap: ap.rearrange("p t f -> p (t f)")
                do(v.tensor_copy(parts[:, 0, :], fl(source)))
                do(v.tensor_tensor(fl(yn[:]), fl(source), parts[:, 0, :], ALU.subtract))
                do(v.tensor_copy(parts[:, 1, :], fl(yn[:])))
                do(v.tensor_tensor(fl(yn[:]), fl(yn[:]), parts[:, 1, :], ALU.subtract))
                do(v.tensor_copy(parts[:, 2, :], fl(yn[:])))

            def take_transposed(o, width, ready, done):
                for b in range(NB + 1):
                    w = min(TBW, N - b * TBW)
                    dve.wait_ge(ready, b + 1)
                    v.tensor_copy(o[:, b * TBW:b * TBW + w], bank[0:width, 1 + b, 0:w]).then_inc(done, 1)

            agg = nsum[:, 0:T, 0:F]

            dve.wait_ge(ev("attn_rows"), 1)
            do(v.tensor_copy(A_sb, bank[0:F, 7, 0:3]))
            do(v.tensor_copy(Tall[:, :, F:F + 1], A_sb[:, 0:1].unsqueeze(1).to_broadcast([F, R, 1])))
            do(v.tensor_copy(Tall1[:, R * YW:], A_sb[:, 2:3]))
            v.tensor_copy(A2_rep, A_sb[:, 1:2].to_broadcast([F, P])).then_inc(ev("attn_rep"), 1)
            dve.wait_ge(ev("attn_row"), 1)
            v.tensor_copy(a2_row[:], bank[0:P, 4, 0:F]).then_inc(ev("a2_ready"), 1)
            dve.wait_ge(ev("rel_sum"), 1)
            v.tensor_copy(rel_sb, bank[0:R, 5, 0:FF]).then_inc(ev("rel_ready"), 1)
            quotient(d_hi, dsts[:, :, 0])
            do(v.scalar_tensor_tensor(out=d_lo, in0=d_hi, scalar=-float(P), in1=dsts[:, :, 0], op0=ALU.mult, op1=ALU.add))
            deg_used.give(dve)

            def degree_onehots(it, par):
                deg_used.wait(dve, it - 1)
                c = ds(it * SLOTS, SLOTS)
                for o, place, w in ((hi_oh, d_hi, T), (lo_oh, d_lo, P)):
                    ins = v.tensor_tensor(o[par], iota[0:P, 0:w].unsqueeze(1).to_broadcast([P, SLOTS, w]),
                                          place[:, c].unsqueeze(2).to_broadcast([P, SLOTS, w]), ALU.is_equal)
                deg_made.on(ins)

            with dve.Fori(0, TURNS // 2) as it:
                for par in range(2):
                    degree_onehots(it * 2 + par, par)
            degree_onehots(TURNS - 1, 0)
            deg_used.wait(dve, TURNS)
            v.tensor_scalar(nt[0][:], bank[0:P, 6, 0:T], 1.0, None, ALU.add).then_inc(ev("deg_ready"), 1)
            dve.wait_ge(ev("inputs"), 16 * N_LOADS)
            do(v.tensor_tensor(tmpf, dst_f, prv_f, ALU.not_equal))
            v.tensor_scalar(tmpf, tmpf, NEG, None, ALU.mult).then_inc(ev("pen_ready"), 1)
            do(v.tensor_copy(slo, rel_idx[:, 0:C]))
            do(v.scalar_tensor_tensor(out=slo, in0=src_i[:, 0:C], scalar=float(R), in1=slo, op0=ALU.mult, op1=ALU.add))
            v.tensor_copy(rel_idx[:, 0:C], slo).then_inc(ev("relidx_ready"), 1)
            W3f = W3.rearrange("k i c o -> k (i c o)")
            do(v.tensor_copy(W3_parts[0], W3f))
            do(v.tensor_tensor(W3_rest, W3f, W3_parts[0], ALU.subtract))
            do(v.tensor_copy(W3_parts[1], W3_rest))
            do(v.tensor_tensor(W3_rest, W3_rest, W3_parts[1], ALU.subtract))
            v.tensor_copy(W3_parts[2], W3_rest).then_inc(ev("w3_ready"), 1)
            dve.wait_ge(ev("deg_root"), 1)
            do(v.reciprocal(dinv[:], nt[1][:]))
            do(v.tensor_tensor(tab[:], xn[:], bct(dinv[:]), ALU.mult))
            v.memset(nt[2][:], 0.0).then_inc(ev("tab"), 1)
            split(tab[:])
            do(v.memset(nsum[:], 0.0))
            dve.wait_ge(ev("att_product"), 1)
            do(v.tensor_reduce(att, ef_sb, X, ALU.add))
            v.memset(nt[2][:], 0.0).then_inc(ev("parts_ready"), 1)
            dve.wait_ge(ev("setup_free"), 32)
            dve.wait_ge(ev("round_trips"), 16 * N_TRIPS)
            dve.wait_ge(ev("w6_ready"), 16 * 9)
            dve.wait_ge(ev("step_dst_ready"), BLOCKS)
            node_pass("l0a")
            do(v.tensor_tensor(yn[:], agg, tab[:], ALU.add))
            v.tensor_tensor(yn[:], yn[:], bct(dinv[:]), ALU.mult).then_inc(ev("ax_ready"), 1)
            take_transposed(xT, F, ev("axT"), ev("xT_ready"))
            do(v.tensor_copy(Tall_parts[0], Tall1))
            do(v.tensor_tensor(Tall_rest, Tall1, Tall_parts[0], ALU.subtract))
            do(v.tensor_copy(Tall_parts[1], Tall_rest))
            do(v.tensor_tensor(Tall_rest, Tall_rest, Tall_parts[1], ALU.subtract))
            v.tensor_copy(Tall_parts[2], Tall_rest).then_inc(ev("tall_split"), 1)
            do(v.memset(nsum[:], 0.0))
            dve.wait_ge(ev("z_sum"), 1)
            v.tensor_tensor(tab[:], bank[0:P, 7, 0:T * F].rearrange("p (t w) -> p t w", w=F), bct(dinv[:]), ALU.mult).then_inc(ev("tab"), 1)
            dve.wait_ge(ev("tab"), 2)
            split(tab[:])
            v.memset(nt[2][:], 0.0).then_inc(ev("parts_ready"), 1)
            node_pass("l0b")
            do(v.tensor_tensor(yn[:], agg, tab[:], ALU.add))
            do(v.tensor_tensor(yn[:], yn[:], bct(dinv[:]), ALU.mult))
            do(v.tensor_tensor(yn[:], yn[:], bcf(b2_sb[:]), ALU.add))
            do(v.tensor_tensor(xn[:], xn[:], yn[:], ALU.add))
            layernorm(0).then_inc(ev("x1_ready"), 1)
            dve.wait_ge(ev("x1_ready"), 1)
            split(xn[:])
            part = lambda q: parts[:, q, :].rearrange("p (t u f) -> p t u f", u=1, f=F)
            rows6 = x6.rearrange("p t (u f) -> p t u f", f=F)
            for q, at, n in ((0, 0, 3), (1, 3, 2), (2, 5, 1)):
                ins = v.tensor_copy(rows6[:, :, at:at + n, :], part(q).to_broadcast([P, T, n, F]))
            ins.then_inc(ev("x1_ready"), 1)
            do(v.memset(nsum[:], 0.0))
            take_transposed(xT6, KX, ev("x1T"), ev("x1T_ready"))
            y_copied.give(dve)
            for slot in range(Y_SLOTS):
                dve.sem_inc(y_wrote[slot], 16)

            def take_tile(t, par, slot, written):
                y_mm.wait(dve, t + 1)
                dve.wait_ge(y_wrote[slot], written)
                w = R * YW // 3
                v.tensor_copy(cn[:, ds(t, 1)], bank[0:P, 3 * par + 2, w:w + 1])
                y_copied.on(v.tensor_copy(Yt[slot].rearrange("p (b w) -> p b w", b=3), bank[0:P, 3 * par:3 * par + 3, 0:w]))

            n = 2 * Y_SLOTS
            with dve.Fori(0, T // n) as it:
                for j in range(n):
                    take_tile(it * n + j, j % 2, j % Y_SLOTS, it * 32 + (16 + 16 * (j // Y_SLOTS)))
            take_tile(T - 1, 0, 0, 16 + 16 * (T // Y_SLOTS))
            dve.sem_inc(ev("f_chain"), 1)
            with dve.Fori(0, PIECES) as it:
                link = LoopChain(dve, ev("f_chain"), it, 5)
                link.value = link.value + 1
                dve.wait_ge(ev("f_in"), it * 16 + 16)
                dve.wait_ge(ev("f_out"), it * (16 * 6) + 48)
                link(v.tensor_copy(f_parts[0], f_x))
                link(v.tensor_tensor(f_rest, f_x, f_parts[0], ALU.subtract))
                link(v.tensor_copy(f_parts[1], f_rest))
                link(v.tensor_tensor(f_rest, f_rest, f_parts[1], ALU.subtract))
                link(v.tensor_copy(f_parts[2], f_rest))
            for slot in range(Y_SLOTS):
                dve.wait_ge(y_wrote[slot], 16 + 16 * (T // Y_SLOTS + (slot == 0)))
            node_pass("l1", attend, 2)
            do(v.tensor_tensor(yn[:], agg, cn[:].unsqueeze(2).to_broadcast([P, T, F]), ALU.mult))
            do(v.tensor_tensor(yn[:], nsum[:, 0:T, F:2 * F], yn[:], ALU.add))
            do(v.tensor_tensor(xn[:], xn[:], yn[:], ALU.add))
            layernorm(1).then_inc(ev("tab"), 1)
            dve.wait_ge(ev("tab"), 3)
            dve.wait_ge(ev("f_out"), 16 * (3 + 6 * PIECES))
            split(xn[:])
            do(v.memset(nsum[:], 0.0))
            v.memset(nt[2][:], 0.0).then_inc(ev("parts_ready"), 1)
            node_pass("l2", weigh, 1)
            do(v.tensor_tensor(yn[:], agg, bcf(l2w_sb[:]), ALU.mult))
            do(v.tensor_tensor(yn[:], yn[:], xn[:], ALU.add))
            do(v.tensor_scalar(tab[:], xn[:], slw_sb[:], None, ALU.mult))
            do(v.tensor_tensor(yn[:], yn[:], tab[:], ALU.add))
            do(v.tensor_scalar(yn[:], yn[:], 0.0, 1.0, ALU.max, ALU.min))
            do(v.tensor_tensor(xn[:], xn[:], yn[:], ALU.add))
            layernorm(2).then_inc(ev("tab"), 1)
            do(v.memset(Macc, 0.0))

            A_e2.give(dve)
            A_scan.give(dve)
            A_add.give(dve)

            def a_product(s, sl, g):
                dve.wait_ge(l3_rows, s + 1)
                A_w.wait(dve, s + 1)
                xs = rows_of[:, ds(g * G, G), :].unsqueeze(3)
                v.tensor_tensor(e2[sl][:, 0:2, :].rearrange("p g (i o) -> p g i o", i=F), bank[0:P, 0, :].rearrange("p (g i o) -> p g i o", g=2, i=F), xs[:, 0:2].to_broadcast([P, 2, F, F]), ALU.mult)
                A_e2.on(v.tensor_tensor(e2[sl][:, 2, :].rearrange("p (i o) -> p i o", i=F), bank[0:P, 1, 0:FF].rearrange("p (i o) -> p i o", i=F), xs[:, 2].to_broadcast([P, F, F]), ALU.mult))

            def a_scan(s, sl, row_count, g):
                if not (isinstance(s, int) and s == 0):
                    dve.wait_ge(ev("A_carry"), s)
                dve.wait_ge(ev(f"A_pen{sl}"), row_count)
                dve.wait_ge(ev("A_tr"), s + 1)
                for half in range(2):
                    ins = v.tensor_tensor_scan(run_max[sl][:, half, :], rows[sl], bank[:, 2 + half, 0:GE], carry[:, half, ds(g, 1)], ALU.add, ALU.max)
                A_scan.on(ins)

            def a_carry(s, sl, g):
                A_scan.wait(dve, s + 1)
                v.tensor_copy(carry[:, :, ds(g + 1, 1)], run_max[sl][:, :, GE - 1:GE]).then_inc(ev("A_carry"), 1)

            def a_add(s, sl, t):
                A_add.wait(dve, s)
                A_sc.wait(dve, s + 1)
                A_add.on(v.tensor_tensor(Macc[:, ds(t, 1), :], bank[0:P, 6 + sl, 0:FF].unsqueeze(1), Macc[:, ds(t, 1), :], ALU.add))

            def a_step(s, sl, row_count, g, g_ahead=None, t_behind=None):
                a_scan(s, sl, row_count, g)
                if g_ahead is not None:
                    a_product(s + 2, sl, g_ahead)
                a_carry(s, sl, g)
                if t_behind is not None:
                    a_add(s - 2, sl, t_behind)

            groups = groups_of(DVE, 0, 4)
            for s in range(2):
                a_product(s, s, groups[s])
            for s in range(2):
                a_step(s, s, 16, groups[s], groups[s + 2])
            with dve.Fori(0, STEPS // 2 - 2) as it:
                groups, tiles = groups_of(DVE, it * 2 + 2, 4), tiles_of(DVE, it * 2, 2)
                for sl in range(2):
                    a_step(it * 2 + (sl + 2), sl, it * 16 + 32, groups[sl], groups[sl + 2], tiles[sl])
            groups, tiles = groups_of(DVE, STEPS - 2, 2), tiles_of(DVE, STEPS - 4, 4)
            for sl in range(2):
                a_step(STEPS - 2 + sl, sl, 16 * (STEPS // 2), groups[sl], None, tiles[sl])
            for sl in range(2):
                a_add(STEPS - 2 + sl, sl, tiles[sl + 2])
            A_add.wait(dve, STEPS)
            do(v.tensor_copy(M16[0], Macc))
            do(v.tensor_tensor(M16[1], Macc, M16[0], ALU.subtract))
            v.memset(Macc, 0.0).then_inc(ev("M_ready"), 1)
            dve.wait_ge(ev("half_cleared"), 1)
            dve.wait_ge(ev("M_ready"), 1)

            B_st.give(dve)
            for sg in (B_em, B_d, B_add):
                sg.give(dve)

            def b_columns(s, sl, row_count):
                dve.wait_ge(ev(f"B_row{sl}"), row_count)
                B_mg.wait(dve, s)
                B_st.on(v.tensor_scalar(ST, rows_b[sl].bitcast(I32), step_node[:, ds(s, 1)], None, ALU.is_equal))

            def b_product(s, sl, g):
                B_w.wait(dve, s + 1)
                B_p.wait(dve, s - 2)
                xs = rows_of[:, ds(g * G, G), :].unsqueeze(3)
                B_em.on(v.tensor_tensor(em[sl], bank[0:P, 0:3, :].rearrange("p g (i w) -> p g i w", i=F), xs.to_broadcast([P, G, F, 2 * F]), ALU.mult))

            def b_difference(s, sl):
                B_em.wait(dve, s + 1)
                B_mg.wait(dve, s + 1)
                B_sc.wait(dve, s - 2)
                v.tensor_tensor(EP[sl][:, 0:2, :, 0:F], em[sl][:, 0:2, :, 0:F], bank[0:P, 3, :].rearrange("p (g i o) -> p g i o", g=2, i=F), ALU.subtract)
                B_d.on(v.tensor_tensor(EP[sl][:, 2, :, 0:F], em[sl][:, 2, :, 0:F], bank[0:P, 4, 0:FF].rearrange("p (i o) -> p i o", i=F), ALU.subtract))

            def b_add(s, sl, t):
                B_add.wait(dve, s)
                B_sc.wait(dve, s + 1)
                B_add.on(v.tensor_tensor(sums[:, ds(t, 1), :, :], bank[0:P, 5 + sl, :].rearrange("p (u i w) -> p u i w", u=1, i=F), sums[:, ds(t, 1), :, :], ALU.add))

            groups, n = groups_of(DVE, 0, B_SLOTS), B_SLOTS
            b_columns(0, 0, 16)
            for s, g in enumerate(groups):
                b_product(s, s, g)
                b_columns(s + 1, (s + 1) % n, 16 * ((s + 1) // n + 1))
                b_difference(s, s)
            with dve.Fori(0, STEPS // n - 2) as it:
                groups, tiles = groups_of(DVE, it * n + n, n), tiles_of(DVE, it * n, n)
                for j in range(n):
                    s = it * n + (j + n)
                    b_product(s, j, groups[j])
                    b_columns(s + 1, (j + 1) % n, it * 16 + 16 * ((n + j + 1) // n + 1))
                    b_difference(s, j)
                    b_add(s - n, j, tiles[j])
            groups, tiles = groups_of(DVE, STEPS - n, n), tiles_of(DVE, STEPS - 2 * n, 2 * n)
            for j in range(n):
                s = STEPS - n + j
                b_product(s, j, groups[j])
                if j < n - 1:
                    b_columns(s + 1, j + 1, 16 * (STEPS // n))
                b_difference(s, j)
                b_add(s - n, j, tiles[j])
            for j in range(n):
                b_add(STEPS - n + j, j, tiles[n + j])
            B_add.wait(dve, STEPS)
            den, num = sums[:, 0:T, :, 0:F], sums[:, 0:T, :, F:2 * F]
            do(v.tensor_scalar(den, den, TINY, None, ALU.max))
            do(v.reciprocal(den, den))
            do(v.tensor_tensor(num, num, den, ALU.mult))
            do(v.tensor_reduce(yn[:], num.rearrange("p t i o -> p t o i"), X, ALU.add))
            do(v.tensor_tensor(xn[:], xn[:], yn[:], ALU.add))
            layernorm(3).then_inc(ev("tab"), 1)

        @block.tensor
        def _(pe):
            mm = nc.tensor.matmul
            idn = ident[0:P, 0:P]
            pe.wait_ge(ev("consts"), 1)
            pe.wait_ge(ev("inc_row"), 1)
            for i in range(3):
                ins = mm(bank[0:SROWS, i, 0:GROUPS], ones[:, 0:SROWS], grow[0:1, i, :], start=True, stop=True)
            ins.then_inc(ev("inc_bc"), 1)
            pe.wait_ge(ev("step_row"), 1)
            mm(bank[0:P, 3, 0:STEPS], ones, step_row[0:1, STEPS:2 * STEPS], start=True, stop=True).then_inc(ev("step_bc"), 1)

            def summed(p, b, par, slot=0):
                width = 2 * F if p == "l1" else F
                source = both if p == "l1" else both[:, :, 0:1, :]
                pe.wait_ge(s_S, b + (PASSES.index(p) * BLOCKS + 1))
                for j, g in enumerate(groups_of(PE, b * PARTS, PARTS)):
                    for k in range(G):
                        ins = mm(bank[0:P, 6 + par, j * width:(j + 1) * width], S[slot][:, j * G + k, :],
                                 source[:, ds(g * G + k, 1), :, :].rearrange("p u h f -> p (u h) f"), start=(k == 0), stop=(k == G - 1))
                ins.then_inc(s_sum, 1)

            pe.wait_ge(ev("inputs"), 16 * N_LOADS)
            mm(bank[0:F, 7, 0:3], Ws_sb, WaT_sb, start=True, stop=True).then_inc(ev("attn_rows"), 1)
            pe.wait_ge(ev("attn_rep"), 1)
            mm(bank[0:P, 4, 0:F], A2_rep, ident[0:F, 0:F], start=True, stop=True).then_inc(ev("attn_row"), 1)
            mm(bank[0:R, 5, 0:FF], wcT_sb, VT_sb, start=True, stop=True).then_inc(ev("rel_sum"), 1)

            def count(it, par, first=False, last=False):
                deg_made.wait(pe, it + 1)
                for k in range(SLOTS):
                    ins = mm(bank[0:P, 6, 0:T], lo_oh[par][:, k, :], hi_oh[par][:, k, :], start=(first and k == 0), stop=(last and k == SLOTS - 1))
                deg_used.on(ins)

            count(0, 0, first=True)
            with pe.Fori(0, TURNS // 2 - 1) as it:
                count(it * 2 + 1, 1)
                count(it * 2 + 2, 0)
            count(TURNS - 2, 1)
            count(TURNS - 1, 0, last=True)
            def node_pass(p):
                te = p in g_oh

                def turn(it):
                    for i in range(TE_PARTS):
                        if i == 0:
                            g_oh[p].wait(pe, it + 1)
                        g_pick[p][i].wait(pe, it)
                        for k in range(G):
                            for q in range(3):
                                ins = mm(bank[0:P, i * G + k, 0:T * F], oh[:, (i * G + k) * P:(i * G + k + 1) * P], parts[:, q, :], start=(q == 0), stop=(q == 2))
                        ins.then_inc(s_te[i], 1)

                if te:
                    turn(0)
                    turn(1)
                summed(p, 0, 0)
                if te:
                    turn(2)
                with pe.Fori(0, (TURNS - 3) // 2) as it:
                    for j in range(2):
                        summed(p, it * 2 + (j + 1), 1 - j)
                        if te:
                            turn(it * 2 + (j + 3))
                summed(p, TURNS - 2, 1)
                with pe.Fori(0, (BLOCKS - TURNS + 1) // 2) as it:
                    for j in range(2):
                        summed(p, it * 2 + (TURNS - 1 + j), j, 1 - j)

            def transpose_nodes(src, done, width=F):
                for t in range(T):
                    ins = nc.tensor.transpose(bank[0:width, 1 + t // TB, (t % TB) * P:(t % TB + 1) * P], src[:, t, :], idn)
                    if t % TB == TB - 1 or t == T - 1:
                        ins.then_inc(done, 1)

            pe.wait_ge(ev("parts_ready"), 1)
            node_pass("l0a")
            pe.wait_ge(ev("ax_ready"), 1)
            transpose_nodes(yn, ev("axT"))
            for b in range(NB + 1):
                w = min(TBW, N - b * TBW)
                pe.wait_ge(ev("xT_ready"), b + 1)
                mm(bank[0:H1, b, 0:w], W1_sb, xT[:, b * TBW:b * TBW + w], start=True, stop=True).then_inc(ev("h_sum"), 1)
            for t in range(T):
                if t % TB == 0:
                    pe.wait_ge(ev("hT_ready"), t // TB + 1)
                ins = mm(bank[0:P, 7, t * F:(t + 1) * F], hT[:, t * P:(t + 1) * P], W2_sb, start=True, stop=True)
            ins.then_inc(ev("z_sum"), 1)
            pe.wait_ge(ev("parts_ready"), 2)
            node_pass("l0b")
            pe.wait_ge(ev("x1_ready"), 2)
            transpose_nodes(x6, ev("x1T"), KX)
            pe.wait_ge(ev("x1T_ready"), NB + 1)
            pe.wait_ge(ev("tall6_ready"), 16 * 6)
            y_mm.give(pe)

            def relation_tile(t, par):
                y_src.wait(pe, t + 1)
                y_copied.wait(pe, t - 1)
                w = R * YW // 3
                for b in range(3):
                    last = b == 2
                    ins = mm(bank[0:P, 3 * par + b, 0:w + last], xTs[par], Tall6[:, b * w:(b + 1) * w + last], start=True, stop=True)
                y_mm.on(ins)

            with pe.Fori(0, T // 2) as it:
                for par in range(2):
                    relation_tile(it * 2 + par, par)
            relation_tile(T - 1, 0)
            node_pass("l1")
            pe.wait_ge(ev("parts_ready"), 3)
            node_pass("l2")

            A_w.give(pe)
            A_sc.give(pe)
            Wa = W6[:].rearrange("k (i c o) -> k i c o", i=F, c=2)[:, :, 0, :]

            def a_weights(s, sl, ef_count):
                pe.wait_ge(ev(f"A_ef{sl}"), ef_count)
                A_e2.wait(pe, s)
                for k in range(G):
                    ins = mm(bank[0:P, k // 2, (k % 2) * FF:(k % 2 + 1) * FF], efs[sl][:, k * P:(k + 1) * P], Wa, start=True, stop=True)
                A_w.on(ins)

            def a_transpose(s, sl):
                A_e2.wait(pe, s + 1)
                A_scan.wait(pe, s)
                for half in range(2):
                    for k in range(G):
                        ins = nc.tensor.transpose(bank[:, 2 + half, k * P:(k + 1) * P], e2[sl][:, k, half * 128:(half + 1) * 128], idn)
                ins.then_inc(ev("A_tr"), 1)

            def a_back(s, sl):
                A_scan.wait(pe, s + 1)
                A_copy.wait(pe, s)
                for half in range(2):
                    for k in range(G):
                        c0 = (k % 2) * FF + half * 128
                        ins = nc.tensor.transpose(bank[0:P, 4 + k // 2, c0:c0 + 128], run_max[sl][:, half, k * P:(k + 1) * P], ident[:])
                ins.then_inc(ev("A_trb"), 1)

            def a_sum(s, sl):
                A_copy.wait(pe, s + 1)
                A_se.wait(pe, s + 1)
                A_add.wait(pe, s - 1 if not isinstance(s, int) else max(s - 1, 0))
                for k in range(G):
                    ins = mm(bank[0:P, 6 + sl, 0:FF], SE[sl][:, k, :], run_maxT[sl][:, k, :], start=(k == 0), stop=(k == G - 1))
                A_sc.on(ins)

            def a_step(s, sl, ef_count=None, ahead=True, before=True):
                if ahead:
                    a_transpose(s + 1, 1 - sl)
                a_back(s, sl)
                if ef_count is not None:
                    a_weights(s + 3, 1 - sl, ef_count)
                if before:
                    a_sum(s - 1, 1 - sl)

            a_weights(0, 0, 16)
            a_transpose(0, 0)
            a_weights(1, 1, 16)
            a_weights(2, 0, 32)
            a_step(0, 0, 32, before=False)
            with pe.Fori(0, STEPS // 2 - 2) as it:
                for j, sl in enumerate((1, 0)):
                    a_step(it * 2 + (j + 1), sl, it * 16 + 48)
            a_step(STEPS - 3, 1)
            a_step(STEPS - 2, 0)
            a_step(STEPS - 1, 1, ahead=False)
            a_sum(STEPS - 1, 1)
            A_add.wait(pe, STEPS)
            pe.wait_ge(ev("M_ready"), 1)

            B_w.give(pe)
            B_sc.give(pe)
            B_mg.give(pe)

            def b_front(s, sl, ef_count, t):
                pe.wait_ge(ev(f"B_ef{sl}"), ef_count)
                B_em.wait(pe, s)
                for k in range(G):
                    ins = mm(bank[0:P, k, :], efs_b[sl][:, k * P:(k + 1) * P], W6[:], start=True, stop=True)
                B_w.on(ins)
                B_st.wait(pe, s + 1)
                B_d.wait(pe, s)
                for k in range(G):
                    for q in range(2):
                        ins = mm(bank[0:P, 3 + k // 2, (k % 2) * FF:(k % 2 + 1) * FF], ST[:, k * P:(k + 1) * P], M16[q][:, ds(t, 1), :].rearrange("p u w -> p (u w)"), start=(q == 0), stop=(q == 1))
                B_mg.on(ins)

            def b_sum(s, sl):
                B_p.wait(pe, s + 1)
                pe.wait_ge(ev("B_sb"), s + 1)
                B_add.wait(pe, s - 2)
                for k in range(G):
                    ins = mm(bank[0:P, 5 + sl, :], SB[sl][:, k, :], EP[sl][:, k, :, :].rearrange("p i w -> p (i w)"), start=(k == 0), stop=(k == G - 1))
                B_sc.on(ins)

            n = B_SLOTS
            for s, t in enumerate(tiles_of(PE, 0, 2)):
                b_front(s, s, 16, t)
            with pe.Fori(0, STEPS // n - 1) as it:
                tiles = tiles_of(PE, it * n + 2, n)
                for j in range(n):
                    b_front(it * n + (j + 2), (j + 2) % n, it * 16 + 16 * ((j + 2) // n + 1), tiles[j])
                    b_sum(it * n + j, j)
            b_front(STEPS - 1, n - 1, 16 * (STEPS // n), tiles_of(PE, STEPS - 1, 1)[0])
            for j in range(n):
                b_sum(STEPS - n + j, j)


def kernel(**inputs):
    import numpy as np
    import concourse.bacc as bacc
    from concourse.bass_utils import run_bass_kernel_spmd as run

    a = {k: np.asarray(v) for k, v in inputs.items()}

    def by_column(e):
        return np.ascontiguousarray(np.moveaxis(e.reshape(C, P, *e.shape[1:]), 0, 1))

    dst, ef = a["dst"], a["edge_attr_16"]
    none = np.full(1, -1, dst.dtype)
    laid = {
        "x": a["x"], "src_pc": by_column(a["src"]), "dst_pc": by_column(dst),
        "dst_next_pc": by_column(np.concatenate([dst[1:], none])), "src_flat": a["src"].reshape(1, E), "dst_flat": dst.reshape(1, E),
        "dst_prev_flat": np.concatenate([none, dst[:-1]]).reshape(1, E),
        "group_ends": np.stack([dst[0::GE], dst[GE - 1::GE]]), "ef_pc": by_column(ef),
        "efT": ef.T, "type_pc": by_column(a["edge_type_90"]),
        "weight_pc": by_column(a["edge_weight"]),
        "W1": a["L0_gnn_W1"], "b1": a["L0_gnn_b1"].reshape(H1, 1), "W2": a["L0_gnn_W2"], "b2": a["L0_gnn_b2"].reshape(1, F),
        "Ws": a["L1_gnn_Ws"], "WaT": a["L1_gnn_Wa"].reshape(3, F).T,
        "VT": a["L1_gnn_weight"].reshape(F, B, F).transpose(1, 0, 2).reshape(B, FF), "wcompT": a["L1_gnn_w_comp"].T,
        "l2w": a["L2_gnn_weight"].reshape(1, F), "slw": a["L2_gnn_self_loop_weight"].reshape(1, 1),
        "Wmsg": a["L3_gnn_W_msg"], "bmsg": a["L3_gnn_b_msg"].reshape(1, FF),
        "Wattn": a["L3_gnn_W_attn"], "battn": a["L3_gnn_b_attn"].reshape(1, FF),
    }
    nc = bacc.Bacc("TRN2", target_bir_lowering=False, num_devices=1)
    arrays, args = {}, []
    for name, v in laid.items():
        v = np.ascontiguousarray(v)
        arrays[f"in_{name}"] = v
        args.append(nc.dram_tensor(f"in_{name}", v.shape, mybir.dt.from_np(v.dtype), kind="ExternalInput").ap())
    out = nc.dram_tensor("out_0", (N, F), FP32, kind="ExternalOutput").ap()
    build(nc, *args, out)
    return run(nc, [arrays], core_ids=[0]).results[0]["out_0"]
```
